# Optimizing a Trainium2 kernel written in Bass

```python
import numpy as np
import jax
import jax.numpy as jnp

def _softmax(x, axis=-1):
    return jax.nn.softmax(x, axis=axis)

def _gelu(x):
    return jax.nn.gelu(x, approximate=True)

def _silu(x):
    return jax.nn.silu(x)

def _sigmoid(x):
    return jax.nn.sigmoid(x)

def _layernorm(x, axis=-1, eps=1e-05):
    m = jnp.mean(x, axis=axis, keepdims=True)
    v = jnp.var(x, axis=axis, keepdims=True)
    return (x - m) / jnp.sqrt(v + eps)

def _scatter_add(tgt, idx, src, axis=0):
    return tgt.at[idx].add(src)

def _segment_sum(src, seg, n):
    return jax.ops.segment_sum(src, seg, n)
kernel_name = 'mk_gnn_resnorm_d4_gnn_r8_03151d'

def setup_inputs(seed: int=0):
    np.random.seed(seed)
    _w = jnp.asarray

    def _rec_inputs():
        import jax
        import jax.numpy as jnp
        _gk = jax.random.key(seed)
        x = -0.0003713 + 1 * jax.random.normal(jax.random.fold_in(_gk, 1), (6250, 128), jnp.float32)
        src = jax.random.randint(jax.random.fold_in(_gk, 2), (200000,), 0, 6250, jnp.int32)
        dst = jax.random.randint(jax.random.fold_in(_gk, 3), (200000,), 0, 6250, jnp.int32)
        _o = jnp.argsort(dst, stable=True)
        src = src[_o]
        dst = dst[_o]
        edge_attr_64 = 0.000167468 + 1.0002 * jax.random.normal(jax.random.fold_in(_gk, 11), (200000, 64), jnp.float32)
        edge_type_8 = jax.random.randint(jax.random.fold_in(_gk, 13), (200000,), 0, 8, jnp.int32)
        edge_weight = jax.random.uniform(jax.random.fold_in(_gk, 14), (200000,), jnp.float32, 0.0, 1)
        return (x, src, dst, edge_attr_64, edge_type_8, edge_weight)
    x, src, dst, edge_attr_64, edge_type_8, edge_weight = _rec_inputs()

    def _L0_gnn_setup():
        import jax, jax.numpy as jnp
        import numpy as np
        N_NODES = 12500
        N_EDGES = 400000
        D_IN = 128
        D_OUT = 128
        key = jax.random.key(seed)
        k1, k2, k3, k4, k5 = jax.random.split(key, 5)
        x = jax.random.normal(k1, (N_NODES, D_IN), dtype=jnp.float32)
        edge_index = jax.random.randint(k2, (2, N_EDGES), 0, N_NODES, dtype=jnp.int64)
        edge_weight = jax.random.uniform(k3, (N_EDGES,), dtype=jnp.float32)
        W = jax.random.normal(k4, (D_IN, D_OUT), dtype=jnp.float32) / np.sqrt(D_IN)
        b = jax.random.normal(k5, (D_OUT,), dtype=jnp.float32)
        return {'x': x, 'edge_index': edge_index, 'edge_weight': edge_weight, 'W': W, 'b': b}
    _L0_gnn_all = _L0_gnn_setup()
    _L0_gnn_in = {k: v for k, v in _L0_gnn_all.items() if k in ('W', 'b')}
    del _L0_gnn_all

    def _L1_gnn_setup():
        import jax, jax.numpy as jnp
        import numpy as np
        N_NODES = 12500
        N_EDGES = 75000
        H = 128
        T = 8
        L = 2

        def _gru_cell(x, h, wih, whh, bih, bhh):
            gi = x @ wih.T + bih
            gh = h @ whh.T + bhh
            i_r, i_z, i_n = jnp.split(gi, 3, axis=-1)
            h_r, h_z, h_n = jnp.split(gh, 3, axis=-1)
            r = jax.nn.sigmoid(i_r + h_r)
            z = jax.nn.sigmoid(i_z + h_z)
            n = jnp.tanh(i_n + r * h_n)
            return (1.0 - z) * n + z * h
        key = jax.random.key(seed)
        ks = jax.random.split(key, 12)
        s = 1.0 / np.sqrt(H)
        inp = {'node_features': jax.random.normal(ks[0], (N_NODES, H), dtype=jnp.float32), 'edge_index': jax.random.randint(ks[1], (2, N_EDGES), 0, N_NODES, dtype=jnp.int64), 'edge_type': jax.random.randint(ks[2], (N_EDGES,), 0, T, dtype=jnp.int64), 'node_proj_w': jax.random.uniform(ks[3], (H, H), jnp.float32, -s, s), 'node_proj_b': jax.random.uniform(ks[4], (H,), jnp.float32, -s, s), 'edge_W': jax.random.uniform(ks[5], (L, T, H, H), jnp.float32, -s, s), 'edge_b': jax.random.uniform(ks[6], (L, T, H), jnp.float32, -s, s), 'gru_wih': jax.random.uniform(ks[7], (L, 3 * H, H), jnp.float32, -s, s), 'gru_whh': jax.random.uniform(ks[8], (L, 3 * H, H), jnp.float32, -s, s), 'gru_bih': jax.random.uniform(ks[9], (L, 3 * H), jnp.float32, -s, s), 'gru_bhh': jax.random.uniform(ks[10], (L, 3 * H), jnp.float32, -s, s), 'out_w': jax.random.uniform(ks[11], (H, H), jnp.float32, -s, s), 'out_b': jnp.zeros((H,), jnp.float32)}
        return inp
    _L1_gnn_all = _L1_gnn_setup()
    _L1_gnn_in = {k: v for k, v in _L1_gnn_all.items() if k in ('node_proj_w', 'node_proj_b', 'edge_W', 'edge_b', 'gru_wih', 'gru_whh', 'gru_bih', 'gru_bhh', 'out_w', 'out_b')}
    del _L1_gnn_all

    def _L2_gnn_setup():
        import jax, jax.numpy as jnp
        import numpy as np
        N_NODES = 12500
        N_EDGES = 200000
        HIDDEN = 128
        HEADS = 8
        HEAD_DIM = HIDDEN // HEADS
        ALPHA = 0.2
        LN_EPS = 1e-05

        def _gat_forward(x, edge_index, W, a, ln_gamma, ln_beta):
            n = x.shape[0]
            row, col = (edge_index[0], edge_index[1])
            x_heads = jnp.einsum('ni,hij->nhj', x, W)
            a_vec = a[..., 0]
            a_i, a_j = (a_vec[:, :HEAD_DIM], a_vec[:, HEAD_DIM:])
            s_i = jnp.einsum('nhd,hd->nh', x_heads, a_i)
            s_j = jnp.einsum('nhd,hd->nh', x_heads, a_j)
            e = s_i[row] + s_j[col]
            e = jnp.where(e >= 0, e, ALPHA * e)
            m = jax.ops.segment_max(e, row, num_segments=n)
            m = jnp.where(jnp.isfinite(m), m, 0.0)
            ex = jnp.exp(e - m[row])
            denom = jax.ops.segment_sum(ex, row, num_segments=n)
            attn = ex / denom[row]
            weighted = x_heads[row] * attn[..., None]
            out_heads = jax.ops.segment_sum(weighted, col, num_segments=n)
            out = out_heads.reshape(n, HIDDEN)
            out = out + x
            mu = jnp.mean(out, axis=-1, keepdims=True)
            var = jnp.mean(jnp.square(out - mu), axis=-1, keepdims=True)
            out = (out - mu) * jax.lax.rsqrt(var + LN_EPS)
            return out * ln_gamma + ln_beta
        key = jax.random.key(seed)
        k1, k2, k3, k4 = jax.random.split(key, 4)
        x = jax.random.normal(k1, (N_NODES, HIDDEN), dtype=jnp.float32)
        edge_index = jax.random.randint(k2, (2, N_EDGES), 0, N_NODES, dtype=jnp.int64)
        w_bound = np.sqrt(6.0 / (HIDDEN + HEAD_DIM))
        a_bound = np.sqrt(6.0 / (2 * HEAD_DIM + 1))
        W = jax.random.uniform(k3, (HEADS, HIDDEN, HEAD_DIM), minval=-w_bound, maxval=w_bound, dtype=jnp.float32)
        a = jax.random.uniform(k4, (HEADS, 2 * HEAD_DIM, 1), minval=-a_bound, maxval=a_bound, dtype=jnp.float32)
        ln_gamma = jnp.ones((HIDDEN,), dtype=jnp.float32)
        ln_beta = jnp.zeros((HIDDEN,), dtype=jnp.float32)
        return {'x': x, 'edge_index': edge_index, 'W': W, 'a': a, 'ln_gamma': ln_gamma, 'ln_beta': ln_beta}
    _L2_gnn_all = _L2_gnn_setup()
    _L2_gnn_in = {k: v for k, v in _L2_gnn_all.items() if k in ('W', 'a', 'ln_gamma', 'ln_beta')}
    del _L2_gnn_all

    def _L3_gnn_setup():
        import jax, jax.numpy as jnp
        import numpy as np
        N_NODES = 12500
        N_EDGES = 80000
        HID = 128
        EDGE_D = 64
        GLOB_D = 64
        LN_EPS = 1e-05

        def _linear(x, W, b):
            return x @ W.T + b
        key = jax.random.key(seed)
        ks = jax.random.split(key, 16)
        s = lambda d: 1.0 / np.sqrt(d)
        inp = {'node_state': jax.random.normal(ks[0], (N_NODES, HID), jnp.float32), 'edge_index': jax.random.randint(ks[1], (2, N_EDGES), 0, N_NODES, jnp.int64), 'edge_state': jax.random.normal(ks[2], (N_EDGES, EDGE_D), jnp.float32), 'global_state': jax.random.normal(ks[3], (GLOB_D,), jnp.float32), 'Wm1': jax.random.uniform(ks[4], (HID, HID + EDGE_D + GLOB_D), jnp.float32, -s(HID + EDGE_D + GLOB_D), s(HID + EDGE_D + GLOB_D)), 'bm1': jnp.zeros((HID,), jnp.float32), 'Wm2': jax.random.uniform(ks[5], (HID, HID), jnp.float32, -s(HID), s(HID)), 'bm2': jnp.zeros((HID,), jnp.float32), 'Wu1': jax.random.uniform(ks[6], (HID, HID + HID + GLOB_D), jnp.float32, -s(HID + HID + GLOB_D), s(HID + HID + GLOB_D)), 'bu1': jnp.zeros((HID,), jnp.float32), 'Wu2': jax.random.uniform(ks[7], (HID, HID), jnp.float32, -s(HID), s(HID)), 'bu2': jnp.zeros((HID,), jnp.float32), 'ln_g': jnp.ones((HID,), jnp.float32), 'ln_b': jnp.zeros((HID,), jnp.float32)}
        return inp
    _L3_gnn_all = _L3_gnn_setup()
    _L3_gnn_in = {k: v for k, v in _L3_gnn_all.items() if k in ('global_state', 'Wm1', 'bm1', 'Wm2', 'bm2', 'Wu1', 'bu1', 'Wu2', 'bu2', 'ln_g', 'ln_b')}
    del _L3_gnn_all
    return {'x': x, 'src': src, 'dst': dst, 'edge_attr_64': edge_attr_64, 'edge_type_8': edge_type_8, 'edge_weight': edge_weight, 'L0_gnn_W': _L0_gnn_in['W'], 'L0_gnn_b': _L0_gnn_in['b'], 'L1_gnn_node_proj_w': _L1_gnn_in['node_proj_w'], 'L1_gnn_node_proj_b': _L1_gnn_in['node_proj_b'], 'L1_gnn_edge_W': _L1_gnn_in['edge_W'], 'L1_gnn_edge_b': _L1_gnn_in['edge_b'], 'L1_gnn_gru_wih': _L1_gnn_in['gru_wih'], 'L1_gnn_gru_whh': _L1_gnn_in['gru_whh'], 'L1_gnn_gru_bih': _L1_gnn_in['gru_bih'], 'L1_gnn_gru_bhh': _L1_gnn_in['gru_bhh'], 'L1_gnn_out_w': _L1_gnn_in['out_w'], 'L1_gnn_out_b': _L1_gnn_in['out_b'], 'L2_gnn_W': _L2_gnn_in['W'], 'L2_gnn_a': _L2_gnn_in['a'], 'L2_gnn_ln_gamma': _L2_gnn_in['ln_gamma'], 'L2_gnn_ln_beta': _L2_gnn_in['ln_beta'], 'L3_gnn_global_state': _L3_gnn_in['global_state'], 'L3_gnn_Wm1': _L3_gnn_in['Wm1'], 'L3_gnn_bm1': _L3_gnn_in['bm1'], 'L3_gnn_Wm2': _L3_gnn_in['Wm2'], 'L3_gnn_bm2': _L3_gnn_in['bm2'], 'L3_gnn_Wu1': _L3_gnn_in['Wu1'], 'L3_gnn_bu1': _L3_gnn_in['bu1'], 'L3_gnn_Wu2': _L3_gnn_in['Wu2'], 'L3_gnn_bu2': _L3_gnn_in['bu2'], 'L3_gnn_ln_g': _L3_gnn_in['ln_g'], 'L3_gnn_ln_b': _L3_gnn_in['ln_b']}

def reference(x, src, dst, edge_attr_64, edge_type_8, edge_weight, L0_gnn_W, L0_gnn_b, L1_gnn_node_proj_w, L1_gnn_node_proj_b, L1_gnn_edge_W, L1_gnn_edge_b, L1_gnn_gru_wih, L1_gnn_gru_whh, L1_gnn_gru_bih, L1_gnn_gru_bhh, L1_gnn_out_w, L1_gnn_out_b, L2_gnn_W, L2_gnn_a, L2_gnn_ln_gamma, L2_gnn_ln_beta, L3_gnn_global_state, L3_gnn_Wm1, L3_gnn_bm1, L3_gnn_Wm2, L3_gnn_bm2, L3_gnn_Wu1, L3_gnn_bu1, L3_gnn_Wu2, L3_gnn_bu2, L3_gnn_ln_g, L3_gnn_ln_b):
    import jax
    import jax.numpy as jnp

    def _L0_gnn_ref(x, edge_index, edge_weight, W, b):
        import jax, jax.numpy as jnp
        import numpy as np
        N_NODES = 12500
        N_EDGES = 400000
        D_IN = 128
        D_OUT = 128
        N = x.shape[0]
        src, dst = (edge_index[0], edge_index[1])
        loops = jnp.arange(N, dtype=edge_index.dtype)
        src_f = jnp.concatenate([src, loops])
        dst_f = jnp.concatenate([dst, loops])
        w_f = jnp.concatenate([edge_weight, jnp.ones((N,), dtype=edge_weight.dtype)])
        deg = jax.ops.segment_sum(w_f, dst_f, num_segments=N)
        deg_inv_sqrt = jnp.where(deg > 0, jax.lax.rsqrt(deg), 0.0)
        norm = deg_inv_sqrt[src_f] * w_f * deg_inv_sqrt[dst_f]
        h = x @ W
        msgs = h[src_f] * norm[:, None]
        out = jax.ops.segment_sum(msgs, dst_f, num_segments=N)
        return out + b

    def _L1_gnn_ref(node_features, edge_index, edge_type, node_proj_w, node_proj_b, edge_W, edge_b, gru_wih, gru_whh, gru_bih, gru_bhh, out_w, out_b):
        import jax, jax.numpy as jnp
        import numpy as np
        N_NODES = 12500
        N_EDGES = 75000
        H = 128
        T = 8
        L = 2

        def _gru_cell(x, h, wih, whh, bih, bhh):
            gi = x @ wih.T + bih
            gh = h @ whh.T + bhh
            i_r, i_z, i_n = jnp.split(gi, 3, axis=-1)
            h_r, h_z, h_n = jnp.split(gh, 3, axis=-1)
            r = jax.nn.sigmoid(i_r + h_r)
            z = jax.nn.sigmoid(i_z + h_z)
            n = jnp.tanh(i_n + r * h_n)
            return (1.0 - z) * n + z * h
        num_nodes = node_features.shape[0]
        src, dst = (edge_index[0], edge_index[1])
        h = jax.nn.relu(node_features @ node_proj_w.T + node_proj_b)
        for l in range(L):
            trans = jnp.einsum('nh,tdh->tnd', h, edge_W[l])
            msgs = trans[edge_type, src]
            agg = jax.ops.segment_sum(msgs, dst, num_segments=num_nodes)
            h = _gru_cell(agg, h, gru_wih[l], gru_whh[l], gru_bih[l], gru_bhh[l])
            h = jax.nn.relu(h)
        return h @ out_w.T + out_b

    def _L2_gnn_ref(x, edge_index, W, a, ln_gamma, ln_beta):
        import jax, jax.numpy as jnp
        import numpy as np
        N_NODES = 12500
        N_EDGES = 200000
        HIDDEN = 128
        HEADS = 8
        HEAD_DIM = HIDDEN // HEADS
        ALPHA = 0.2
        LN_EPS = 1e-05

        def _gat_forward(x, edge_index, W, a, ln_gamma, ln_beta):
            n = x.shape[0]
            row, col = (edge_index[0], edge_index[1])
            x_heads = jnp.einsum('ni,hij->nhj', x, W)
            a_vec = a[..., 0]
            a_i, a_j = (a_vec[:, :HEAD_DIM], a_vec[:, HEAD_DIM:])
            s_i = jnp.einsum('nhd,hd->nh', x_heads, a_i)
            s_j = jnp.einsum('nhd,hd->nh', x_heads, a_j)
            e = s_i[row] + s_j[col]
            e = jnp.where(e >= 0, e, ALPHA * e)
            m = jax.ops.segment_max(e, row, num_segments=n)
            m = jnp.where(jnp.isfinite(m), m, 0.0)
            ex = jnp.exp(e - m[row])
            denom = jax.ops.segment_sum(ex, row, num_segments=n)
            attn = ex / denom[row]
            weighted = x_heads[row] * attn[..., None]
            out_heads = jax.ops.segment_sum(weighted, col, num_segments=n)
            out = out_heads.reshape(n, HIDDEN)
            out = out + x
            mu = jnp.mean(out, axis=-1, keepdims=True)
            var = jnp.mean(jnp.square(out - mu), axis=-1, keepdims=True)
            out = (out - mu) * jax.lax.rsqrt(var + LN_EPS)
            return out * ln_gamma + ln_beta
        return _gat_forward(x, edge_index, W, a, ln_gamma, ln_beta)

    def _L3_gnn_ref(node_state, edge_index, edge_state, global_state, Wm1, bm1, Wm2, bm2, Wu1, bu1, Wu2, bu2, ln_g, ln_b):
        import jax, jax.numpy as jnp
        import numpy as np
        N_NODES = 12500
        N_EDGES = 80000
        HID = 128
        EDGE_D = 64
        GLOB_D = 64
        LN_EPS = 1e-05

        def _linear(x, W, b):
            return x @ W.T + b
        src, dst = (edge_index[0], edge_index[1])
        num_nodes = node_state.shape[0]
        num_edges = edge_state.shape[0]
        g_edges = jnp.broadcast_to(global_state[None, :], (num_edges, GLOB_D))
        msg_in = jnp.concatenate([node_state[src], edge_state, g_edges], axis=-1)
        messages = _linear(jax.nn.relu(_linear(msg_in, Wm1, bm1)), Wm2, bm2)
        aggregated = jax.ops.segment_sum(messages, dst, num_segments=num_nodes)
        degree = jax.ops.segment_sum(jnp.ones((num_edges,), node_state.dtype), dst, num_segments=num_nodes)
        aggregated = aggregated / jnp.maximum(degree, 1.0)[:, None]
        g_nodes = jnp.broadcast_to(global_state[None, :], (num_nodes, GLOB_D))
        upd_in = jnp.concatenate([node_state, aggregated, g_nodes], axis=-1)
        delta = _linear(jax.nn.relu(_linear(upd_in, Wu1, bu1)), Wu2, bu2)
        h = node_state + delta
        mu = jnp.mean(h, axis=-1, keepdims=True)
        var = jnp.mean(jnp.square(h - mu), axis=-1, keepdims=True)
        return (h - mu) * jax.lax.rsqrt(var + LN_EPS) * ln_g + ln_b
    edge_index = jnp.stack([src, dst])
    x = _layernorm(x + _L0_gnn_ref(x, edge_index, edge_weight, L0_gnn_W, L0_gnn_b), axis=-1)
    x = _layernorm(x + _L1_gnn_ref(x, edge_index, edge_type_8, L1_gnn_node_proj_w, L1_gnn_node_proj_b, L1_gnn_edge_W, L1_gnn_edge_b, L1_gnn_gru_wih, L1_gnn_gru_whh, L1_gnn_gru_bih, L1_gnn_gru_bhh, L1_gnn_out_w, L1_gnn_out_b), axis=-1)
    x = _layernorm(x + _L2_gnn_ref(x, edge_index, L2_gnn_W, L2_gnn_a, L2_gnn_ln_gamma, L2_gnn_ln_beta), axis=-1)
    x = _layernorm(x + _L3_gnn_ref(x, edge_index, edge_attr_64, L3_gnn_global_state, L3_gnn_Wm1, L3_gnn_bm1, L3_gnn_Wm2, L3_gnn_bm2, L3_gnn_Wu1, L3_gnn_bu1, L3_gnn_Wu2, L3_gnn_bu2, L3_gnn_ln_g, L3_gnn_ln_b), axis=-1)
    return x

_drawn_inputs = setup_inputs


def setup_inputs(seed=0):
    import zlib

    import numpy as np

    out = dict(_drawn_inputs(seed))
    spreads = {'L1_gnn_out_b': (0.0, 0.1),
     'L2_gnn_ln_gamma': (1.0, 0.2),
     'L2_gnn_ln_beta': (0.0, 0.1),
     'L3_gnn_bm1': (0.0, 0.8),
     'L3_gnn_bm2': (0.0, 0.8),
     'L3_gnn_bu1': (0.0, 0.424),
     'L3_gnn_bu2': (0.0, 0.1),
     'L3_gnn_ln_g': (1.0, 0.2),
     'L3_gnn_ln_b': (0.0, 0.1)}
    factors = {'edge_attr_64': 8.0,
     'L1_gnn_gru_bih': 4.537,
     'L1_gnn_gru_bhh': 6.356,
     'L3_gnn_Wm1': 5.441,
     'L3_gnn_Wm2': 3.079}
    for name, (base, spread) in spreads.items():
        noise = np.random.default_rng([zlib.crc32(name.encode()), seed]).standard_normal(out[name].shape)
        drawn = base * np.exp(spread * noise) if base else spread * noise
        out[name] = jnp.asarray(drawn.astype(out[name].dtype))
    for name, factor in factors.items():
        out[name] = (out[name] * factor).astype(out[name].dtype)
    return out
```

```python
from contextlib import ExitStack

import concourse.bass as bass
from concourse import mybir

F32 = mybir.dt.float32
I32 = mybir.dt.int32
U32 = mybir.dt.uint32
ALU = mybir.AluOpType
ACT = mybir.ActivationFunctionType
AX = mybir.AxisListType.X
ds = bass.ds

P = 128
D = 128
N = 6250
E = 200000
NT = -(-N // P)
NPAD = NT * P
NLAST = N - (NT - 1) * P
TC = 7
NCH = NT // TC
CW = TC * P
GC = 16
GE = GC * P
NG = -(-E // GE)
PLAST = (E - (NG - 1) * GE) // GC
T = 8
H = 8
HD = 16
ED = 64
ACCW = NPAD + P
FAR = 1000000
KCAP = -(-(NG * NT) // P) * P
KT = KCAP // P
NOBASE = 8000000.0
EPS = 1e-5
ALPHA = 0.2
assert NT == NCH * TC and (NG - 1) * GE + PLAST * GC == E

W_PROJ, W_EDGE, W_IH, W_HH, W_OUT, W_HEADS, W_M1X, W_M1E, W_M1G, W_U1X, W_U1A, W_U1G, W_U2 = (
    0, 1, 17, 23, 29, 30, 31, 32, 33, 34, 35, 36, 37)
NW = 40


class Chain:

    def __init__(self, eng, sem, per_turn=0, turn=0):
        self.eng, self.sem, self.n, self.base = eng, sem, 0, turn * per_turn

    def step(self, ins):
        ins.then_inc(self.sem, 1)
        self.n += 1
        self.eng.wait_ge(self.sem, self.base + self.n)


def passed(eng, tick):
    eng.sem_inc(tick, 1)


def over(ap, n):
    return ap.unsqueeze(2).to_broadcast([ap.shape[0], ap.shape[1], n])


def rows(ap, n):
    return ap.unsqueeze(1).to_broadcast([ap.shape[0], n, ap.shape[1]])


def build(nc, x, src, dst, edge_attr_64, edge_type_8, edge_weight, L0_gnn_W, L0_gnn_b, L1_gnn_node_proj_w,
          L1_gnn_node_proj_b, L1_gnn_edge_W, L1_gnn_edge_b, L1_gnn_gru_wih, L1_gnn_gru_whh, L1_gnn_gru_bih,
          L1_gnn_gru_bhh, L1_gnn_out_w, L1_gnn_out_b, L2_gnn_W, L2_gnn_a, L2_gnn_ln_gamma, L2_gnn_ln_beta,
          L3_gnn_global_state, L3_gnn_Wm1, L3_gnn_bm1, L3_gnn_Wm2, L3_gnn_bm2, L3_gnn_Wu1, L3_gnn_bu1,
          L3_gnn_Wu2, L3_gnn_bu2, L3_gnn_ln_g, L3_gnn_ln_b, out):
    V = nc.vector

    def dram(name, shape, dt=F32):
        return nc.dram_tensor(name, shape, dt, kind="Internal").ap()

    items_d = dram("items_d", [KCAP, 4], I32)
    dst_d = dram("dst_d", [NG, GE], I32)
    src_d = dram("src_d", [NG, GE], I32)
    row_d = dram("row_d", [NG, GE], I32)
    gcn_d = dram("gcn_d", [NPAD, D])
    trans_d = dram("trans_d", [NPAD, T * D])
    att_d = dram("att_d", [NPAD, 2 * H])
    sj_d = dram("sj_d", [ACCW, 2 * H])
    heads_d = dram("heads_d", [NPAD, D])
    msg_d = dram("msg_d", [NPAD, D])

    def sb(ctx, name, shape, dt=F32):
        return ctx.enter_context(nc.sbuf_tensor(name, shape, dt))

    def ps(ctx, name, shape):
        return ctx.enter_context(nc.psum_tensor(name, shape, F32))

    in_stage = []

    def sems(prefix, names):
        made = [nc.alloc_semaphore(name=f"{prefix}_{n}") for n in names.split()]
        in_stage.extend(made)
        return made

    def end_stage():
        nc.clear_and_free_semaphores(list(in_stage))
        in_stage.clear()
        nc.all_engine_barrier()

    with ExitStack() as whole:
        tick = whole.enter_context(nc.semaphore("tick"))
        X = sb(whole, "X", [P, NPAD])
        HB = sb(whole, "HB", [P, NPAD])
        acc = sb(whole, "acc", [P, ACCW])
        dstI = sb(whole, "dstI", [P, NG * GC], I32)
        wgt = sb(whole, "wgt", [P, NG * GC])
        iota_row = sb(whole, "iota_row", [P, P])
        iota_col = sb(whole, "iota_col", [P, 1])
        iota_colI = sb(whole, "iota_colI", [P, 1], I32)
        ident = sb(whole, "ident", [P, P])
        ones = sb(whole, "ones", [P, P])
        wt = sb(whole, "wt", [P, NW * P])
        w0 = sb(whole, "w0", [P, D])
        wall = sb(whole, "wall", [P, D])
        wa = sb(whole, "wa", [P, 2 * H])
        wcomb = sb(whole, "wcomb", [P, D])
        bias = sb(whole, "bias", [P, 11, D])
        bcol = sb(whole, "bcol", [P, 32])
        deg = sb(whole, "deg", [P, 2, NT])
        dinv = sb(whole, "dinv", [P, NT])
        cntinv = sb(whole, "cntinv", [P, NT])
        has = sb(whole, "has", [P, NT])
        nturn = sb(whole, "nturn", [1, 1], I32)

        B_L0, B_OUT, B_GAMMA, B_BETA, B_M1, B_U1, B_U2, B_LNG, B_LNB, B_M2, B_V = range(11)
        C_PROJ, C_IH, C_HH, C_RZ = 0, 1, 7, 13

        def W(i, n=1):
            return wt[:, i * P:(i + n) * P]

        with ExitStack() as ctx:
            ctx.callback(end_stage)
            ws = sb(ctx, "ws", [P, NW * P])
            wm2 = sb(ctx, "wm2", [P, D])
            srcI = sb(ctx, "srcI", [P, NG * GC], I32)
            typI = sb(ctx, "typI", [P, NG * GC], I32)
            rowI = sb(ctx, "rowI", [P, NG * GC], I32)
            acol = sb(ctx, "acol", [P, 2])
            a_blk = sb(ctx, "a_blk", [P, 2 * H])
            hmask = sb(ctx, "hmask", [P, H])
            h8 = sb(ctx, "h8", [P, H])
            gcol = sb(ctx, "gcol", [ED, 1])
            bm2c = sb(ctx, "bm2c", [P, 1])
            vecs = sb(ctx, "vecs", [P, 2, P])
            wps = ps(ctx, "wps", [P, 2, 512])
            sps = ps(ctx, "sps", [P, 512])
            fill, x_in, edges_in, w_in, small_in, iotas, wtp, wtc, mini, minis, made, chain, rowed = sems(
                "setup", "fill x_in edges_in w_in small_in iotas wtp wtc mini minis made chain rowed")
            with nc.Block() as block:
                w_loads = []

                def wload(slot, ap, n=1, view=None):
                    w_loads.append((slot, ap, n))

                wload(W_PROJ, L1_gnn_node_proj_w)
                for l in range(2):
                    w_loads.append((W_EDGE + 8 * l, L1_gnn_edge_W[l].rearrange("t d h -> d t h"), 8))
                    w_loads.append((W_IH + 3 * l, L1_gnn_gru_wih[l].rearrange("(k d) h -> d k h", k=3), 3))
                    w_loads.append((W_HH + 3 * l, L1_gnn_gru_whh[l].rearrange("(k d) h -> d k h", k=3), 3))
                wload(W_OUT, L1_gnn_out_w)
                wload(W_M1X, L3_gnn_Wm1[:, 0:D])
                wload(W_U1X, L3_gnn_Wu1[:, 0:D])
                wload(W_U1A, L3_gnn_Wu1[:, D:2 * D])
                wload(W_U2, L3_gnn_Wu2)
                half_loads = [
                    (W_M1E * P, L3_gnn_Wm1[:, D:D + ED]), (W_M1E * P + ED, L3_gnn_Wm1[:, D:D + ED]),
                    (W_M1G * P, L3_gnn_Wm1[:, D + ED:D + 2 * ED]), (W_U1G * P, L3_gnn_Wu1[:, 2 * D:2 * D + ED])]
                bias_loads = [L0_gnn_b, L1_gnn_out_b, L2_gnn_ln_gamma, L2_gnn_ln_beta, L3_gnn_bm1, L3_gnn_bu1,
                              L3_gnn_bu2, L3_gnn_ln_g, L3_gnn_ln_b, L3_gnn_bm2]
                col_loads = [(C_PROJ, 1, L1_gnn_node_proj_b.rearrange("(p a) -> p a", a=1))]
                for l in range(2):
                    col_loads.append((C_IH + 3 * l, 3, L1_gnn_gru_bih[l].rearrange("(k p) -> p k", k=3)))
                    col_loads.append((C_HH + 3 * l, 3, L1_gnn_gru_bhh[l].rearrange("(k p) -> p k", k=3)))
                NWL = len(w_loads) + len(half_loads) + 1
                NSL = 4 + len(bias_loads) + len(col_loads)

                @block.sync
                def _(sp):
                    sp.wait_ge(fill, 6)
                    body = E // GE * GE
                    for tile, array in ((dstI, dst), (srcI, src), (typI, edge_type_8), (wgt, edge_weight)):
                        sp.dma_start(tile[:, 0:(NG - 1) * GC].rearrange("p (g c) -> p g c", c=GC),
                                     array[0:body].rearrange("(g p c) -> p g c", p=P, c=GC)).then_inc(edges_in, 16)
                        sp.dma_start(tile[0:PLAST, (NG - 1) * GC:],
                                     array[body:E].rearrange("(p c) -> p c", c=GC)).then_inc(edges_in, 16)
                    sp.dma_start(X[:, 0:NPAD - P].rearrange("p (t f) -> p t f", f=D),
                                 x[0:NPAD - P, :].rearrange("(t p) f -> p t f", p=P)).then_inc(x_in, 16)
                    sp.dma_start(X[0:NLAST, NPAD - P:], x[NPAD - P:N, :]).then_inc(x_in, 16)
                    for slot, ap, n in w_loads:
                        view = ws[:, slot * P:(slot + n) * P]
                        sp.dma_start(view if n == 1 else view.rearrange("p (n h) -> p n h", n=n), ap).then_inc(w_in, 16)
                    for col, ap in half_loads:
                        sp.dma_start(ws[:, col:col + ED], ap).then_inc(w_in, 16)
                    sp.dma_start(wm2[:], L3_gnn_Wm2).then_inc(w_in, 16)
                    sp.dma_start(w0[:], L0_gnn_W).then_inc(small_in, 16)
                    sp.dma_start(wall[:].rearrange("i (h j) -> i h j", h=H),
                                 L2_gnn_W.rearrange("h i j -> i h j")).then_inc(small_in, 16)
                    for b, ap in enumerate(bias_loads):
                        sp.dma_start(bias[:, b, :], ap.unsqueeze(0).to_broadcast([P, D])).then_inc(small_in, 16)
                    sp.dma_start(gcol[:], L3_gnn_global_state.rearrange("(p a) -> p a", a=1)).then_inc(small_in, 16)
                    sp.dma_start(bm2c[:], L3_gnn_bm2.rearrange("(p a) -> p a", a=1)).then_inc(small_in, 16)
                    with nc.allow_non_contiguous_dma("a few columns of biases"):
                        for col, n, ap in col_loads:
                            sp.dma_start(bcol[:, col:col + n], ap).then_inc(small_in, 16)
                        for t in range(2):
                            for h in range(H):
                                sp.dma_start(acol[h * HD:(h + 1) * HD, t:t + 1],
                                             L2_gnn_a[h, t * HD:(t + 1) * HD, :]).then_inc(small_in, 16)
                    sp.wait_ge(edges_in, 8 * 16)
                    for table, tile in ((dst_d, dstI), (src_d, srcI), (row_d, rowI)):
                        if tile is rowI:
                            sp.wait_ge(rowed, 1)
                        sp.dma_start(table.rearrange("g (p c) -> p g c", c=GC),
                                     tile[:].rearrange("p (g c) -> p g c", c=GC)).then_inc(edges_in, 16)
                    sp.wait_ge(edges_in, 11 * 16)
                    sp.wait_ge(x_in, 32)

                @block.gpsimd
                def _(pool):
                    pool.iota(iota_row[:], [[1, P]], base=0, channel_multiplier=0,
                              allow_small_or_imprecise_dtypes=True).then_inc(iotas, 1)
                    pool.iota(iota_colI[:], [[0, 1]], base=0, channel_multiplier=1).then_inc(iotas, 1)
                    pool.iota(h8[:], [[-HD, H]], base=0, channel_multiplier=1,
                              allow_small_or_imprecise_dtypes=True).then_inc(iotas, 1)
                    pool.memset(X[:, NPAD - P:], 0.0).then_inc(fill, 1)
                    pool.memset(dstI[:, (NG - 1) * GC:], FAR).then_inc(fill, 1)
                    pool.memset(srcI[:, (NG - 1) * GC:], 0).then_inc(fill, 1)
                    pool.memset(typI[:, (NG - 1) * GC:], 0).then_inc(fill, 1)
                    pool.memset(wgt[:, (NG - 1) * GC:], 0.0).then_inc(fill, 1)
                    pool.memset(ws[:], 0.0).then_inc(fill, 1)

                @block.tensor
                def _(pe):
                    pe.wait_ge(w_in, 16 * NWL)
                    pe.wait_ge(made, 1)
                    pe.wait_ge(made, 2)
                    for q in range(NW // 4):
                        if q >= 2:
                            pe.wait_ge(wtc, q - 1)
                        for j in range(4):
                            mm = pe.transpose(wps[:, q % 2, j * P:(j + 1) * P], ws[:, (4 * q + j) * P:(4 * q + j + 1) * P],
                                              ident[:])
                        mm.then_inc(wtp, 1)
                    pe.wait_ge(wtc, NW // 4)
                    pe.wait_ge(made, 3)
                    pe.matmul(sps[:, 0:16], W(W_HEADS), a_blk[:], start=True, stop=True)
                    pe.matmul(sps[:, 128:256], vecs[0:ED, 0, :], W(W_M1G)[0:ED, :], start=True, stop=True)
                    pe.matmul(sps[:, 256:384], vecs[0:ED, 0, :], W(W_U1G)[0:ED, :], start=True, stop=True)
                    pe.matmul(sps[:, 384:512], vecs[:, 1, :], W(W_U1A), start=True, stop=True).then_inc(mini, 1)
                    pe.wait_ge(minis, 1)
                    pe.matmul(sps[:, 0:128], wm2[:], W(W_U1A), start=True, stop=True).then_inc(mini, 1)

                @block.scalar
                def _(act):
                    for q in range(NW // 4):
                        act.wait_ge(wtp, q + 1)
                        act.copy(wt[:, q * 512:(q + 1) * 512], wps[:, q % 2, :]).then_inc(wtc, 1)

                @block.vector
                def _(dve):
                    own = Chain(dve, chain)
                    dve.wait_ge(iotas, 3)
                    own.step(V.tensor_copy(iota_col[:], iota_colI[:]))
                    own.step(V.memset(ones[:], 1.0))
                    V.tensor_tensor(out=ident[:], in0=iota_row[:], in1=iota_col[:].to_broadcast([P, P]),
                                    op=ALU.is_equal).then_inc(made, 1)
                    dve.wait_ge(small_in, 16 * (2 + len(bias_loads) + 2 + len(col_loads) + 2 * H))
                    dve.wait_ge(w_in, 16 * NWL)
                    V.tensor_copy(ws[:, W_HEADS * P:(W_HEADS + 1) * P], wall[:]).then_inc(made, 1)
                    own.step(V.tensor_scalar(hmask[:], h8[:], 0.0, None, ALU.is_ge))
                    own.step(V.tensor_scalar(h8[:], h8[:], float(HD), None, ALU.is_lt))
                    own.step(V.tensor_tensor(out=hmask[:], in0=hmask[:], in1=h8[:], op=ALU.mult))
                    for t in range(2):
                        own.step(V.tensor_scalar(a_blk[:, t * H:(t + 1) * H], hmask[:], acol[:, t:t + 1], None, ALU.mult))
                    own.step(V.tensor_scalar(vecs[0:ED, 0, :], ones[0:ED, :], gcol[:, 0:1], None, ALU.mult))
                    own.step(V.tensor_scalar(vecs[:, 1, :], ones[:], bm2c[:, 0:1], None, ALU.mult))
                    V.tensor_tensor(out=bcol[:, C_RZ:C_RZ + 6], in0=bcol[:, C_IH:C_IH + 6], in1=bcol[:, C_HH:C_HH + 6],
                                    op=ALU.add).then_inc(made, 1)
                    dve.wait_ge(edges_in, 8 * 16)
                    V.scalar_tensor_tensor(out=rowI[:], in0=srcI[:], scalar=float(T), in1=typI[:],
                                           op0=ALU.mult, op1=ALU.add).then_inc(rowed, 1)
                    dve.wait_ge(mini, 1)
                    own.step(V.tensor_copy(wa[:], sps[:, 0:16]))
                    own.step(V.tensor_tensor(out=bias[:, B_M1, :], in0=bias[:, B_M1, :], in1=sps[:, 128:256], op=ALU.add))
                    own.step(V.tensor_tensor(out=bias[:, B_U1, :], in0=bias[:, B_U1, :], in1=sps[:, 256:384], op=ALU.add))
                    own.step(V.tensor_copy(bias[:, B_V, :], sps[:, 384:512]))
                    dve.sem_inc(minis, 1)
                    dve.wait_ge(mini, 2)
                    own.step(V.tensor_copy(wcomb[:], sps[:, 0:128]))

        with ExitStack() as ctx:
            ctx.callback(end_stage)
            dstF = sb(ctx, "dstF", [P, NG * GC])
            near = sb(ctx, "near", [P, NG * GC])
            mm_ = sb(ctx, "mm_", [P, 2, P])
            gm = sb(ctx, "gm", [P, 8])
            nwI = sb(ctx, "nwI", [P, 1], I32)
            upto = sb(ctx, "upto", [P, P])
            kk = sb(ctx, "kk", [P, KCAP])
            sel = sb(ctx, "sel", [P, KCAP])
            vals = sb(ctx, "vals", [P, 4])
            kcol = sb(ctx, "kcol", [P, KT])
            it = sb(ctx, "it", [P, KT, 4])
            itI = sb(ctx, "itI", [P, KT, 4], I32)
            kf = sb(ctx, "kf", [1, 4])
            kI = sb(ctx, "kI", [1, 2], I32)
            tps = ps(ctx, "tps", [P, 2, P])
            cps = ps(ctx, "cps", [P, 8])
            ips = ps(ctx, "ips", [P, KT, 4])
            iotas, mins, turned, nwin, cums, sels, itp, table, stored, chain, nw1 = sems(
                "items", "iotas mins turned nwin cums sels itp table stored chain nw1")
            with nc.Block() as block:
                @block.gpsimd
                def _(pool):
                    pool.iota(kk[:], [[1, KCAP]], base=0, channel_multiplier=0,
                              allow_small_or_imprecise_dtypes=True).then_inc(iotas, 1)
                    pool.iota(kcol[:], [[P, KT]], base=0, channel_multiplier=1,
                              allow_small_or_imprecise_dtypes=True).then_inc(iotas, 1)

                @block.vector
                def _(dve):
                    own = Chain(dve, chain)
                    own.step(V.tensor_copy(dstF[:], dstI[:]))
                    own.step(V.memset(mm_[:], 0.0))
                    own.step(V.tensor_reduce(mm_[:, 0, 0:NG], dstF[:].rearrange("p (g c) -> p g c", c=GC), AX, ALU.min))
                    own.step(V.tensor_scalar(near[:], dstF[:], float(N), None, ALU.is_lt))
                    own.step(V.tensor_tensor(out=near[:], in0=near[:], in1=dstF[:], op=ALU.mult))
                    V.tensor_reduce(mm_[:, 1, 0:NG], near[:].rearrange("p (g c) -> p g c", c=GC), AX,
                                    ALU.max).then_inc(mins, 1)
                    dve.wait_ge(turned, 1)
                    own.step(V.tensor_reduce(gm[0:NG, 0:1], tps[0:NG, 0, :], AX, ALU.min))
                    own.step(V.tensor_reduce(gm[0:NG, 1:2], tps[0:NG, 1, :], AX, ALU.max))
                    own.step(V.tensor_tensor(out=nwI[0:NG], in0=gm[0:NG, 1:2], in1=gm[0:NG, 0:1], op=ALU.subtract))
                    own.step(V.tensor_single_scalar(nwI[0:NG], nwI[0:NG], 7, op=ALU.arith_shift_right))
                    own.step(V.tensor_scalar(gm[0:NG, 2:3], nwI[0:NG], 1.0, None, ALU.add))
                    own.step(V.tensor_tensor(out=upto[:], in0=iota_row[:], in1=iota_col[:].to_broadcast([P, P]), op=ALU.is_ge))
                    dve.sem_inc(nwin, 1)
                    dve.wait_ge(cums, 1)
                    own.step(V.tensor_copy(gm[0:NG, 3:4], cps[0:NG, 0:1]))
                    own.step(V.tensor_tensor(out=gm[0:NG, 4:5], in0=gm[0:NG, 3:4], in1=gm[0:NG, 2:3], op=ALU.subtract))
                    own.step(V.scalar_tensor_tensor(out=vals[0:NG, 0:1], in0=gm[0:NG, 4:5], scalar=-float(P),
                                                    in1=gm[0:NG, 0:1], op0=ALU.mult, op1=ALU.add))
                    own.step(V.tensor_copy(vals[0:NG, 1:2], iota_col[0:NG]))
                    own.step(V.memset(vals[0:NG, 2:4], 1.0))
                    dve.wait_ge(iotas, 2)
                    own.step(V.tensor_scalar(sel[0:NG], kk[0:NG], gm[0:NG, 3:4], None, ALU.is_lt))
                    V.scalar_tensor_tensor(out=sel[0:NG], in0=kk[0:NG], scalar=gm[0:NG, 4:5], in1=sel[0:NG],
                                           op0=ALU.is_ge, op1=ALU.mult).then_inc(sels, 1)
                    own.step(V.tensor_copy(kI[:, 0:1], cps[0:1, 4:5]))
                    own.step(V.tensor_scalar(kf[:, 0:1], kI[:, 0:1], 1.0, None, ALU.add))
                    own.step(V.tensor_copy(kI[:, 1:2], kf[:, 0:1]))
                    own.step(V.tensor_single_scalar(nturn[:], kI[:, 1:2], 1, op=ALU.arith_shift_right))
                    dve.wait_ge(itp, 1)
                    own.step(V.tensor_copy(it[:], ips[:]))
                    own.step(V.scalar_tensor_tensor(out=it[:, :, 0], in0=kcol[:], scalar=float(P), in1=it[:, :, 0],
                                                    op0=ALU.mult, op1=ALU.add))
                    own.step(V.tensor_scalar(it[:, :, 3], it[:, :, 2], -NOBASE, NOBASE, ALU.mult, ALU.add))
                    own.step(V.tensor_tensor(out=itI[:, :, 0], in0=it[:, :, 0], in1=it[:, :, 3], op=ALU.add))
                    own.step(V.tensor_tensor(out=itI[:, :, 1], in0=it[:, :, 0], in1=it[:, :, 2], op=ALU.mult))
                    own.step(V.tensor_copy(itI[:, :, 2:4], it[:, :, 1:3]))
                    dve.sem_inc(table, 1)

                @block.tensor
                def _(pe):
                    pe.wait_ge(mins, 1)
                    pe.transpose(tps[:, 0, :], mm_[:, 0, :], ident[:])
                    pe.transpose(tps[:, 1, :], mm_[:, 1, :], ident[:]).then_inc(turned, 1)
                    pe.wait_ge(nwin, 1)
                    pe.matmul(cps[0:NG, 0:1], upto[0:NG, 0:NG], gm[0:NG, 2:3], start=True, stop=True)
                    pe.matmul(cps[0:1, 4:5], ones[0:NG, 0:1], gm[0:NG, 2:3], start=True, stop=True).then_inc(cums, 1)
                    pe.wait_ge(sels, 1)
                    for k in range(KT):
                        mm = pe.matmul(ips[:, k, :], sel[0:NG, k * P:(k + 1) * P], vals[0:NG, :], start=True, stop=True)
                    mm.then_inc(itp, 1)

                @block.sync
                def _(sp):
                    sp.wait_ge(table, 1)
                    sp.dma_start(items_d.rearrange("(k p) c -> p k c", p=P), itI[:]).then_inc(stored, 16)
                    sp.wait_ge(stored, 16)

        with ExitStack() as ctx:
            ctx.callback(end_stage)
            loI = sb(ctx, "loI", [P, NG * GC], I32)
            hiI = sb(ctx, "hiI", [P, NG * GC], I32)
            ohlo = sb(ctx, "ohlo", [P, 2, GC, P])
            ohhi = sb(ctx, "ohhi", [P, 2, GC, 2, NT])
            zero = sb(ctx, "zero", [P, P])
            dps = ps(ctx, "dps", [P, 2, NT])
            made, used, chain, zeroed, summed, dsq, rooted = sems("deg", "made used chain zeroed summed dsq rooted")
            with nc.Block() as block:
                @block.vector
                def _(dve):
                    own = Chain(dve, chain)
                    own.step(V.tensor_single_scalar(loI[:], dstI[:], P - 1, op=ALU.bitwise_and))
                    own.step(V.tensor_single_scalar(hiI[:], dstI[:], 7, op=ALU.arith_shift_right))
                    V.memset(zero[:], 0.0).then_inc(zeroed, 1)
                    with dve.Fori(0, NG // 2) as i:
                        turn = Chain(dve, chain, 2, i)
                        turn.base = i * 2 + 2
                        for s in range(2):
                            at = ds((i * 2 + s) * GC, GC)
                            dve.wait_ge(used, i * 2 + s + 1)
                            V.tensor_tensor(out=ohlo[:, s], in0=over(loI[:, at], P), in1=rows(iota_row[:], GC),
                                            op=ALU.is_equal)
                            turn.step(V.tensor_tensor(out=ohhi[:, s, :, 1, :], in0=over(hiI[:, at], NT),
                                                      in1=rows(iota_row[:, 0:NT], GC), op=ALU.is_equal))
                            V.tensor_tensor(out=ohhi[:, s, :, 0, :], in0=ohhi[:, s, :, 1, :], in1=over(wgt[:, at], NT),
                                            op=ALU.mult).then_inc(made, 1)
                    n = NG // 2 * 2 + 2
                    own.base, own.n = n, 0
                    dve.wait_ge(summed, 1)
                    own.step(V.tensor_scalar(deg[:, 0, :], dps[:, 0, :], 1.0, None, ALU.add))
                    own.step(V.tensor_copy(deg[:, 1, :], dps[:, 1, :]))
                    own.step(V.tensor_scalar(dinv[:], deg[:, 0, :], 1e-30, None, ALU.max))
                    own.step(V.reciprocal(dinv[:], dinv[:]))
                    dve.sem_inc(dsq, 1)
                    dve.wait_ge(rooted, 1)
                    own.step(V.scalar_tensor_tensor(out=dinv[:], in0=deg[:, 0, :], scalar=0.0, in1=dinv[:],
                                                    op0=ALU.is_gt, op1=ALU.mult))
                    own.step(V.tensor_scalar(cntinv[:], deg[:, 1, :], 1.0, None, ALU.max))
                    own.step(V.reciprocal(cntinv[:], cntinv[:]))
                    own.step(V.tensor_scalar(has[:], deg[:, 1, :], 0.0, None, ALU.is_gt))

                @block.scalar
                def _(act):
                    act.wait_ge(dsq, 1)
                    act.activation(dinv[:], dinv[:], ACT.Sqrt).then_inc(rooted, 1)

                @block.tensor
                def _(pe):
                    pe.wait_ge(zeroed, 1)
                    pe.matmul(dps[:], zero[:], zero[:, 0:2 * NT], start=True, stop=False,
                              skip_group_check=True).then_inc(used, 2)
                    with pe.Fori(0, NG // 2) as i:
                        for s in range(2):
                            pe.wait_ge(made, i * 2 + s + 1)
                            for c in range(GC):
                                mm = pe.matmul(dps[:], ohlo[:, s, c, :], ohhi[:, s, c], start=False, stop=False,
                                               skip_group_check=True)
                            mm.then_inc(used, 1)
                    pe.matmul(dps[:], zero[:], zero[:, 0:2 * NT], start=False, stop=True,
                              skip_group_check=True).then_inc(summed, 1)

        def turn_tiles(pe, out_ps, in_sb):
            for t in range(TC):
                mm = pe.transpose(out_ps[:, t * P:(t + 1) * P], in_sb[:, t * P:(t + 1) * P], ident[:])
            return mm

        def times(pe, out_ps, tiles_sb, w, width=D):
            for t in range(TC):
                mm = pe.matmul(out_ps[:, t * width:(t + 1) * width], tiles_sb[:, t * P:(t + 1) * P], w, start=True, stop=True)
            return mm

        def norm(dve, own, r, sq, st, var_ready, rooted, turn, n, k):
            r3, q3 = r.rearrange("p (t f) -> p t f", f=D), sq.rearrange("p (t f) -> p t f", f=D)
            own.step(V.tensor_reduce(st[:, 0:TC], r3, AX, ALU.add))
            own.step(V.tensor_scalar(st[:, 0:TC], st[:, 0:TC], 1.0 / D, None, ALU.mult))
            own.step(V.tensor_tensor(out=r3, in0=r3, in1=over(st[:, 0:TC], D), op=ALU.subtract))
            own.step(V.tensor_tensor(out=q3, in0=r3, in1=r3, op=ALU.mult))
            own.step(V.tensor_reduce(st[:, TC:2 * TC], q3, AX, ALU.add))
            V.tensor_scalar(st[:, TC:2 * TC], st[:, TC:2 * TC], 1.0 / D, EPS, ALU.mult, ALU.add).then_inc(var_ready, 1)
            dve.wait_ge(rooted, turn * n + (k + 1))
            own.step(V.reciprocal(st[:, TC:2 * TC], st[:, TC:2 * TC]))
            own.step(V.tensor_tensor(out=r3, in0=r3, in1=over(st[:, TC:2 * TC], D), op=ALU.mult))

        NORM_STEPS = 7

        def root(act, st, var_ready, rooted, turn, n, k):
            act.wait_ge(var_ready, turn * n + (k + 1))
            act.activation(st[:, TC:2 * TC], st[:, TC:2 * TC], ACT.Sqrt).then_inc(rooted, 1)

        def tiles3(ap):
            return ap.rearrange("p (t f) -> p t f", f=D)

        with ExitStack() as ctx:
            ctx.callback(end_stage)
            xs = sb(ctx, "xs", [P, CW])
            xT = sb(ctx, "xT", [P, CW])
            tp = ps(ctx, "tp", [P, CW])
            hp = ps(ctx, "hp", [P, CW])
            staged, turned, copied, product, scaled, stored = sems("gcn", "staged turned copied product scaled stored")
            with nc.Block() as block:
                @block.scalar
                def _(act):
                    act.sem_inc(scaled, 1)
                    with act.Fori(0, NCH) as i:
                        act.wait_ge(scaled, i + 1)
                        act.copy(xs[:], X[:, ds(i * CW, CW)]).then_inc(staged, 1)
                        act.wait_ge(turned, i + 1)
                        act.copy(xT[:], tp[:]).then_inc(copied, 1)

                @block.tensor
                def _(pe):
                    with pe.Fori(0, NCH) as i:
                        pe.wait_ge(staged, i + 1)
                        turn_tiles(pe, tp, xs).then_inc(turned, 1)
                        pe.wait_ge(copied, i + 1)
                        times(pe, hp, xT, w0[:]).then_inc(product, 1)

                @block.vector
                def _(dve):
                    with dve.Fori(0, NCH) as i:
                        dve.wait_ge(product, i + 1)
                        V.tensor_tensor(out=tiles3(HB[:, ds(i * CW, CW)]), in0=tiles3(hp[:]),
                                        in1=over(dinv[:, ds(i * TC, TC)], D), op=ALU.mult).then_inc(scaled, 1)

                @block.sync
                def _(sp):
                    sp.wait_ge(scaled, NCH + 1)
                    sp.dma_start(gcn_d.rearrange("(t p) f -> p t f", p=P), tiles3(HB[:])).then_inc(stored, 16)
                    sp.wait_ge(stored, 16)

        def aggregate(name, table, index, weighted=False, ex=None, attr=False):
            with ExitStack() as ctx:
                ctx.callback(end_stage)
                G = sb(ctx, f"{name}_G", [P, 2, GC, D])
                OH = sb(ctx, f"{name}_OH", [P, 2, GC, P])
                idx = sb(ctx, f"{name}_idx", [P, 2, GC], I32)
                itm = sb(ctx, f"{name}_itm", [P, 2, 4], I32)
                wp = [ps(ctx, f"{name}_wp{s}", [P, 512]) for s in range(2)]
                item_ready = sems(name, "item_ready0 item_ready1")
                gathered = sems(name, "gathered0 gathered1")
                slot_free = sems(name, "slot_free0 slot_free1")
                added = sems(name, "added0 added1")
                idx_ready = sems(name, "idx_ready0 idx_ready1")
                oh_ready, chain, rows_ready = sems(name, "oh_ready chain rows_ready")
                if attr:
                    at_ = sb(ctx, f"{name}_at", [P, 2, GC, ED])
                    atT = sb(ctx, f"{name}_atT", [P, GC // 2, P])
                    tp = ps(ctx, f"{name}_tp", [P, GC // 2, P])
                    ep = ps(ctx, f"{name}_ep", [P, 2, GC // 2, P])
                    attr_in = sems(name, "attr_in0 attr_in1")
                    turned, copied, ep_ready, summed = sems(name, "turned copied ep_ready summed")
                    at_last = edge_attr_64[(NG - 1) * GE:E, :].rearrange("(p c) f -> p (c f)", c=GC)
                    at_rows = edge_attr_64[0:(NG - 1) * GE, :].rearrange("(g p c) f -> g p (c f)", p=P, c=GC)
                with nc.Block() as block:
                    @block.sync
                    def _(sp):
                        for s in range(2):
                            sp.wait_ge(added[s], 1)
                        n = sp.value_load(nturn[0:1, 0:1], min_val=1, max_val=KCAP // 2)
                        with sp.Fori(0, n) as i:
                            for s in range(2):
                                sp.wait_ge(added[s], i + 1)
                                sp.dma_start(itm[:, s, :], items_d[ds(i * 2 + s, 1), :].to_broadcast([P, 4])
                                             ).then_inc(item_ready[s], 16)
                                sp.wait_ge(item_ready[s], i * 16 + 16)
                                passed(sp, tick)
                                g = sp.value_load(itm[0:1, s, 2:3], min_val=0, max_val=NG - 1)
                                sp.dma_start(idx[:, s, :], index[ds(g, 1), :].rearrange("a (p c) -> (a p) c", c=GC)
                                             ).then_inc(idx_ready[s], 16)
                                if attr:
                                    with sp.If(g < NG - 1):
                                        g = sp.value_load(itm[0:1, s, 2:3], min_val=0, max_val=NG - 2)
                                        sp.dma_start(at_[:, s].rearrange("p c f -> p (c f)"),
                                                     at_rows[ds(g, 1)].rearrange("a p f -> (a p) f")).then_inc(attr_in[s], 16)
                                    with sp.Else():
                                        sp.dma_start(at_[0:PLAST, s].rearrange("p c f -> p (c f)"), at_last
                                                     ).then_inc(attr_in[s], 16)

                    @block.scalar
                    def _(act):
                        if attr:
                            n = act.value_load(nturn[0:1, 0:1], min_val=1, max_val=KCAP // 2)
                            with act.Fori(0, n) as i:
                                for s in range(2):
                                    act.wait_ge(turned, i * 2 + s + 1)
                                    act.copy(atT[:], tp[:]).then_inc(copied, 1)
                                    act.wait_ge(summed, i * 2 + s + 1)
                                    act.activation(G[:, s], G[:, s], ACT.Relu).then_inc(rows_ready, 1)

                    @block.gpsimd
                    def _(pool):
                        n = pool.value_load(nturn[0:1, 0:1], min_val=1, max_val=KCAP // 2)
                        with pool.Fori(0, n) as i:
                            for s in range(2):
                                pool.wait_ge(idx_ready[s], i * 16 + 16)
                                passed(pool, tick)
                                for c in range(GC):
                                    pool.indirect_dma_start(
                                        G[:, s, c, :], None, table,
                                        bass.IndirectOffsetOnAxis(ap=idx[:, s, c:c + 1].bitcast(U32), axis=0)
                                    ).then_inc(gathered[s], 16)

                    @block.vector
                    def _(dve):
                        V.memset(acc[:], 0.0).then_inc(chain, 1)
                        dve.wait_ge(chain, 1)
                        if attr:
                            for s in range(2):
                                V.memset(at_[:, s], 0.0).then_inc(chain, 1)
                            dve.wait_ge(chain, 3)
                        first = 3 if attr else 1
                        for s in range(2):
                            dve.sem_inc(added[s], 1)
                        n = dve.value_load(nturn[0:1, 0:1], min_val=1, max_val=KCAP // 2)
                        with dve.Fori(0, n) as i:
                            own = Chain(dve, chain, 2, i)
                            own.base = i * 2 + first
                            g = [None, None]
                            col = [None, None]
                            for s in range(2):
                                dve.wait_ge(item_ready[s], i * 16 + 16)
                                dve.wait_ge(slot_free[s], i + 1)
                                passed(dve, tick)
                                g[s] = dve.value_load(itm[0:1, s, 2:3], min_val=0, max_val=NG - 1)
                                col[s] = dve.value_load(itm[0:1, s, 1:2], min_val=0, max_val=N - 1)
                                oh = V.scalar_tensor_tensor(
                                    out=OH[:, s], in0=over(dstI[:, ds(g[s] * GC, GC)], P), scalar=itm[:, s, 0:1],
                                    in1=rows(iota_row[:], GC), op0=ALU.subtract, op1=ALU.is_equal)
                                if weighted:
                                    own.step(oh)
                                    oh = V.tensor_tensor(out=OH[:, s], in0=OH[:, s], in1=over(wgt[:, ds(g[s] * GC, GC)], P),
                                                         op=ALU.mult)
                                oh.then_inc(oh_ready, 1)
                            for s in range(2):
                                if ex is not None:
                                    dve.wait_ge(gathered[s], i * 16 * GC + 16 * GC)
                                    V.tensor_tensor(out=G[:, s].rearrange("p c (h j) -> p (c h) j", h=H),
                                                    in0=G[:, s].rearrange("p c (h j) -> p (c h) j", h=H),
                                                    in1=over(ex[:, ds(g[s] * GC * H, GC * H)], HD),
                                                    op=ALU.mult).then_inc(rows_ready, 1)
                                if attr:
                                    dve.wait_ge(gathered[s], i * 16 * GC + 16 * GC)
                                    dve.wait_ge(ep_ready, i * 2 + s + 1)
                                    g4 = G[:, s].rearrange("p (q a) f -> p q a f", a=2)
                                    V.tensor_tensor(out=g4, in0=g4, in1=ep[:].rearrange("p a q f -> p q a f"), op=ALU.add).then_inc(summed, 1)
                                dve.wait_ge(slot_free[s], i + 2)
                                dve.wait_ge(added[1 - s], i + 1 + s)
                                V.tensor_tensor(out=acc[:, ds(col[s], P)], in0=acc[:, ds(col[s], P)], in1=wp[s][:, 0:P],
                                                op=ALU.add).then_inc(added[s], 1)

                    @block.tensor
                    def _(pe):
                        for s in range(2):
                            pe.sem_inc(slot_free[s], 1)
                        n = pe.value_load(nturn[0:1, 0:1], min_val=1, max_val=KCAP // 2)
                        with pe.Fori(0, n) as i:
                            for s in range(2):
                                if attr:
                                    pe.wait_ge(attr_in[s], i * 16 + 16)
                                    for c in range(GC // 2):
                                        mm = pe.transpose(tp[:, c, :], at_[:, s, 2 * c:2 * c + 2].rearrange("p a f -> p (a f)"),
                                                          ident[:])
                                    mm.then_inc(turned, 1)
                                    pe.wait_ge(copied, i * 2 + s + 1)
                                    for c in range(GC):
                                        h = c % 2 * ED
                                        mm = pe.matmul(ep[:, c % 2, c // 2, :], atT[h:h + ED, c // 2, :], W(W_M1E)[h:h + ED, :],
                                                       start=True, stop=True)
                                    mm.then_inc(ep_ready, 1)
                                pe.wait_ge(gathered[s], i * 16 * GC + 16 * GC)
                                pe.wait_ge(oh_ready, i * 2 + s + 1)
                                if ex is not None or attr:
                                    pe.wait_ge(rows_ready, i * 2 + s + 1)
                                pe.wait_ge(added[s], i + 1)
                                for c in range(GC):
                                    mm = pe.matmul(wp[s][:, 0:P], G[:, s, c, :], OH[:, s, c, :], start=c == 0, stop=c == GC - 1)
                                mm.then_inc(slot_free[s], 1)

        aggregate("gcn_edges", gcn_d, src_d, weighted=True)

        with ExitStack() as ctx:
            ctx.callback(end_stage)
            st_ = sb(ctx, "st_", [P, CW])
            r = sb(ctx, "r", [P, CW])
            sq = sb(ctx, "sq", [P, CW])
            xT = sb(ctx, "xT1", [P, CW])
            st = sb(ctx, "st", [P, 2 * TC])
            ap_ = ps(ctx, "ap_", [P, CW])
            tp = ps(ctx, "tp1", [P, CW])
            hp = ps(ctx, "hp1", [P, 2, 512])
            staged, turned, chain, var_ready, rooted, normed, xturned, copied, product, done = sems(
                "n0", "staged turned chain var_ready rooted normed xturned copied product done")
            HW_ = CW // 2
            with nc.Block() as block:
                @block.scalar
                def _(act):
                    act.sem_inc(done, 1)
                    with act.Fori(0, NCH) as i:
                        act.wait_ge(done, i + 1)
                        act.copy(st_[:], acc[:, ds(i * CW, CW)]).then_inc(staged, 1)
                        root(act, st, var_ready, rooted, i, 1, 0)
                        act.wait_ge(xturned, i + 1)
                        act.copy(xT[:], tp[:]).then_inc(copied, 1)
                        act.wait_ge(product, i + 1)
                        act.activation(HB[:, ds(i * CW, CW)].rearrange("p (a n) -> p a n", a=2), hp[:, :, 0:HW_], ACT.Relu,
                                       bias=bcol[:, C_PROJ:C_PROJ + 1]).then_inc(done, 1)

                @block.tensor
                def _(pe):
                    with pe.Fori(0, NCH) as i:
                        pe.wait_ge(staged, i + 1)
                        turn_tiles(pe, ap_, st_).then_inc(turned, 1)
                        pe.wait_ge(normed, i + 1)
                        turn_tiles(pe, tp, r).then_inc(xturned, 1)
                        pe.wait_ge(copied, i + 1)
                        for a in range(2):
                            mm = pe.matmul(hp[:, a, 0:HW_], W(W_PROJ), xT[:, a * HW_:(a + 1) * HW_], start=True, stop=True)
                        mm.then_inc(product, 1)

                @block.vector
                def _(dve):
                    with dve.Fori(0, NCH) as i:
                        own = Chain(dve, chain, 3 + NORM_STEPS + 2, i)
                        at, r3 = ds(i * CW, CW), tiles3(r[:])
                        dve.wait_ge(turned, i + 1)
                        own.step(V.tensor_tensor(out=r[:], in0=HB[:, at], in1=ap_[:], op=ALU.add))
                        own.step(V.tensor_tensor(out=r3, in0=r3, in1=over(dinv[:, ds(i * TC, TC)], D), op=ALU.mult))
                        own.step(V.tensor_tensor(out=r3, in0=r3, in1=rows(bias[:, B_L0, :], TC), op=ALU.add))
                        own.step(V.tensor_tensor(out=r[:], in0=r[:], in1=X[:, at], op=ALU.add))
                        norm(dve, own, r[:], sq[:], st, var_ready, rooted, i, 1, 0)
                        passed(dve, tick)
                        own.step(V.tensor_copy(X[:, at], r[:]))
                        dve.sem_inc(normed, 1)
                        assert own.n == 3 + NORM_STEPS + 2, own.n

        def transform(l):
            with ExitStack() as ctx:
                ctx.callback(end_stage)
                hs = sb(ctx, f"hs{l}", [P, CW])
                tb = sb(ctx, f"tb{l}", [P, 2, T * D])
                pp = [ps(ctx, f"pp{l}{s}", [P, 2, 512]) for s in range(2)]
                staged, product = sems(f"tr{l}", "staged product")
                copied = sems(f"tr{l}", "copied0 copied1")
                stored = sems(f"tr{l}", "stored0 stored1")
                rows_d = trans_d.rearrange("(t p) f -> t p f", p=P)
                with nc.Block() as block:
                    @block.tensor
                    def _(pe):
                        for s in range(2):
                            pe.sem_inc(copied[s], 1)
                        with pe.Fori(0, NCH) as i:
                            pe.wait_ge(staged, i + 1)
                            for t in range(TC):
                                s = t % 2
                                per = TC // 2 + (1 - s)
                                pe.wait_ge(copied[s], i * per + t // 2 + 1)
                                for a in range(2):
                                    mm = pe.matmul(pp[s][:, a, :], hs[:, t * P:(t + 1) * P],
                                                   W(W_EDGE + 8 * l + 4 * a, 4), start=True, stop=True)
                                mm.then_inc(product, 1)

                    @block.scalar
                    def _(act):
                        with act.Fori(0, NCH) as i:
                            act.copy(hs[:], HB[:, ds(i * CW, CW)]).then_inc(staged, 1)
                            for t in range(0, TC, 2):
                                act.wait_ge(product, i * TC + t + 1)
                                act.wait_ge(stored[0], (i * (TC // 2 + 1) + t // 2 + 1) * 16)
                                act.copy(tb[:, 0, :], pp[0][:].rearrange("p a f -> p (a f)")).then_inc(copied[0], 1)

                    @block.vector
                    def _(dve):
                        with dve.Fori(0, NCH) as i:
                            for t in range(1, TC, 2):
                                dve.wait_ge(product, i * TC + t + 1)
                                dve.wait_ge(stored[1], (i * (TC // 2) + t // 2 + 1) * 16)
                                V.tensor_copy(tb[:, 1, :], pp[1][:].rearrange("p a f -> p (a f)")).then_inc(copied[1], 1)

                    @block.sync
                    def _(sp):
                        for s in range(2):
                            sp.sem_inc(stored[s], 16)
                        with sp.Fori(0, NCH) as i:
                            for t in range(TC):
                                s = t % 2
                                per = TC // 2 + (1 - s)
                                sp.wait_ge(copied[s], i * per + t // 2 + 2)
                                sp.dma_start(rows_d[ds(i * TC + t, 1)].rearrange("a p f -> (a p) f"),
                                             tb[:, s, :]).then_inc(stored[s], 16)
                        sp.wait_ge(stored[0], (NCH * (TC // 2 + 1) + 1) * 16)
                        sp.wait_ge(stored[1], (NCH * (TC // 2) + 1) * 16)

        def gru(l):
            with ExitStack() as ctx:
                ctx.callback(end_stage)
                HW_ = CW // 2
                gp = [ps(ctx, f"gp{l}{k}", [P, 2, 512]) for k in range(4)]
                rg = sb(ctx, f"rg{l}", [P, 2, HW_])
                zg = sb(ctx, f"zg{l}", [P, 2, HW_])
                ng = sb(ctx, f"ng{l}", [P, 2, HW_])
                product, gates, pre, tanhed, chain, done = sems(f"gru{l}", "product gates pre tanhed chain done")
                with nc.Block() as block:
                    @block.tensor
                    def _(pe):
                        pe.sem_inc(done, 1)
                        with pe.Fori(0, NCH) as i:
                            pe.wait_ge(done, i + 1)
                            for a in range(2):
                                x_ = acc[:, ds(i * CW + a * HW_, HW_)]
                                h_ = HB[:, ds(i * CW + a * HW_, HW_)]
                                for k in range(2):
                                    pe.matmul(gp[k][:, a, 0:HW_], W(W_IH + 3 * l + k), x_, start=True, stop=False)
                                    pe.matmul(gp[k][:, a, 0:HW_], W(W_HH + 3 * l + k), h_, start=False, stop=True)
                                pe.matmul(gp[2][:, a, 0:HW_], W(W_IH + 3 * l + 2), x_, start=True, stop=True)
                                mm = pe.matmul(gp[3][:, a, 0:HW_], W(W_HH + 3 * l + 2), h_, start=True, stop=True)
                            mm.then_inc(product, 1)

                    @block.scalar
                    def _(act):
                        with act.Fori(0, NCH) as i:
                            act.wait_ge(product, i + 1)
                            rz = C_RZ + 3 * l
                            act.activation(rg[:], gp[0][:, :, 0:HW_], ACT.Sigmoid, bias=bcol[:, rz:rz + 1]).then_inc(gates, 1)
                            act.activation(zg[:], gp[1][:, :, 0:HW_], ACT.Sigmoid,
                                           bias=bcol[:, rz + 1:rz + 2]).then_inc(gates, 1)
                            act.wait_ge(pre, i + 1)
                            act.activation(ng[:], ng[:], ACT.Tanh,
                                           bias=bcol[:, C_IH + 3 * l + 2:C_IH + 3 * l + 3]).then_inc(tanhed, 1)

                    @block.vector
                    def _(dve):
                        with dve.Fori(0, NCH) as i:
                            own = Chain(dve, chain, 4, i)
                            h_ = HB[:, ds(i * CW, CW)].rearrange("p (a n) -> p a n", a=2)
                            dve.wait_ge(gates, i * 2 + 2)
                            hh = C_HH + 3 * l + 2
                            own.step(V.scalar_tensor_tensor(out=ng[:], in0=gp[3][:, :, 0:HW_], scalar=bcol[:, hh:hh + 1],
                                                            in1=rg[:], op0=ALU.add, op1=ALU.mult))
                            V.tensor_tensor(out=ng[:], in0=ng[:], in1=gp[2][:, :, 0:HW_], op=ALU.add).then_inc(pre, 1)
                            dve.wait_ge(tanhed, i + 1)
                            own.step(V.tensor_tensor(out=rg[:], in0=h_, in1=ng[:], op=ALU.subtract))
                            own.step(V.tensor_tensor(out=rg[:], in0=rg[:], in1=zg[:], op=ALU.mult))
                            own.step(V.tensor_tensor(out=rg[:], in0=rg[:], in1=ng[:], op=ALU.add))
                            V.tensor_scalar(h_, rg[:], 0.0, None, ALU.max).then_inc(done, 1)

        for l in range(2):
            transform(l)
            aggregate(f"ggnn{l}_edges", trans_d.rearrange("n (t f) -> (n t) f", t=T), row_d)
            gru(l)

        gat = whole.enter_context(ExitStack())
        S = sb(gat, "S", [P, NT, 2 * H])
        with ExitStack() as ctx:
            ctx.callback(end_stage)
            hs = sb(ctx, "hs2", [P, CW])
            r = sb(ctx, "r2", [P, CW])
            sq = sb(ctx, "sq2", [P, CW])
            xT = sb(ctx, "xT2", [P, CW])
            st = sb(ctx, "st2", [P, 2 * TC])
            op_ = ps(ctx, "op_", [P, CW])
            tp = ps(ctx, "tp2", [P, CW])
            xp = ps(ctx, "xp", [P, CW])
            sp_ = ps(ctx, "sp_", [P, TC * 2 * H])
            staged, product, chain, var_ready, rooted, normed, xturned, copied, heads, done = sems(
                "n1", "staged product chain var_ready rooted normed xturned copied heads done")
            with nc.Block() as block:
                @block.scalar
                def _(act):
                    act.sem_inc(done, 1)
                    with act.Fori(0, NCH) as i:
                        act.wait_ge(done, i + 1)
                        act.copy(hs[:], HB[:, ds(i * CW, CW)]).then_inc(staged, 1)
                        root(act, st, var_ready, rooted, i, 1, 0)
                        act.wait_ge(xturned, i + 1)
                        act.copy(xT[:], tp[:]).then_inc(copied, 1)

                @block.tensor
                def _(pe):
                    with pe.Fori(0, NCH) as i:
                        pe.wait_ge(staged, i + 1)
                        times(pe, op_, hs, W(W_OUT)).then_inc(product, 1)
                        pe.wait_ge(normed, i + 1)
                        turn_tiles(pe, tp, r).then_inc(xturned, 1)
                        pe.wait_ge(copied, i + 1)
                        times(pe, xp, xT, wall[:])
                        times(pe, sp_, xT, wa[:], width=2 * H).then_inc(heads, 1)

                @block.vector
                def _(dve):
                    with dve.Fori(0, NCH) as i:
                        own = Chain(dve, chain, 2 + NORM_STEPS + 2, i)
                        at, r3 = ds(i * CW, CW), tiles3(r[:])
                        dve.wait_ge(product, i + 1)
                        own.step(V.tensor_tensor(out=r[:], in0=X[:, at], in1=op_[:], op=ALU.add))
                        own.step(V.tensor_tensor(out=r3, in0=r3, in1=rows(bias[:, B_OUT, :], TC), op=ALU.add))
                        norm(dve, own, r[:], sq[:], st, var_ready, rooted, i, 1, 0)
                        passed(dve, tick)
                        own.step(V.tensor_copy(X[:, at], r[:]))
                        dve.sem_inc(normed, 1)
                        dve.wait_ge(heads, i + 1)
                        passed(dve, tick)
                        own.step(V.tensor_copy(S[:, ds(i * TC, TC), :], sp_[:].rearrange("p (t s) -> p t s", t=TC)))
                        passed(dve, tick)
                        V.tensor_copy(HB[:, at], xp[:]).then_inc(done, 1)
                        assert own.n == 2 + NORM_STEPS + 2

        ex = sb(gat, "ex", [P, NG * GC * H])
        with ExitStack() as ctx:
            ctx.callback(end_stage)
            sjm = sb(ctx, "sjm", [P, NT, H])
            real = sb(ctx, "real", [P, NT])
            A = sb(ctx, "A", [P, NT, 2 * H])
            J = sb(ctx, "J", [P, NT, 2 * H])
            zr = sb(ctx, "zr", [P, 2 * H])
            mx = sb(ctx, "mx", [P, H])
            m8 = sb(ctx, "m8", [H, 1])
            dg = sb(ctx, "dg", [H, H])
            mb = sb(ctx, "mb", [P, H])
            mp = ps(ctx, "mp", [P, P])
            bp = ps(ctx, "bp", [P, H])
            iotas, maxed, turned, diag, spread, tables, stored, chain = sems(
                "max", "iotas maxed turned diag spread tables stored chain")
            with nc.Block() as block:
                @block.gpsimd
                def _(pool):
                    pool.iota(real[:], [[P, NT]], base=0, channel_multiplier=1,
                              allow_small_or_imprecise_dtypes=True).then_inc(iotas, 1)

                @block.vector
                def _(dve):
                    own = Chain(dve, chain)
                    own.step(V.memset(ex[:], 0.0))
                    own.step(V.memset(zr[:], 0.0))
                    dve.wait_ge(iotas, 1)
                    own.step(V.tensor_scalar(real[:], real[:], float(N), None, ALU.is_lt))
                    own.step(V.tensor_tensor(out=sjm[:], in0=S[:, :, H:2 * H], in1=over(real[:], H), op=ALU.mult))
                    own.step(V.tensor_scalar(real[:], real[:], 3e38, -3e38, ALU.mult, ALU.add))
                    own.step(V.tensor_tensor(out=sjm[:], in0=sjm[:], in1=over(real[:], H), op=ALU.add))
                    V.tensor_reduce(mx[:], sjm[:].rearrange("p t h -> p h t"), AX, ALU.max).then_inc(maxed, 1)
                    dve.wait_ge(turned, 1)
                    own.step(V.tensor_reduce(m8[:], mp[0:H, :], AX, ALU.max))
                    V.tensor_scalar(dg[:], ident[0:H, 0:H], m8[:, 0:1], None, ALU.mult).then_inc(diag, 1)
                    dve.wait_ge(spread, 1)
                    own.step(V.tensor_copy(mb[:], bp[:]))
                    own.step(V.tensor_copy(A[:, :, 0:H], S[:, :, 0:H]))
                    own.step(V.tensor_tensor(out=J[:, :, 0:H], in0=S[:, :, 0:H], in1=rows(mb[:], NT), op=ALU.add))
                    own.step(V.scalar_tensor_tensor(out=A[:, :, H:2 * H], in0=J[:, :, 0:H], scalar=ALPHA, in1=J[:, :, 0:H],
                                                    op0=ALU.mult, op1=ALU.max))
                    own.step(V.memset(J[:, :, H:2 * H], 1.0))
                    own.step(V.tensor_copy(J[:, :, 0:H], S[:, :, H:2 * H]))
                    dve.sem_inc(tables, 1)

                @block.tensor
                def _(pe):
                    pe.wait_ge(maxed, 1)
                    pe.transpose(mp[0:H, :], mx[:], ident[:]).then_inc(turned, 1)
                    pe.wait_ge(diag, 1)
                    pe.matmul(bp[:], ones[0:H, :], dg[:], start=True, stop=True).then_inc(spread, 1)

                @block.sync
                def _(sp):
                    sp.wait_ge(tables, 1)
                    sp.dma_start(att_d.rearrange("(t p) s -> p t s", p=P), A[:]).then_inc(stored, 16)
                    sp.dma_start(sj_d[0:NPAD].rearrange("(t p) s -> p t s", p=P), J[:]).then_inc(stored, 16)
                    sp.dma_start(sj_d[NPAD:ACCW], zr[:]).then_inc(stored, 16)
                    sp.wait_ge(stored, 48)

        den = sb(gat, "den", [P, NT, H])
        with ExitStack() as ctx:
            ctx.callback(end_stage)
            G = sb(ctx, "at_G", [P, 2, GC, 2 * H])
            dr = sb(ctx, "dr", [P, GE], I32)
            ohT = acc[:, 0:GE].rearrange("p (c e) -> p c e", c=GC)
            ohl = acc[:, GE:2 * GE].rearrange("p (c n) -> p c n", c=GC)
            exh = sb(ctx, "exh", [P, 2, 4, NT, H])
            sjw = sb(ctx, "sjw", [P, 2, 2 * H])
            idx = sb(ctx, "at_idx", [P, 2, GC], I32)
            srch = sb(ctx, "srch", [P, 2, GC], I32)
            srcl = sb(ctx, "srcl", [P, 2, GC], I32)
            itm = sb(ctx, "at_itm", [P, 2, 4], I32)
            e_ = sb(ctx, "e_", [P, GC, H])
            x_ = sb(ctx, "x_", [P, GC, H])
            em = sb(ctx, "em", [P, GC, H])
            zero = sb(ctx, "zero2", [P, NT * H])
            jp = ps(ctx, "jp", [P, GC, 2 * H])
            dp = ps(ctx, "dp", [P, NT * H])
            item_ready = sems("at", "item_ready0 item_ready1")
            gathered = sems("at", "gathered0 gathered1")
            done = sems("at", "done0 done1")
            idx_ready = sems("at", "idx_ready0 idx_ready1")
            window_in, oht_ready, sj_ready, chain, diff, exped, exh_ready, exh_free, zeroed, summed = sems(
                "at", "window_in oht_ready sj_ready chain diff exped exh_ready exh_free zeroed summed")
            q4 = GC // 4
            with nc.Block() as block:
                @block.sync
                def _(sp):
                    n = sp.value_load(nturn[0:1, 0:1], min_val=1, max_val=KCAP // 2)
                    with sp.Fori(0, n) as i:
                        for s in range(2):
                            sp.wait_ge(done[s], i + 1)
                            sp.dma_start(itm[:, s, :], items_d[ds(i * 2 + s, 1), :].to_broadcast([P, 4])
                                         ).then_inc(item_ready[s], 16)
                            sp.wait_ge(item_ready[s], i * 16 + 16)
                            passed(sp, tick)
                            g = sp.value_load(itm[0:1, s, 2:3], min_val=0, max_val=NG - 1)
                            sp.dma_start(idx[:, s, :], src_d[ds(g, 1), :].rearrange("a (p c) -> (a p) c", c=GC)
                                         ).then_inc(idx_ready[s], 16)
                            sp.wait_ge(sj_ready, i * 2 + s + 1)
                            passed(sp, tick)
                            col = sp.value_load(itm[0:1, s, 1:2], min_val=0, max_val=N - 1)
                            sp.dma_start(dr[:], dst_d[ds(g, 1), :].to_broadcast([P, GE])
                                         ).then_inc(window_in, 16)
                            sp.dma_start(sjw[:, s, :], sj_d[ds(col, P), :]).then_inc(window_in, 16)

                @block.scalar
                def _(act):
                    n = act.value_load(nturn[0:1, 0:1], min_val=1, max_val=KCAP // 2)
                    with act.Fori(0, n) as i:
                        for s in range(2):
                            act.wait_ge(diff, i * 2 + s + 1)
                            act.activation(x_[:], e_[:], ACT.Exp).then_inc(exped, 1)

                @block.gpsimd
                def _(pool):
                    n = pool.value_load(nturn[0:1, 0:1], min_val=1, max_val=KCAP // 2)
                    with pool.Fori(0, n) as i:
                        for s in range(2):
                            pool.wait_ge(idx_ready[s], i * 16 + 16)
                            passed(pool, tick)
                            for c in range(GC):
                                pool.indirect_dma_start(
                                    G[:, s, c, :], None, att_d,
                                    bass.IndirectOffsetOnAxis(ap=idx[:, s, c:c + 1].bitcast(U32), axis=0)
                                ).then_inc(gathered[s], 16)

                @block.tensor
                def _(pe):
                    pe.wait_ge(zeroed, 1)
                    pe.matmul(dp[:], zero[:, 0:P], zero[:], start=True, stop=False, skip_group_check=True).then_inc(exh_free, 2)
                    pe.sem_inc(sj_ready, 1)
                    n = pe.value_load(nturn[0:1, 0:1], min_val=1, max_val=KCAP // 2)
                    with pe.Fori(0, n) as i:
                        for s in range(2):
                            pe.wait_ge(oht_ready, i * 2 + s + 1)
                            for c in range(GC):
                                mm = pe.matmul(jp[:, c, :], ohT[:, c, :], sjw[:, s, :], start=True, stop=True)
                            mm.then_inc(sj_ready, 1)
                            for q in range(q4):
                                pe.wait_ge(exh_ready, i * (2 * q4) + s * q4 + q + 1)
                                for c in range(4):
                                    mm = pe.matmul(dp[:], ohl[:, 4 * q + c, :], exh[:, q % 2, c].rearrange("p t h -> p (t h)"),
                                                   start=False, stop=False, skip_group_check=True)
                                mm.then_inc(exh_free, 1)
                    pe.matmul(dp[:], zero[:, 0:P], zero[:], start=False, stop=True, skip_group_check=True).then_inc(summed, 1)

                @block.vector
                def _(dve):
                    V.memset(zero[:], 0.0).then_inc(zeroed, 1)
                    for s in range(2):
                        dve.sem_inc(done[s], 1)
                    n = dve.value_load(nturn[0:1, 0:1], min_val=1, max_val=KCAP // 2)
                    STEPS = 2 * 7
                    with dve.Fori(0, n) as i:
                        own = Chain(dve, chain, STEPS, i)
                        for s in range(2):
                            dve.wait_ge(item_ready[s], i * 16 + 16)
                            passed(dve, tick)
                            g = dve.value_load(itm[0:1, s, 2:3], min_val=0, max_val=NG - 1)
                            dve.wait_ge(window_in, (i * 2 + s) * 32 + 32)
                            V.tensor_scalar(ohT, dr[:].rearrange("n (p c) -> n c p", c=GC), itm[:, s, 0:1], iota_colI[:, 0:1],
                                            ALU.subtract, ALU.is_equal).then_inc(oht_ready, 1)
                            dve.wait_ge(idx_ready[s], i * 16 + 16)
                            own.step(V.tensor_single_scalar(srcl[:, s, :], idx[:, s, :], P - 1, op=ALU.bitwise_and))
                            own.step(V.tensor_single_scalar(srch[:, s, :], idx[:, s, :], 7, op=ALU.arith_shift_right))
                            dve.wait_ge(exh_free, i * (2 * q4) + s * q4 + 2)
                            V.tensor_tensor(out=ohl, in0=over(srcl[:, s, :], P), in1=rows(iota_row[:], GC), op=ALU.is_equal)
                            dve.wait_ge(gathered[s], i * 16 * GC + 16 * GC)
                            dve.wait_ge(sj_ready, i * 2 + s + 2)
                            own.step(V.tensor_tensor(out=x_[:], in0=G[:, s, :, 0:H], in1=jp[:, :, 0:H], op=ALU.add))
                            own.step(V.scalar_tensor_tensor(out=e_[:], in0=x_[:], scalar=ALPHA, in1=x_[:], op0=ALU.mult, op1=ALU.max))
                            own.step(V.tensor_tensor(out=e_[:], in0=e_[:], in1=G[:, s, :, H:2 * H], op=ALU.subtract))
                            V.tensor_scalar(e_[:], e_[:], 0.0, None, ALU.min).then_inc(diff, 1)
                            dve.wait_ge(exped, i * 2 + s + 1)
                            own.step(V.tensor_tensor(out=em[:], in0=x_[:], in1=jp[:, :, H:2 * H], op=ALU.mult))
                            exg = ex[:, ds(g * GC * H, GC * H)].rearrange("p (c h) -> p c h", h=H)
                            own.step(V.tensor_tensor(out=exg, in0=exg, in1=em[:], op=ALU.add))
                            for q in range(q4):
                                dve.wait_ge(exh_free, i * (2 * q4) + s * q4 + q + 1)
                                for c in range(4):
                                    k = 4 * q + c
                                    last = V.scalar_tensor_tensor(
                                        out=exh[:, q % 2, c], in0=over(iota_row[:, 0:NT], H), scalar=srch[:, s, k:k + 1],
                                        in1=rows(em[:, k, :], NT), op0=ALU.is_equal, op1=ALU.mult)
                                last.then_inc(exh_ready, 1)
                            dve.sem_inc(done[s], 1)
                        assert own.n == STEPS, own.n
                    dve.wait_ge(summed, 1)
                    V.tensor_copy(den[:].rearrange("p t h -> p (t h)"), dp[:]).then_inc(zeroed, 1)
                    dve.wait_ge(zeroed, 2)

        with ExitStack() as ctx:
            ctx.callback(end_stage)
            chain, scaled, stored = sems("heads", "chain scaled stored")
            with nc.Block() as block:
                @block.vector
                def _(dve):
                    own = Chain(dve, chain)
                    own.step(V.tensor_scalar(den[:], den[:], 1e-30, None, ALU.max))
                    own.step(V.reciprocal(den[:], den[:]))
                    hb = HB[:].rearrange("p (q j) -> p q j", j=HD)
                    V.tensor_tensor(out=hb, in0=hb, in1=over(den[:].rearrange("p t h -> p (t h)"), HD),
                                    op=ALU.mult).then_inc(scaled, 1)

                @block.sync
                def _(sp):
                    sp.wait_ge(scaled, 1)
                    sp.dma_start(heads_d.rearrange("(t p) f -> p t f", p=P), tiles3(HB[:])).then_inc(stored, 16)
                    sp.wait_ge(stored, 16)

        aggregate("gat_edges", heads_d, src_d, ex=ex)
        gat.close()

        with ExitStack() as ctx:
            ctx.callback(end_stage)
            st_ = sb(ctx, "st3_", [P, CW])
            r = sb(ctx, "r3", [P, CW])
            sq = sb(ctx, "sq3", [P, CW])
            xT = sb(ctx, "xT3", [P, CW])
            st = sb(ctx, "st3", [P, 2 * TC])
            ap_ = ps(ctx, "ap3", [P, CW])
            tp = ps(ctx, "tp3", [P, CW])
            hp = ps(ctx, "hp3", [P, CW])
            staged, turned, chain, var_ready, rooted, normed, xturned, copied, product, done, stored = sems(
                "n2", "staged turned chain var_ready rooted normed xturned copied product done stored")
            with nc.Block() as block:
                @block.scalar
                def _(act):
                    act.sem_inc(done, 1)
                    with act.Fori(0, NCH) as i:
                        act.wait_ge(done, i + 1)
                        act.copy(st_[:], acc[:, ds(i * CW, CW)]).then_inc(staged, 1)
                        for k in range(2):
                            root(act, st, var_ready, rooted, i, 2, k)
                        act.wait_ge(xturned, i + 1)
                        act.copy(xT[:], tp[:]).then_inc(copied, 1)

                @block.tensor
                def _(pe):
                    with pe.Fori(0, NCH) as i:
                        pe.wait_ge(staged, i + 1)
                        turn_tiles(pe, ap_, st_).then_inc(turned, 1)
                        pe.wait_ge(normed, i + 1)
                        turn_tiles(pe, tp, r).then_inc(xturned, 1)
                        pe.wait_ge(copied, i + 1)
                        times(pe, hp, xT, W(W_M1X)).then_inc(product, 1)

                @block.vector
                def _(dve):
                    STEPS = 5 + 2 * NORM_STEPS
                    with dve.Fori(0, NCH) as i:
                        own = Chain(dve, chain, STEPS, i)
                        at, r3 = ds(i * CW, CW), tiles3(r[:])
                        dve.wait_ge(turned, i + 1)
                        own.step(V.tensor_tensor(out=r[:], in0=X[:, at], in1=ap_[:], op=ALU.add))
                        norm(dve, own, r[:], sq[:], st, var_ready, rooted, i, 2, 0)
                        own.step(V.tensor_tensor(out=r3, in0=r3, in1=rows(bias[:, B_GAMMA, :], TC), op=ALU.mult))
                        own.step(V.tensor_tensor(out=r3, in0=r3, in1=rows(bias[:, B_BETA, :], TC), op=ALU.add))
                        own.step(V.tensor_tensor(out=r[:], in0=r[:], in1=X[:, at], op=ALU.add))
                        norm(dve, own, r[:], sq[:], st, var_ready, rooted, i, 2, 1)
                        passed(dve, tick)
                        own.step(V.tensor_copy(X[:, at], r[:]))
                        dve.sem_inc(normed, 1)
                        dve.wait_ge(product, i + 1)
                        V.tensor_tensor(out=tiles3(HB[:, at]), in0=tiles3(hp[:]), in1=rows(bias[:, B_M1, :], TC),
                                        op=ALU.add).then_inc(done, 1)
                        assert own.n == STEPS, own.n

                @block.sync
                def _(sp):
                    sp.wait_ge(done, NCH + 1)
                    sp.dma_start(msg_d.rearrange("(t p) f -> p t f", p=P), tiles3(HB[:])).then_inc(stored, 16)
                    sp.wait_ge(stored, 16)

        aggregate("mpnn_edges", msg_d, src_d, attr=True)

        with ExitStack() as ctx:
            ctx.callback(end_stage)
            as_ = sb(ctx, "as4", [P, CW])
            xs = sb(ctx, "xs4", [P, CW])
            xT = sb(ctx, "xT4", [P, CW])
            u = sb(ctx, "u4", [P, CW])
            r = sb(ctx, "r4", [P, CW])
            sq = sb(ctx, "sq4", [P, CW])
            st = sb(ctx, "st4", [P, 2 * TC])
            tp = ps(ctx, "tp4", [P, CW])
            xp = ps(ctx, "xp4", [P, CW])
            mp = ps(ctx, "mp4", [P, CW])
            staged, turned, copied, product, chain, hidden, delta, var_ready, rooted, done, stored = sems(
                "n3", "staged turned copied product chain hidden delta var_ready rooted done stored")
            with nc.Block() as block:
                @block.scalar
                def _(act):
                    act.sem_inc(done, 1)
                    with act.Fori(0, NCH) as i:
                        act.wait_ge(done, i + 1)
                        act.copy(as_[:], acc[:, ds(i * CW, CW)])
                        act.copy(xs[:], X[:, ds(i * CW, CW)]).then_inc(staged, 1)
                        act.wait_ge(turned, i * 2 + 1)
                        act.copy(xT[:], tp[:]).then_inc(copied, 1)
                        act.wait_ge(turned, i * 2 + 2)
                        act.copy(xT[:], tp[:]).then_inc(copied, 1)
                        for k in range(2):
                            root(act, st, var_ready, rooted, i, 2, k)

                @block.tensor
                def _(pe):
                    with pe.Fori(0, NCH) as i:
                        pe.wait_ge(staged, i + 1)
                        turn_tiles(pe, tp, xs).then_inc(turned, 1)
                        times(pe, mp, as_, wcomb[:])
                        pe.wait_ge(copied, i * 2 + 1)
                        times(pe, xp, xT, W(W_U1X)).then_inc(product, 1)
                        pe.wait_ge(hidden, i + 1)
                        turn_tiles(pe, tp, u).then_inc(turned, 1)
                        pe.wait_ge(copied, i * 2 + 2)
                        times(pe, xp, xT, W(W_U2)).then_inc(delta, 1)

                @block.vector
                def _(dve):
                    STEPS = 11 + 2 * NORM_STEPS
                    with dve.Fori(0, NCH) as i:
                        own = Chain(dve, chain, STEPS, i)
                        at, att, r3, u3 = ds(i * CW, CW), ds(i * TC, TC), tiles3(r[:]), tiles3(u[:])
                        dve.wait_ge(product, i + 1)
                        own.step(V.tensor_tensor(out=u3, in0=tiles3(mp[:]), in1=over(cntinv[:, att], D), op=ALU.mult))
                        own.step(V.tensor_tensor(out=u[:], in0=u[:], in1=xp[:], op=ALU.add))
                        own.step(V.tensor_tensor(out=r3, in0=over(has[:, att], D), in1=rows(bias[:, B_V, :], TC), op=ALU.mult))
                        own.step(V.tensor_tensor(out=u[:], in0=u[:], in1=r[:], op=ALU.add))
                        own.step(V.tensor_tensor(out=u3, in0=u3, in1=rows(bias[:, B_U1, :], TC), op=ALU.add))
                        V.tensor_scalar(u[:], u[:], 0.0, None, ALU.max).then_inc(hidden, 1)
                        dve.wait_ge(delta, i + 1)
                        own.step(V.tensor_tensor(out=r[:], in0=X[:, at], in1=xp[:], op=ALU.add))
                        own.step(V.tensor_tensor(out=r3, in0=r3, in1=rows(bias[:, B_U2, :], TC), op=ALU.add))
                        norm(dve, own, r[:], sq[:], st, var_ready, rooted, i, 2, 0)
                        own.step(V.tensor_tensor(out=r3, in0=r3, in1=rows(bias[:, B_LNG, :], TC), op=ALU.mult))
                        own.step(V.tensor_tensor(out=r3, in0=r3, in1=rows(bias[:, B_LNB, :], TC), op=ALU.add))
                        own.step(V.tensor_tensor(out=r[:], in0=r[:], in1=X[:, at], op=ALU.add))
                        norm(dve, own, r[:], sq[:], st, var_ready, rooted, i, 2, 1)
                        passed(dve, tick)
                        own.step(V.tensor_copy(X[:, at], r[:]))
                        dve.sem_inc(done, 1)
                        assert own.n == STEPS, own.n

                @block.sync
                def _(sp):
                    sp.wait_ge(done, NCH + 1)
                    sp.dma_start(out[0:NPAD - P].rearrange("(t p) f -> p t f", p=P), tiles3(X[:, 0:NPAD - P])).then_inc(stored, 16)
                    sp.dma_start(out[NPAD - P:N], X[0:NLAST, NPAD - P:]).then_inc(stored, 16)
                    sp.wait_ge(stored, 32)


_INS = ['x', 'src', 'dst', 'edge_attr_64', 'edge_type_8', 'edge_weight', 'L0_gnn_W', 'L0_gnn_b', 'L1_gnn_node_proj_w',
        'L1_gnn_node_proj_b', 'L1_gnn_edge_W', 'L1_gnn_edge_b', 'L1_gnn_gru_wih', 'L1_gnn_gru_whh', 'L1_gnn_gru_bih',
        'L1_gnn_gru_bhh', 'L1_gnn_out_w', 'L1_gnn_out_b', 'L2_gnn_W', 'L2_gnn_a', 'L2_gnn_ln_gamma', 'L2_gnn_ln_beta',
        'L3_gnn_global_state', 'L3_gnn_Wm1', 'L3_gnn_bm1', 'L3_gnn_Wm2', 'L3_gnn_bm2', 'L3_gnn_Wu1', 'L3_gnn_bu1',
        'L3_gnn_Wu2', 'L3_gnn_bu2', 'L3_gnn_ln_g', 'L3_gnn_ln_b']


def kernel(**inputs):
    import concourse.bacc as _bacc
    import numpy as _np
    from concourse.bass_utils import run_bass_kernel_spmd as _run

    nc = _bacc.Bacc("TRN2", target_bir_lowering=False, num_devices=1)
    arrays, args = {}, []
    for name in _INS:
        a = _np.ascontiguousarray(inputs[name])
        arrays[f"in_{name}"] = a
        args.append(nc.dram_tensor(f"in_{name}", a.shape, mybir.dt.from_np(a.dtype), kind="ExternalInput").ap())
    args.append(nc.dram_tensor("out_0", (N, D), F32, kind="ExternalOutput").ap())
    build(nc, *args)
    r = _run(nc, [arrays], core_ids=[0])
    return r.results[0]["out_0"]
```

```python
from contextlib import ExitStack

import concourse.bass as bass
from concourse import mybir

F32 = mybir.dt.float32
BF16 = mybir.dt.bfloat16
I32 = mybir.dt.int32
U32 = mybir.dt.uint32
ALU = mybir.AluOpType
ACT = mybir.ActivationFunctionType
AX = mybir.AxisListType.X
ds = bass.ds

P = 128
D = 128
N = 6250
E = 200000
NT = -(-N // P)
NPAD = NT * P
NLAST = N - (NT - 1) * P
TC = 7
NCH = NT // TC
CW = TC * P
GC = 14
GE = GC * P
NG = -(-E // GE)
PLAST = (E - (NG - 1) * GE) // GC
CLAST = (E - (NG - 1) * GE) % GC
SL = 4
T = 8
H = 8
HD = 16
ED = 64
ACCW = NPAD + P
FAR = 1000000
KCAP = -(-(NG * NT) // P) * P
KT = KCAP // P
NOBASE = 8000000.0
EPS = 1e-5
ALPHA = 0.2
assert NT == NCH * TC and NG <= P and CLAST > 0

W_PROJ, W_EDGE, W_IH, W_HH, W_OUT, W_HEADS, W_M1X, W_M1E, W_M1G, W_U1X, W_U1A, W_U1G, W_U2 = (
    0, 1, 17, 23, 29, 30, 31, 32, 33, 34, 35, 36, 37)
NW = 40


class Chain:

    def __init__(self, eng, sem, per_turn=0, turn=0):
        self.eng, self.sem, self.n, self.base = eng, sem, 0, turn * per_turn

    def step(self, ins):
        ins.then_inc(self.sem, 1)
        self.n += 1
        self.eng.wait_ge(self.sem, self.base + self.n)


def passed(eng, tick):
    eng.sem_inc(tick, 1)


def over(ap, n):
    return ap.unsqueeze(2).to_broadcast([ap.shape[0], ap.shape[1], n])


def rows(ap, n):
    return ap.unsqueeze(1).to_broadcast([ap.shape[0], n, ap.shape[1]])


def build(nc, x, src, dst, edge_attr_64, edge_type_8, edge_weight, L0_gnn_W, L0_gnn_b, L1_gnn_node_proj_w,
          L1_gnn_node_proj_b, L1_gnn_edge_W, L1_gnn_edge_b, L1_gnn_gru_wih, L1_gnn_gru_whh, L1_gnn_gru_bih,
          L1_gnn_gru_bhh, L1_gnn_out_w, L1_gnn_out_b, L2_gnn_W, L2_gnn_a, L2_gnn_ln_gamma, L2_gnn_ln_beta,
          L3_gnn_global_state, L3_gnn_Wm1, L3_gnn_bm1, L3_gnn_Wm2, L3_gnn_bm2, L3_gnn_Wu1, L3_gnn_bu1,
          L3_gnn_Wu2, L3_gnn_bu2, L3_gnn_ln_g, L3_gnn_ln_b, out):
    V = nc.vector

    def dram(name, shape, dt=F32):
        return nc.dram_tensor(name, shape, dt, kind="Internal").ap()

    items_d = dram("items_d", [KCAP, 4], I32)
    dst_d = dram("dst_d", [NG, GE], I32)
    src_d = dram("src_d", [NG, GE], I32)
    row_d = dram("row_d", [NG, GE], I32)
    gcn_d = dram("gcn_d", [NPAD, D])
    trans_d = [dram(f"trans_d{l}", [NPAD, T * D]) for l in range(2)]
    att_d = dram("att_d", [NPAD, 2 * H])
    sj_d = dram("sj_d", [ACCW, 6 * H], BF16)
    heads_d = dram("heads_d", [NPAD, D])
    msg_d = dram("msg_d", [NPAD, D])

    def sb(ctx, name, shape, dt=F32):
        return ctx.enter_context(nc.sbuf_tensor(name, shape, dt))

    def ps(ctx, name, shape):
        return ctx.enter_context(nc.psum_tensor(name, shape, F32))

    in_stage = []

    def sems(prefix, names):
        made = [nc.alloc_semaphore(name=f"{prefix}_{n}") for n in names.split()]
        in_stage.extend(made)
        return made

    def end_stage():
        nc.clear_and_free_semaphores(list(in_stage))
        in_stage.clear()
        nc.all_engine_barrier()

    with ExitStack() as whole:
        tick = whole.enter_context(nc.semaphore("tick"))
        X = sb(whole, "X", [P, NPAD])
        HB = sb(whole, "HB", [P, NPAD])
        acc = sb(whole, "acc", [P, ACCW])
        dstI = sb(whole, "dstI", [P, NG * GC], I32)
        iota_row = sb(whole, "iota_row", [P, P])
        iota_col = sb(whole, "iota_col", [P, 1])
        iota_colI = sb(whole, "iota_colI", [P, 1], I32)
        ident = sb(whole, "ident", [P, P])
        ones = sb(whole, "ones", [P, P])
        wt_late = sb(whole, "wt_late", [P, (NW - W_HEADS) * P])
        w0 = sb(whole, "w0", [P, D])
        wall = sb(whole, "wall", [P, D])
        wa = sb(whole, "wa", [P, 2 * H])
        wcomb = sb(whole, "wcomb", [P, D])
        bias = sb(whole, "bias", [P, 11, D])
        bcol = sb(whole, "bcol", [P, 32])
        deg = sb(whole, "deg", [P, 2, NT])
        dinv = sb(whole, "dinv", [P, NT])
        cntinv = sb(whole, "cntinv", [P, NT])
        has = sb(whole, "has", [P, NT])
        turns_to = sb(whole, "turns_to", [1, NCH + 1], I32)
        S = sb(whole, "S", [P, NT, 2 * H])
        den = sb(whole, "den", [P, NT, H])

        B_L0, B_OUT, B_GAMMA, B_BETA, B_M1, B_U1, B_U2, B_LNG, B_LNB, B_M2, B_V = range(11)
        C_PROJ, C_IH, C_HH, C_RZ = 0, 1, 7, 13

        early = whole.enter_context(ExitStack())
        wgt = sb(early, "wgt", [P, NG * GC])
        wt_early = sb(early, "wt_early", [P, W_HEADS * P])

        def W(i, n=1):
            return wt_early[:, i * P:(i + n) * P] if i < W_HEADS else wt_late[:, (i - W_HEADS) * P:(i - W_HEADS + n) * P]

        with ExitStack() as ctx:
            ctx.callback(end_stage)
            ws = sb(ctx, "ws", [P, NW * P])
            wm2 = sb(ctx, "wm2", [P, D])
            srcI = sb(ctx, "srcI", [P, NG * GC], I32)
            typI = sb(ctx, "typI", [P, NG * GC], I32)
            rowI = sb(ctx, "rowI", [P, NG * GC], I32)
            acol = sb(ctx, "acol", [P, 2])
            a_blk = sb(ctx, "a_blk", [P, 2 * H])
            hmask = sb(ctx, "hmask", [P, H])
            h8 = sb(ctx, "h8", [P, H])
            gcol = sb(ctx, "gcol", [ED, 1])
            bm2c = sb(ctx, "bm2c", [P, 1])
            vecs = sb(ctx, "vecs", [P, 2, P])
            wps = ps(ctx, "wps", [P, 2, 512])
            sps = ps(ctx, "sps", [P, 512])
            fill, x_in, edges_in, w_in, small_in, iotas, wtp, wtc, mini, minis, made, chain, rowed = sems(
                "setup", "fill x_in edges_in w_in small_in iotas wtp wtc mini minis made chain rowed")
            with nc.Block() as block:
                w_loads = []

                def wload(slot, ap, n=1, view=None):
                    w_loads.append((slot, ap, n))

                wload(W_PROJ, L1_gnn_node_proj_w)
                for l in range(2):
                    w_loads.append((W_EDGE + 8 * l, L1_gnn_edge_W[l].rearrange("t d h -> d t h"), 8))
                    w_loads.append((W_IH + 3 * l, L1_gnn_gru_wih[l].rearrange("(k d) h -> d k h", k=3), 3))
                    w_loads.append((W_HH + 3 * l, L1_gnn_gru_whh[l].rearrange("(k d) h -> d k h", k=3), 3))
                wload(W_OUT, L1_gnn_out_w)
                wload(W_M1X, L3_gnn_Wm1[:, 0:D])
                wload(W_U1X, L3_gnn_Wu1[:, 0:D])
                wload(W_U1A, L3_gnn_Wu1[:, D:2 * D])
                wload(W_U2, L3_gnn_Wu2)
                half_loads = [
                    (W_M1E * P, L3_gnn_Wm1[:, D:D + ED]), (W_M1E * P + ED, L3_gnn_Wm1[:, D:D + ED]),
                    (W_M1G * P, L3_gnn_Wm1[:, D + ED:D + 2 * ED]), (W_U1G * P, L3_gnn_Wu1[:, 2 * D:2 * D + ED])]
                bias_loads = [L0_gnn_b, L1_gnn_out_b, L2_gnn_ln_gamma, L2_gnn_ln_beta, L3_gnn_bm1, L3_gnn_bu1,
                              L3_gnn_bu2, L3_gnn_ln_g, L3_gnn_ln_b, L3_gnn_bm2]
                col_loads = [(C_PROJ, 1, L1_gnn_node_proj_b.rearrange("(p a) -> p a", a=1))]
                for l in range(2):
                    col_loads.append((C_IH + 3 * l, 3, L1_gnn_gru_bih[l].rearrange("(k p) -> p k", k=3)))
                    col_loads.append((C_HH + 3 * l, 3, L1_gnn_gru_bhh[l].rearrange("(k p) -> p k", k=3)))
                NWL = len(w_loads) + len(half_loads) + 1
                NSL = 4 + len(bias_loads) + len(col_loads)

                @block.sync
                def _(sp):
                    sp.wait_ge(fill, 6)
                    body = E // GE * GE
                    for tile, array in ((dstI, dst), (srcI, src), (typI, edge_type_8), (wgt, edge_weight)):
                        sp.dma_start(tile[:, 0:(NG - 1) * GC].rearrange("p (g c) -> p g c", c=GC),
                                     array[0:body].rearrange("(g p c) -> p g c", p=P, c=GC)).then_inc(edges_in, 16)
                        sp.dma_start(tile[0:PLAST, (NG - 1) * GC:],
                                     array[body:body + PLAST * GC].rearrange("(p c) -> p c", c=GC)).then_inc(edges_in, 16)
                        sp.dma_start(tile[PLAST:PLAST + 1, (NG - 1) * GC:(NG - 1) * GC + CLAST],
                                     array[body + PLAST * GC:E].unsqueeze(0)).then_inc(edges_in, 16)
                    sp.dma_start(X[:, 0:NPAD - P].rearrange("p (t f) -> p t f", f=D),
                                 x[0:NPAD - P, :].rearrange("(t p) f -> p t f", p=P)).then_inc(x_in, 16)
                    sp.dma_start(X[0:NLAST, NPAD - P:], x[NPAD - P:N, :]).then_inc(x_in, 16)
                    for slot, ap, n in w_loads:
                        view = ws[:, slot * P:(slot + n) * P]
                        sp.dma_start(view if n == 1 else view.rearrange("p (n h) -> p n h", n=n), ap).then_inc(w_in, 16)
                    for col, ap in half_loads:
                        sp.dma_start(ws[:, col:col + ED], ap).then_inc(w_in, 16)
                    sp.dma_start(wm2[:], L3_gnn_Wm2).then_inc(w_in, 16)
                    sp.dma_start(w0[:], L0_gnn_W).then_inc(small_in, 16)
                    sp.dma_start(wall[:].rearrange("i (h j) -> i h j", h=H),
                                 L2_gnn_W.rearrange("h i j -> i h j")).then_inc(small_in, 16)
                    for b, ap in enumerate(bias_loads):
                        sp.dma_start(bias[:, b, :], ap.unsqueeze(0).to_broadcast([P, D])).then_inc(small_in, 16)
                    sp.dma_start(gcol[:], L3_gnn_global_state.rearrange("(p a) -> p a", a=1)).then_inc(small_in, 16)
                    sp.dma_start(bm2c[:], L3_gnn_bm2.rearrange("(p a) -> p a", a=1)).then_inc(small_in, 16)
                    with nc.allow_non_contiguous_dma("a few columns of biases"):
                        for col, n, ap in col_loads:
                            sp.dma_start(bcol[:, col:col + n], ap).then_inc(small_in, 16)
                        for t in range(2):
                            for h in range(H):
                                sp.dma_start(acol[h * HD:(h + 1) * HD, t:t + 1],
                                             L2_gnn_a[h, t * HD:(t + 1) * HD, :]).then_inc(small_in, 16)
                    sp.wait_ge(edges_in, 12 * 16)
                    for table, tile in ((dst_d, dstI), (src_d, srcI), (row_d, rowI)):
                        if tile is rowI:
                            sp.wait_ge(rowed, 1)
                        sp.dma_start(table.rearrange("g (p c) -> p g c", c=GC),
                                     tile[:].rearrange("p (g c) -> p g c", c=GC)).then_inc(edges_in, 16)
                    sp.wait_ge(edges_in, 15 * 16)
                    sp.wait_ge(x_in, 32)

                @block.gpsimd
                def _(pool):
                    pool.iota(iota_row[:], [[1, P]], base=0, channel_multiplier=0,
                              allow_small_or_imprecise_dtypes=True).then_inc(iotas, 1)
                    pool.iota(iota_colI[:], [[0, 1]], base=0, channel_multiplier=1).then_inc(iotas, 1)
                    pool.iota(h8[:], [[-HD, H]], base=0, channel_multiplier=1,
                              allow_small_or_imprecise_dtypes=True).then_inc(iotas, 1)
                    pool.memset(X[:, NPAD - P:], 0.0).then_inc(fill, 1)
                    pool.memset(dstI[:, (NG - 1) * GC:], FAR).then_inc(fill, 1)
                    pool.memset(srcI[:, (NG - 1) * GC:], 0).then_inc(fill, 1)
                    pool.memset(typI[:, (NG - 1) * GC:], 0).then_inc(fill, 1)
                    pool.memset(wgt[:, (NG - 1) * GC:], 0.0).then_inc(fill, 1)
                    pool.memset(ws[:], 0.0).then_inc(fill, 1)

                @block.tensor
                def _(pe):
                    pe.wait_ge(w_in, 16 * NWL)
                    pe.wait_ge(made, 1)
                    pe.wait_ge(made, 2)
                    for q in range(NW // 4):
                        if q >= 2:
                            pe.wait_ge(wtc, q - 1)
                        for j in range(4):
                            mm = pe.transpose(wps[:, q % 2, j * P:(j + 1) * P], ws[:, (4 * q + j) * P:(4 * q + j + 1) * P],
                                              ident[:])
                        mm.then_inc(wtp, 1)
                    pe.wait_ge(wtc, NW // 4)
                    pe.wait_ge(made, 3)
                    pe.matmul(sps[:, 0:16], W(W_HEADS), a_blk[:], start=True, stop=True)
                    pe.matmul(sps[:, 128:256], vecs[0:ED, 0, :], W(W_M1G)[0:ED, :], start=True, stop=True)
                    pe.matmul(sps[:, 256:384], vecs[0:ED, 0, :], W(W_U1G)[0:ED, :], start=True, stop=True)
                    pe.matmul(sps[:, 384:512], vecs[:, 1, :], W(W_U1A), start=True, stop=True).then_inc(mini, 1)
                    pe.wait_ge(minis, 1)
                    pe.matmul(sps[:, 0:128], wm2[:], W(W_U1A), start=True, stop=True).then_inc(mini, 1)

                @block.scalar
                def _(act):
                    for q in range(NW // 4):
                        act.wait_ge(wtp, q + 1)
                        for j in range(0, 4, 2):
                            cp = act.copy(W(4 * q + j, 2), wps[:, q % 2, j * P:(j + 2) * P])
                        cp.then_inc(wtc, 1)

                @block.vector
                def _(dve):
                    own = Chain(dve, chain)
                    dve.wait_ge(iotas, 3)
                    own.step(V.tensor_copy(iota_col[:], iota_colI[:]))
                    own.step(V.memset(ones[:], 1.0))
                    V.tensor_tensor(out=ident[:], in0=iota_row[:], in1=iota_col[:].to_broadcast([P, P]),
                                    op=ALU.is_equal).then_inc(made, 1)
                    dve.wait_ge(small_in, 16 * (2 + len(bias_loads) + 2 + len(col_loads) + 2 * H))
                    dve.wait_ge(w_in, 16 * NWL)
                    V.tensor_copy(ws[:, W_HEADS * P:(W_HEADS + 1) * P], wall[:]).then_inc(made, 1)
                    own.step(V.tensor_scalar(hmask[:], h8[:], 0.0, None, ALU.is_ge))
                    own.step(V.tensor_scalar(h8[:], h8[:], float(HD), None, ALU.is_lt))
                    own.step(V.tensor_tensor(out=hmask[:], in0=hmask[:], in1=h8[:], op=ALU.mult))
                    for t in range(2):
                        own.step(V.tensor_scalar(a_blk[:, t * H:(t + 1) * H], hmask[:], acol[:, t:t + 1], None, ALU.mult))
                    own.step(V.tensor_scalar(vecs[0:ED, 0, :], ones[0:ED, :], gcol[:, 0:1], None, ALU.mult))
                    own.step(V.tensor_scalar(vecs[:, 1, :], ones[:], bm2c[:, 0:1], None, ALU.mult))
                    V.tensor_tensor(out=bcol[:, C_RZ:C_RZ + 6], in0=bcol[:, C_IH:C_IH + 6], in1=bcol[:, C_HH:C_HH + 6],
                                    op=ALU.add).then_inc(made, 1)
                    dve.wait_ge(edges_in, 12 * 16)
                    V.scalar_tensor_tensor(out=rowI[:], in0=srcI[:], scalar=float(T), in1=typI[:],
                                           op0=ALU.mult, op1=ALU.add).then_inc(rowed, 1)
                    dve.wait_ge(mini, 1)
                    own.step(V.tensor_copy(wa[:], sps[:, 0:16]))
                    own.step(V.tensor_tensor(out=bias[:, B_M1, :], in0=bias[:, B_M1, :], in1=sps[:, 128:256], op=ALU.add))
                    own.step(V.tensor_tensor(out=bias[:, B_U1, :], in0=bias[:, B_U1, :], in1=sps[:, 256:384], op=ALU.add))
                    own.step(V.tensor_copy(bias[:, B_V, :], sps[:, 384:512]))
                    dve.sem_inc(minis, 1)
                    dve.wait_ge(mini, 2)
                    own.step(V.tensor_copy(wcomb[:], sps[:, 0:128]))

        with ExitStack() as ctx:
            ctx.callback(end_stage)
            dstF = sb(ctx, "dstF", [P, NG * GC])
            near = sb(ctx, "near", [P, NG * GC])
            mm_ = sb(ctx, "mm_", [P, 2, P])
            gm = sb(ctx, "gm", [P, 8])
            nwI = sb(ctx, "nwI", [P, 1], I32)
            upto = sb(ctx, "upto", [P, P])
            kk = sb(ctx, "kk", [P, KCAP])
            sel = sb(ctx, "sel", [P, KCAP])
            vals = sb(ctx, "vals", [P, 4])
            kcol = sb(ctx, "kcol", [P, KT])
            it = sb(ctx, "it", [P, KT, 4])
            itI = sb(ctx, "itI", [P, KT, 4], I32)
            kf = sb(ctx, "kf", [P, KCAP // SL + 1])
            before = sb(ctx, "before", [P, 3, NCH, KT])
            last = sb(ctx, "last", [P, P])
            tt = sb(ctx, "tt", [P, 2])
            tps = ps(ctx, "tps", [P, 2, P])
            cps = ps(ctx, "cps", [P, 8])
            lps = ps(ctx, "lps", [P, P])
            ips = ps(ctx, "ips", [P, KT, 4])
            iotas, mins, turned, nwin, cums, sels, itp, table, stored, chain, lastm, lastt, tcol, trow = sems(
                "items", "iotas mins turned nwin cums sels itp table stored chain lastm lastt tcol trow")
            with nc.Block() as block:
                @block.gpsimd
                def _(pool):
                    pool.iota(kk[:], [[1, KCAP]], base=0, channel_multiplier=0,
                              allow_small_or_imprecise_dtypes=True).then_inc(iotas, 1)
                    pool.iota(kcol[:], [[P, KT]], base=0, channel_multiplier=1,
                              allow_small_or_imprecise_dtypes=True).then_inc(iotas, 1)
                    pool.iota(kf[:], [[SL, KCAP // SL + 1]], base=0, channel_multiplier=0,
                              allow_small_or_imprecise_dtypes=True).then_inc(iotas, 1)

                @block.vector
                def _(dve):
                    own = Chain(dve, chain)
                    own.step(V.tensor_copy(dstF[:], dstI[:]))
                    own.step(V.memset(mm_[:], 0.0))
                    own.step(V.tensor_reduce(mm_[:, 0, 0:NG], dstF[:].rearrange("p (g c) -> p g c", c=GC), AX, ALU.min))
                    own.step(V.tensor_scalar(near[:], dstF[:], float(N), None, ALU.is_lt))
                    own.step(V.tensor_tensor(out=near[:], in0=near[:], in1=dstF[:], op=ALU.mult))
                    V.tensor_reduce(mm_[:, 1, 0:NG], near[:].rearrange("p (g c) -> p g c", c=GC), AX,
                                    ALU.max).then_inc(mins, 1)
                    dve.wait_ge(turned, 1)
                    own.step(V.tensor_reduce(gm[0:NG, 0:1], tps[0:NG, 0, :], AX, ALU.min))
                    own.step(V.tensor_reduce(gm[0:NG, 1:2], tps[0:NG, 1, :], AX, ALU.max))
                    own.step(V.tensor_tensor(out=nwI[0:NG], in0=gm[0:NG, 1:2], in1=gm[0:NG, 0:1], op=ALU.subtract))
                    own.step(V.tensor_single_scalar(nwI[0:NG], nwI[0:NG], 7, op=ALU.arith_shift_right))
                    own.step(V.tensor_scalar(gm[0:NG, 2:3], nwI[0:NG], 1.0, None, ALU.add))
                    own.step(V.tensor_tensor(out=upto[:], in0=iota_row[:], in1=iota_col[:].to_broadcast([P, P]), op=ALU.is_ge))
                    dve.sem_inc(nwin, 1)
                    dve.wait_ge(cums, 1)
                    own.step(V.tensor_copy(gm[0:NG, 3:4], cps[0:NG, 0:1]))
                    own.step(V.tensor_tensor(out=gm[0:NG, 4:5], in0=gm[0:NG, 3:4], in1=gm[0:NG, 2:3], op=ALU.subtract))
                    own.step(V.scalar_tensor_tensor(out=vals[0:NG, 0:1], in0=gm[0:NG, 4:5], scalar=-float(P),
                                                    in1=gm[0:NG, 0:1], op0=ALU.mult, op1=ALU.add))
                    own.step(V.tensor_copy(vals[0:NG, 1:2], iota_col[0:NG]))
                    own.step(V.memset(vals[0:NG, 2:4], 1.0))
                    dve.wait_ge(iotas, 3)
                    own.step(V.tensor_scalar(sel[0:NG], kk[0:NG], gm[0:NG, 3:4], None, ALU.is_lt))
                    V.scalar_tensor_tensor(out=sel[0:NG], in0=kk[0:NG], scalar=gm[0:NG, 4:5], in1=sel[0:NG],
                                           op0=ALU.is_ge, op1=ALU.mult).then_inc(sels, 1)
                    dve.wait_ge(itp, 1)
                    own.step(V.tensor_copy(it[:], ips[:]))
                    own.step(V.scalar_tensor_tensor(out=it[:, :, 0], in0=kcol[:], scalar=float(P), in1=it[:, :, 0],
                                                    op0=ALU.mult, op1=ALU.add))
                    own.step(V.tensor_scalar(it[:, :, 3], it[:, :, 2], -NOBASE, NOBASE, ALU.mult, ALU.add))
                    own.step(V.tensor_tensor(out=itI[:, :, 0], in0=it[:, :, 0], in1=it[:, :, 3], op=ALU.add))
                    own.step(V.tensor_tensor(out=itI[:, :, 1], in0=it[:, :, 0], in1=it[:, :, 2], op=ALU.mult))
                    own.step(V.tensor_copy(itI[:, :, 2:4], it[:, :, 1:3]))
                    dve.sem_inc(table, 1)
                    own.step(V.tensor_scalar(before[:, 1, 0, :], kcol[:], 1.0, None, ALU.add))
                    own.step(V.tensor_tensor(out=before[:, 1, 0, :], in0=before[:, 1, 0, :], in1=it[:, :, 2], op=ALU.mult))
                    own.step(V.memset(last[:], 0.0))
                    for c in range(NCH):
                        own.step(V.scalar_tensor_tensor(out=before[:, 0, c, :], in0=it[:, :, 0], scalar=float(CW * (c + 1)),
                                                        in1=before[:, 1, 0, :], op0=ALU.is_lt, op1=ALU.mult))
                    own.step(V.tensor_reduce(last[:, 0:NCH], before[:, 0], AX, ALU.max))
                    dve.sem_inc(lastm, 1)
                    dve.wait_ge(lastt, 1)
                    own.step(V.tensor_reduce(tt[0:NCH, 0:1], lps[0:NCH, :], AX, ALU.max))
                    own.step(V.tensor_scalar(kf[0:NCH], kf[0:NCH], tt[0:NCH, 0:1], None, ALU.is_lt))
                    own.step(V.tensor_reduce(tt[0:NCH, 1:2], kf[0:NCH], AX, ALU.add))
                    dve.sem_inc(tcol, 1)
                    dve.wait_ge(trow, 1)
                    own.step(V.memset(turns_to[:], 0))
                    own.step(V.tensor_copy(turns_to[:, 1:NCH + 1], lps[0:1, 0:NCH]))

                @block.tensor
                def _(pe):
                    pe.wait_ge(mins, 1)
                    pe.transpose(tps[:, 0, :], mm_[:, 0, :], ident[:])
                    pe.transpose(tps[:, 1, :], mm_[:, 1, :], ident[:]).then_inc(turned, 1)
                    pe.wait_ge(nwin, 1)
                    pe.matmul(cps[0:NG, 0:1], upto[0:NG, 0:NG], gm[0:NG, 2:3], start=True, stop=True).then_inc(cums, 1)
                    pe.wait_ge(sels, 1)
                    for k in range(KT):
                        mm = pe.matmul(ips[:, k, :], sel[0:NG, k * P:(k + 1) * P], vals[0:NG, :], start=True, stop=True)
                    mm.then_inc(itp, 1)
                    pe.wait_ge(lastm, 1)
                    pe.transpose(lps[:], last[:], ident[:]).then_inc(lastt, 1)
                    pe.wait_ge(tcol, 1)
                    pe.transpose(lps[0:1, 0:NCH], tt[0:NCH, 1:2], ident[0:NCH, 0:NCH]).then_inc(trow, 1)

                @block.sync
                def _(sp):
                    sp.wait_ge(table, 1)
                    sp.dma_start(items_d.rearrange("(k p) c -> p k c", p=P), itI[:]).then_inc(stored, 16)
                    sp.wait_ge(stored, 16)

        with ExitStack() as ctx:
            ctx.callback(end_stage)
            loI = sb(ctx, "loI", [P, NG * GC], I32)
            hiI = sb(ctx, "hiI", [P, NG * GC], I32)
            ohlo = sb(ctx, "ohlo", [P, 2, GC, P])
            ohhi = sb(ctx, "ohhi", [P, 2, GC, 2, NT])
            zero = sb(ctx, "zero", [P, P])
            dps = ps(ctx, "dps", [P, 2, NT])
            made, used, chain, zeroed, summed, dsq, rooted = sems("deg", "made used chain zeroed summed dsq rooted")
            with nc.Block() as block:
                @block.vector
                def _(dve):
                    own = Chain(dve, chain)
                    own.step(V.tensor_single_scalar(loI[:], dstI[:], P - 1, op=ALU.bitwise_and))
                    own.step(V.tensor_single_scalar(hiI[:], dstI[:], 7, op=ALU.arith_shift_right))
                    V.memset(zero[:], 0.0).then_inc(zeroed, 1)
                    with dve.Fori(0, NG // 2) as i:
                        turn = Chain(dve, chain, 2, i)
                        turn.base = i * 2 + 2
                        for s in range(2):
                            at = ds((i * 2 + s) * GC, GC)
                            dve.wait_ge(used, i * 2 + s + 1)
                            V.tensor_tensor(out=ohlo[:, s], in0=over(loI[:, at], P), in1=rows(iota_row[:], GC),
                                            op=ALU.is_equal)
                            turn.step(V.tensor_tensor(out=ohhi[:, s, :, 1, :], in0=over(hiI[:, at], NT),
                                                      in1=rows(iota_row[:, 0:NT], GC), op=ALU.is_equal))
                            V.tensor_tensor(out=ohhi[:, s, :, 0, :], in0=ohhi[:, s, :, 1, :], in1=over(wgt[:, at], NT),
                                            op=ALU.mult).then_inc(made, 1)
                    n = NG // 2 * 2 + 2
                    own.base, own.n = n, 0
                    dve.wait_ge(summed, 1)
                    own.step(V.tensor_scalar(deg[:, 0, :], dps[:, 0, :], 1.0, None, ALU.add))
                    own.step(V.tensor_copy(deg[:, 1, :], dps[:, 1, :]))
                    own.step(V.tensor_scalar(dinv[:], deg[:, 0, :], 1e-30, None, ALU.max))
                    own.step(V.reciprocal(dinv[:], dinv[:]))
                    dve.sem_inc(dsq, 1)
                    dve.wait_ge(rooted, 1)
                    own.step(V.scalar_tensor_tensor(out=dinv[:], in0=deg[:, 0, :], scalar=0.0, in1=dinv[:],
                                                    op0=ALU.is_gt, op1=ALU.mult))
                    own.step(V.tensor_scalar(cntinv[:], deg[:, 1, :], 1.0, None, ALU.max))
                    own.step(V.reciprocal(cntinv[:], cntinv[:]))
                    own.step(V.tensor_scalar(has[:], deg[:, 1, :], 0.0, None, ALU.is_gt))

                @block.scalar
                def _(act):
                    act.wait_ge(dsq, 1)
                    act.activation(dinv[:], dinv[:], ACT.Sqrt).then_inc(rooted, 1)

                @block.tensor
                def _(pe):
                    pe.wait_ge(zeroed, 1)
                    pe.matmul(dps[:], zero[:], zero[:, 0:2 * NT], start=True, stop=False,
                              skip_group_check=True).then_inc(used, 2)
                    with pe.Fori(0, NG // 2) as i:
                        for s in range(2):
                            pe.wait_ge(made, i * 2 + s + 1)
                            for c in range(GC):
                                mm = pe.matmul(dps[:], ohlo[:, s, c, :], ohhi[:, s, c], start=False, stop=False,
                                               skip_group_check=True)
                            mm.then_inc(used, 1)
                    pe.matmul(dps[:], zero[:], zero[:, 0:2 * NT], start=False, stop=True,
                              skip_group_check=True).then_inc(summed, 1)

        def turn_tiles(pe, out_ps, in_sb):
            for t in range(TC):
                mm = pe.transpose(out_ps[:, t * P:(t + 1) * P], in_sb[:, t * P:(t + 1) * P], ident[:])
            return mm

        def times(pe, out_ps, tiles_sb, w, width=D):
            for t in range(TC):
                mm = pe.matmul(out_ps[:, t * width:(t + 1) * width], tiles_sb[:, t * P:(t + 1) * P], w, start=True, stop=True)
            return mm

        def norm(dve, own, r, sq, st, var_ready, rooted, turn, n, k):
            r3, q3 = r.rearrange("p (t f) -> p t f", f=D), sq.rearrange("p (t f) -> p t f", f=D)
            own.step(V.tensor_reduce(st[:, 0:TC], r3, AX, ALU.add))
            own.step(V.tensor_scalar(st[:, 0:TC], st[:, 0:TC], 1.0 / D, None, ALU.mult))
            own.step(V.tensor_tensor(out=r3, in0=r3, in1=over(st[:, 0:TC], D), op=ALU.subtract))
            own.step(V.tensor_tensor(out=q3, in0=r3, in1=r3, op=ALU.mult))
            own.step(V.tensor_reduce(st[:, TC:2 * TC], q3, AX, ALU.add))
            V.tensor_scalar(st[:, TC:2 * TC], st[:, TC:2 * TC], 1.0 / D, EPS, ALU.mult, ALU.add).then_inc(var_ready, 1)
            dve.wait_ge(rooted, turn * n + (k + 1))
            own.step(V.reciprocal(st[:, TC:2 * TC], st[:, TC:2 * TC]))
            own.step(V.tensor_tensor(out=r3, in0=r3, in1=over(st[:, TC:2 * TC], D), op=ALU.mult))

        NORM_STEPS = 7

        def root(act, st, var_ready, rooted, turn, n, k):
            act.wait_ge(var_ready, turn * n + (k + 1))
            act.activation(st[:, TC:2 * TC], st[:, TC:2 * TC], ACT.Sqrt).then_inc(rooted, 1)

        def tiles3(ap):
            return ap.rearrange("p (t f) -> p t f", f=D)

        with ExitStack() as ctx:
            ctx.callback(end_stage)
            xs = sb(ctx, "xs", [P, CW])
            xT = sb(ctx, "xT", [P, CW])
            tp = ps(ctx, "tp", [P, CW])
            hp = ps(ctx, "hp", [P, CW])
            staged, turned, copied, product, scaled, stored = sems("gcn", "staged turned copied product scaled stored")
            with nc.Block() as block:
                @block.scalar
                def _(act):
                    act.sem_inc(scaled, 1)
                    with act.Fori(0, NCH) as i:
                        act.wait_ge(scaled, i + 1)
                        act.copy(xs[:], X[:, ds(i * CW, CW)]).then_inc(staged, 1)
                        act.wait_ge(turned, i + 1)
                        act.copy(xT[:], tp[:]).then_inc(copied, 1)

                @block.tensor
                def _(pe):
                    with pe.Fori(0, NCH) as i:
                        pe.wait_ge(staged, i + 1)
                        turn_tiles(pe, tp, xs).then_inc(turned, 1)
                        pe.wait_ge(copied, i + 1)
                        times(pe, hp, xT, w0[:]).then_inc(product, 1)

                @block.vector
                def _(dve):
                    with dve.Fori(0, NCH) as i:
                        dve.wait_ge(product, i + 1)
                        V.tensor_tensor(out=tiles3(HB[:, ds(i * CW, CW)]), in0=tiles3(hp[:]),
                                        in1=over(dinv[:, ds(i * TC, TC)], D), op=ALU.mult).then_inc(scaled, 1)

                @block.sync
                def _(sp):
                    sp.wait_ge(scaled, NCH + 1)
                    sp.dma_start(gcn_d.rearrange("(t p) f -> p t f", p=P), tiles3(HB[:])).then_inc(stored, 16)
                    sp.wait_ge(stored, 16)

        def turns(eng, c, body):
            t0 = eng.value_load(turns_to[0:1, ds(c, 1)], min_val=0, max_val=KCAP // SL)
            t1 = eng.value_load(turns_to[0:1, ds(c + 1, 1)], min_val=0, max_val=KCAP // SL)
            with eng.If(t0 < t1):
                with eng.Fori(t0, t1) as i:
                    body(i)

        def aggregate(name, table, index, stage, weighted=False, ex=None, attr=False):
            with ExitStack() as ctx:
                ctx.callback(end_stage)
                G = sb(ctx, f"{name}_G", [P, SL, GC, D])
                OH = sb(ctx, f"{name}_OH", [P, 2, GC, P])
                idx = sb(ctx, f"{name}_idx", [P, SL, GC], I32)
                itm = sb(ctx, f"{name}_itm", [P, SL, 4], I32)
                PS = ps(ctx, f"{name}_PS", [P, 8, 512])
                wp = [PS[:, 6, 0:P], PS[:, 7, 0:P]]
                OHf = OH[:].rearrange("p a c n -> p (a c n)")
                buf = [OHf[:, k * CW:(k + 1) * CW] for k in range(4)]
                st = sb(ctx, f"{name}_st", [P, 2 * TC])
                gathered = sems(name, " ".join(f"gathered{s}" for s in range(SL)))
                idx_ready = sems(name, " ".join(f"idx_ready{s}" for s in range(SL)))
                item_ready, added, product, oh_ready, chain, rows_ready, acc_ready, done = sems(
                    name, "item_ready added product oh_ready chain rows_ready acc_ready done")
                if attr:
                    at_ = sb(ctx, f"{name}_at", [P, SL, GC, ED])
                    atT = sb(ctx, f"{name}_atT", [P, GC // 2, P])
                    tp = PS[:, 0:2].rearrange("p a n -> p (a n)")[:, 0:GC // 2 * P].rearrange("p (q n) -> p q n", n=P)
                    ep = [PS[:, 2 + 2 * a:4 + 2 * a].rearrange("p a n -> p (a n)")[:, 0:GC // 2 * P].rearrange(
                        "p (q n) -> p q n", n=P) for a in range(2)]
                    attr_in = sems(name, " ".join(f"attr_in{s}" for s in range(SL)))
                    turned, copied, ep_ready, summed = sems(name, "at_turned at_copied ep_ready summed")
                    full = (NG - 1) * GE
                    at_rows = edge_attr_64[0:full, :].rearrange("(g p c) f -> g p (c f)", p=P, c=GC)
                    at_last = edge_attr_64[full:full + PLAST * GC, :].rearrange("(p c) f -> p (c f)", c=GC)
                    at_rest = edge_attr_64[full + PLAST * GC:E, :].rearrange("(p c) f -> p (c f)", c=CLAST)
                run = stage(ctx, name, PS, buf, st, acc_ready, done)
                with nc.Block() as block:
                    @block.sync
                    def _(sp):
                        n = sp.value_load(turns_to[0:1, NCH:NCH + 1], min_val=1, max_val=KCAP // SL)
                        with sp.Fori(0, n) as i:
                            for s in range(SL):
                                k = i * SL + s
                                sp.wait_ge(added, k + 1)
                                sp.dma_start(itm[:, s, :], items_d[ds(k, 1), :].to_broadcast([P, 4])
                                             ).then_inc(item_ready, 16)
                                sp.wait_ge(item_ready, k * 16 + 16)
                                passed(sp, tick)
                                g = sp.value_load(itm[0:1, s, 2:3], min_val=0, max_val=NG - 1)
                                sp.dma_start(idx[:, s, :], index[ds(g, 1), :].rearrange("a (p c) -> (a p) c", c=GC)
                                             ).then_inc(idx_ready[s], 16)
                                if attr:
                                    with sp.If(g < NG - 1):
                                        g = sp.value_load(itm[0:1, s, 2:3], min_val=0, max_val=NG - 2)
                                        sp.dma_start(at_[:, s].rearrange("p c f -> p (c f)"),
                                                     at_rows[ds(g, 1)].rearrange("a p f -> (a p) f")).then_inc(attr_in[s], 32)
                                    with sp.Else():
                                        at = at_[:, s].rearrange("p c f -> p (c f)")
                                        sp.dma_start(at[0:PLAST], at_last).then_inc(attr_in[s], 16)
                                        sp.dma_start(at[PLAST:PLAST + 1, 0:CLAST * ED], at_rest).then_inc(attr_in[s], 16)
                        run.sync(sp)

                    @block.scalar
                    def _(act):
                        def items(i):
                            def attr_copy(s):
                                act.wait_ge(turned, i * SL + s + 1)
                                act.copy(atT[:], tp).then_inc(copied, 1)

                            attr_copy(0)
                            attr_copy(1)
                            for s in range(SL):
                                act.wait_ge(summed, i * SL + s + 1)
                                act.activation(G[:, s], G[:, s], ACT.Relu).then_inc(rows_ready, 1)
                                if s + 2 < SL:
                                    attr_copy(s + 2)

                        run.before(act)
                        with act.Fori(0, NCH) as c:
                            if attr:
                                turns(act, c, items)
                            run.scalar(act, c)

                    @block.gpsimd
                    def _(pool):
                        n = pool.value_load(turns_to[0:1, NCH:NCH + 1], min_val=1, max_val=KCAP // SL)
                        with pool.Fori(0, n) as i:
                            for s in range(SL):
                                pool.wait_ge(idx_ready[s], i * 16 + 16)
                                passed(pool, tick)
                                for c in range(GC):
                                    pool.indirect_dma_start(
                                        G[:, s, c, :], None, table,
                                        bass.IndirectOffsetOnAxis(ap=idx[:, s, c:c + 1].bitcast(U32), axis=0)
                                    ).then_inc(gathered[s], 16)

                    @block.vector
                    def _(dve):
                        V.memset(acc[:], 0.0).then_inc(chain, 1)
                        if attr:
                            V.memset(at_[:], 0.0).then_inc(chain, 1)
                        first = 2 if attr else 1
                        dve.wait_ge(chain, first)
                        dve.sem_inc(added, SL)

                        def items(i):
                            own = Chain(dve, chain)
                            own.base = i * SL + first
                            g = [None] * SL

                            def one_hot(s):
                                dve.wait_ge(item_ready, (i * SL + s) * 16 + 16)
                                passed(dve, tick)
                                g[s] = dve.value_load(itm[0:1, s, 2:3], min_val=0, max_val=NG - 1)
                                oh = V.scalar_tensor_tensor(
                                    out=OH[:, s % 2], in0=over(dstI[:, ds(g[s] * GC, GC)], P), scalar=itm[:, s, 0:1],
                                    in1=rows(iota_row[:], GC), op0=ALU.subtract, op1=ALU.is_equal)
                                if weighted:
                                    own.step(oh)
                                    oh = V.tensor_tensor(out=OH[:, s % 2], in0=OH[:, s % 2],
                                                         in1=over(wgt[:, ds(g[s] * GC, GC)], P), op=ALU.mult)
                                oh.then_inc(oh_ready, 1)

                            one_hot(0)
                            for s in range(SL):
                                k = i * SL + s
                                if s + 1 < SL:
                                    one_hot(s + 1)
                                col = dve.value_load(itm[0:1, s, 1:2], min_val=0, max_val=N - 1)
                                if ex is not None:
                                    dve.wait_ge(gathered[s], i * 16 * GC + 16 * GC)
                                    V.tensor_tensor(out=G[:, s].rearrange("p c (h j) -> p (c h) j", h=H),
                                                    in0=G[:, s].rearrange("p c (h j) -> p (c h) j", h=H),
                                                    in1=over(ex[:, ds(g[s] * GC * H, GC * H)], HD),
                                                    op=ALU.mult).then_inc(rows_ready, 1)
                                if attr:
                                    dve.wait_ge(gathered[s], i * 16 * GC + 16 * GC)
                                    dve.wait_ge(ep_ready, k + 1)
                                    for a in range(2):
                                        ga = G[:, s].rearrange("p (q a) f -> p q a f", a=2)[:, :, a, :]
                                        last = V.tensor_tensor(out=ga, in0=ga, in1=ep[a], op=ALU.add)
                                    last.then_inc(summed, 1)
                                dve.wait_ge(product, k + 1)
                                dve.wait_ge(added, k + SL)
                                V.tensor_tensor(out=acc[:, ds(col, P)], in0=acc[:, ds(col, P)], in1=wp[s % 2],
                                                op=ALU.add).then_inc(added, 1)

                        with dve.Fori(0, NCH) as c:
                            turns(dve, c, items)
                            t1 = dve.value_load(turns_to[0:1, ds(c + 1, 1)], min_val=0, max_val=KCAP // SL)
                            dve.wait_ge(added, t1 * SL + SL)
                            dve.sem_inc(acc_ready, 1)
                            run.vector(dve, c)
                            dve.wait_ge(done, c + 1)

                    @block.tensor
                    def _(pe):
                        def items(i):
                            def attr_turn(s):
                                pe.wait_ge(attr_in[s], i * 32 + 32)
                                for c in range(GC // 2):
                                    mm = pe.transpose(tp[:, c, :], at_[:, s, 2 * c:2 * c + 2].rearrange("p a f -> p (a f)"),
                                                      ident[:])
                                mm.then_inc(turned, 1)

                            def attr_product(s):
                                pe.wait_ge(copied, i * SL + s + 1)
                                for c in range(GC):
                                    h = c % 2 * ED
                                    mm = pe.matmul(ep[c % 2][:, c // 2, :], atT[h:h + ED, c // 2, :],
                                                   W(W_M1E)[h:h + ED, :], start=True, stop=True)
                                mm.then_inc(ep_ready, 1)

                            if attr:
                                attr_turn(0)
                                attr_product(0)
                                attr_turn(1)
                            for s in range(SL):
                                k = i * SL + s
                                if attr and s + 1 < SL:
                                    pe.wait_ge(summed, k + 1)
                                    attr_product(s + 1)
                                    if s + 2 < SL:
                                        attr_turn(s + 2)
                                pe.wait_ge(gathered[s], i * 16 * GC + 16 * GC)
                                pe.wait_ge(oh_ready, k + 1)
                                if ex is not None or attr:
                                    pe.wait_ge(rows_ready, k + 1)
                                pe.wait_ge(added, k + SL - 1)
                                for c in range(GC):
                                    mm = pe.matmul(wp[s % 2], G[:, s, c, :], OH[:, s % 2, c, :], start=c == 0, stop=c == GC - 1)
                                mm.then_inc(product, 1)

                        with pe.Fori(0, NCH) as c:
                            turns(pe, c, items)
                            pe.wait_ge(acc_ready, c + 1)
                            run.tensor(pe, c)
                            pe.wait_ge(done, c + 1)

        class Stage:

            def before(self, act):
                pass

            def sync(self, sp):
                pass

        def banks(PS, b, n=CW):
            return PS[:, b:b + 2].rearrange("p a n -> p (a n)")[:, 0:n]

        HW_ = CW // 2

        def transformer(ctx, name, l, PS, hs):
            tb = sb(ctx, f"{name}_tb", [P, 2, T * D])
            pp = [PS[:, 2 * s:2 * s + 2] for s in range(2)]
            tprod, = sems(name, "tprod")
            copied = sems(name, "tcopied0 tcopied1")
            stored = sems(name, "stored0 stored1")
            per = [TC - TC // 2, TC // 2]
            rows_d = trans_d[l].rearrange("(t p) f -> t p f", p=P)

            class Transformer:
                def before(self, act):
                    for s in range(2):
                        act.sem_inc(copied[s], 1)
                        act.sem_inc(stored[s], 16)

                def tensor(self, pe, c):
                    for t in range(TC):
                        s = t % 2
                        pe.wait_ge(copied[s], c * per[s] + t // 2 + 1)
                        for a in range(2):
                            mm = pe.matmul(pp[s][:, a, :], hs[:, t * P:(t + 1) * P], W(W_EDGE + 8 * l + 4 * a, 4),
                                           start=True, stop=True)
                        mm.then_inc(tprod, 1)

                def tile(self, eng, c, t, copy):
                    s = t % 2
                    eng.wait_ge(tprod, c * TC + t + 1)
                    eng.wait_ge(stored[s], (c * per[s] + t // 2 + 1) * 16)
                    copy(tb[:, s, :], pp[s].rearrange("p a f -> p (a f)")).then_inc(copied[s], 1)

                def vector(self, dve, c):
                    for t in range(1, TC, 2):
                        self.tile(dve, c, t, V.tensor_copy)

                def scalar(self, act, c):
                    for t in range(TC):
                        s = t % 2
                        if s == 0:
                            self.tile(act, c, t, act.copy)
                        act.wait_ge(copied[s], c * per[s] + t // 2 + 2)
                        act.dma_start(rows_d[ds(c * TC + t, 1)].rearrange("a p f -> (a p) f"), tb[:, s, :]
                                      ).then_inc(stored[s], 16)

                def sync(self, sp):
                    for s in range(2):
                        sp.wait_ge(stored[s], (NCH * per[s] + 1) * 16)

            return Transformer()

        def gcn_end(ctx, name, PS, buf, st, acc_ready, done):
            st_, r, sq, xT = buf
            hs = sq
            ap_, tp, hp = banks(PS, 0), banks(PS, 2), PS[:, 4:6, 0:HW_]
            staged, turned, nchain, var_ready, rooted, normed, xturned, xcopied, hprod, hready, kept = sems(
                name, "staged turned nchain var_ready rooted normed xturned xcopied hprod hready kept")
            table = transformer(ctx, name, 0, PS, hs)

            class GcnEnd(Stage):
                before, sync = table.before, table.sync

                def scalar(self, act, c):
                    act.wait_ge(acc_ready, c + 1)
                    act.copy(st_, acc[:, ds(c * CW, CW)]).then_inc(staged, 1)
                    root(act, st, var_ready, rooted, c, 1, 0)
                    act.wait_ge(xturned, c + 1)
                    act.copy(xT, tp).then_inc(xcopied, 1)
                    act.wait_ge(hprod, c + 1)
                    act.activation(hs.rearrange("p (a n) -> p a n", a=2), hp, ACT.Relu,
                                   bias=bcol[:, C_PROJ:C_PROJ + 1]).then_inc(hready, 1)
                    table.scalar(act, c)
                    act.wait_ge(kept, c + 1)
                    act.sem_inc(done, 1)

                def tensor(self, pe, c):
                    pe.wait_ge(staged, c + 1)
                    turn_tiles(pe, ap_, st_).then_inc(turned, 1)
                    pe.wait_ge(normed, c + 1)
                    turn_tiles(pe, tp, r).then_inc(xturned, 1)
                    pe.wait_ge(xcopied, c + 1)
                    for a in range(2):
                        mm = pe.matmul(hp[:, a, :], W(W_PROJ), xT[:, a * HW_:(a + 1) * HW_], start=True, stop=True)
                    mm.then_inc(hprod, 1)
                    pe.wait_ge(hready, c + 1)
                    table.tensor(pe, c)

                def vector(self, dve, c):
                    own = Chain(dve, nchain, 4 + NORM_STEPS, c)
                    at, r3 = ds(c * CW, CW), tiles3(r)
                    dve.wait_ge(turned, c + 1)
                    own.step(V.tensor_tensor(out=r, in0=HB[:, at], in1=ap_, op=ALU.add))
                    own.step(V.tensor_tensor(out=r3, in0=r3, in1=over(dinv[:, ds(c * TC, TC)], D), op=ALU.mult))
                    own.step(V.tensor_tensor(out=r3, in0=r3, in1=rows(bias[:, B_L0, :], TC), op=ALU.add))
                    own.step(V.tensor_tensor(out=r, in0=r, in1=X[:, at], op=ALU.add))
                    norm(dve, own, r, sq, st, var_ready, rooted, c, 1, 0)
                    dve.sem_inc(normed, 1)
                    passed(dve, tick)
                    V.tensor_copy(X[:, at], r)
                    dve.wait_ge(hready, c + 1)
                    passed(dve, tick)
                    V.tensor_copy(HB[:, at], hs).then_inc(kept, 1)
                    table.vector(dve, c)
                    assert own.n == 4 + NORM_STEPS, own.n

            return GcnEnd()

        def gru_parts(name, l, PS, buf):
            rg, zg, ng, hs = (b.rearrange("p (a n) -> p a n", a=2) for b in buf)
            gp = [PS[:, 2 * k:2 * k + 2, 0:HW_] for k in range(4)]
            gprod, gates, pre, tanhed, gchain, hready = sems(name, "gprod gates pre tanhed gchain hready")

            class Gru:
                ready = hready

                def tensor(self, pe, c):
                    for a in range(2):
                        x_ = acc[:, ds(c * CW + a * HW_, HW_)]
                        h_ = HB[:, ds(c * CW + a * HW_, HW_)]
                        for k in range(2):
                            pe.matmul(gp[k][:, a, :], W(W_IH + 3 * l + k), x_, start=True, stop=False)
                            pe.matmul(gp[k][:, a, :], W(W_HH + 3 * l + k), h_, start=False, stop=True)
                        pe.matmul(gp[2][:, a, :], W(W_IH + 3 * l + 2), x_, start=True, stop=True)
                        mm = pe.matmul(gp[3][:, a, :], W(W_HH + 3 * l + 2), h_, start=True, stop=True)
                    mm.then_inc(gprod, 1)

                def scalar(self, act, c):
                    rz = C_RZ + 3 * l
                    act.wait_ge(gprod, c + 1)
                    act.activation(rg, gp[0], ACT.Sigmoid, bias=bcol[:, rz:rz + 1]).then_inc(gates, 1)
                    act.activation(zg, gp[1], ACT.Sigmoid, bias=bcol[:, rz + 1:rz + 2]).then_inc(gates, 1)
                    act.wait_ge(pre, c + 1)
                    act.activation(ng, ng, ACT.Tanh, bias=bcol[:, C_IH + 3 * l + 2:C_IH + 3 * l + 3]).then_inc(tanhed, 1)

                def vector(self, dve, c):
                    own = Chain(dve, gchain, 4, c)
                    h_ = HB[:, ds(c * CW, CW)].rearrange("p (a n) -> p a n", a=2)
                    hh = C_HH + 3 * l + 2
                    dve.wait_ge(gates, c * 2 + 2)
                    own.step(V.scalar_tensor_tensor(out=ng, in0=gp[3], scalar=bcol[:, hh:hh + 1], in1=rg,
                                                    op0=ALU.add, op1=ALU.mult))
                    V.tensor_tensor(out=ng, in0=ng, in1=gp[2], op=ALU.add).then_inc(pre, 1)
                    dve.wait_ge(tanhed, c + 1)
                    own.step(V.tensor_tensor(out=rg, in0=h_, in1=ng, op=ALU.subtract))
                    own.step(V.tensor_tensor(out=rg, in0=rg, in1=zg, op=ALU.mult))
                    own.step(V.tensor_tensor(out=rg, in0=rg, in1=ng, op=ALU.add))
                    V.tensor_scalar(hs, rg, 0.0, None, ALU.max).then_inc(hready, 1)

            return Gru()

        def ggnn_next(ctx, name, PS, buf, st, acc_ready, done):
            hs = buf[3]
            kept, = sems(name, "kept")
            gru, table = gru_parts(name, 0, PS, buf), transformer(ctx, name, 1, PS, hs)

            class GgnnNext(Stage):
                before, sync = table.before, table.sync

                def scalar(self, act, c):
                    gru.scalar(act, c)
                    table.scalar(act, c)
                    act.wait_ge(kept, c + 1)
                    act.sem_inc(done, 1)

                def tensor(self, pe, c):
                    gru.tensor(pe, c)
                    pe.wait_ge(gru.ready, c + 1)
                    table.tensor(pe, c)

                def vector(self, dve, c):
                    gru.vector(dve, c)
                    dve.wait_ge(gru.ready, c + 1)
                    passed(dve, tick)
                    V.tensor_copy(HB[:, ds(c * CW, CW)], hs).then_inc(kept, 1)
                    table.vector(dve, c)

            return GgnnNext()

        def ggnn_end(ctx, name, PS, buf, st, acc_ready, done):
            r, sq, xT, hs = buf
            op_, tp, xp, sp_ = banks(PS, 0), banks(PS, 2), banks(PS, 4), PS[:, 6, 0:TC * 2 * H]
            gru = gru_parts(name, 1, PS, buf)
            oprod, nchain, var_ready, rooted, normed, xturned, xcopied, heads = sems(
                name, "oprod nchain var_ready rooted normed xturned xcopied heads")

            class GgnnEnd(Stage):
                def scalar(self, act, c):
                    gru.scalar(act, c)
                    root(act, st, var_ready, rooted, c, 1, 0)
                    act.wait_ge(xturned, c + 1)
                    act.copy(xT, tp).then_inc(xcopied, 1)

                def tensor(self, pe, c):
                    gru.tensor(pe, c)
                    pe.wait_ge(gru.ready, c + 1)
                    times(pe, op_, hs, W(W_OUT)).then_inc(oprod, 1)
                    pe.wait_ge(normed, c + 1)
                    turn_tiles(pe, tp, r).then_inc(xturned, 1)
                    pe.wait_ge(xcopied, c + 1)
                    times(pe, xp, xT, wall[:])
                    times(pe, sp_, xT, wa[:], width=2 * H).then_inc(heads, 1)

                def vector(self, dve, c):
                    gru.vector(dve, c)
                    STEPS = 2 + NORM_STEPS + 1
                    own = Chain(dve, nchain, STEPS, c)
                    at, r3 = ds(c * CW, CW), tiles3(r)
                    dve.wait_ge(oprod, c + 1)
                    own.step(V.tensor_tensor(out=r, in0=X[:, at], in1=op_, op=ALU.add))
                    own.step(V.tensor_tensor(out=r3, in0=r3, in1=rows(bias[:, B_OUT, :], TC), op=ALU.add))
                    norm(dve, own, r, sq, st, var_ready, rooted, c, 1, 0)
                    dve.sem_inc(normed, 1)
                    passed(dve, tick)
                    V.tensor_copy(X[:, at], r)
                    dve.wait_ge(heads, c + 1)
                    passed(dve, tick)
                    own.step(V.tensor_copy(S[:, ds(c * TC, TC), :], sp_.rearrange("p (t s) -> p t s", t=TC)))
                    passed(dve, tick)
                    V.tensor_copy(HB[:, at], xp).then_inc(done, 1)
                    assert own.n == STEPS, own.n

            return GgnnEnd()

        def gat_end(ctx, name, PS, buf, st, acc_ready, done):
            st_, r, sq, xT = buf
            ap_, tp, hp = banks(PS, 0), banks(PS, 2), banks(PS, 4)
            staged, turned, nchain, var_ready, rooted, normed, xturned, xcopied, mprod, stored = sems(
                name, "staged turned nchain var_ready rooted normed xturned xcopied mprod stored")

            class GatEnd(Stage):
                def scalar(self, act, c):
                    act.wait_ge(acc_ready, c + 1)
                    act.copy(st_, acc[:, ds(c * CW, CW)]).then_inc(staged, 1)
                    for k in range(2):
                        root(act, st, var_ready, rooted, c, 2, k)
                    act.wait_ge(xturned, c + 1)
                    act.copy(xT, tp).then_inc(xcopied, 1)

                def tensor(self, pe, c):
                    pe.wait_ge(staged, c + 1)
                    turn_tiles(pe, ap_, st_).then_inc(turned, 1)
                    pe.wait_ge(normed, c + 1)
                    turn_tiles(pe, tp, r).then_inc(xturned, 1)
                    pe.wait_ge(xcopied, c + 1)
                    times(pe, hp, xT, W(W_M1X)).then_inc(mprod, 1)

                def vector(self, dve, c):
                    STEPS = 4 + 2 * NORM_STEPS
                    own = Chain(dve, nchain, STEPS, c)
                    at, r3 = ds(c * CW, CW), tiles3(r)
                    dve.wait_ge(turned, c + 1)
                    own.step(V.tensor_tensor(out=r, in0=X[:, at], in1=ap_, op=ALU.add))
                    norm(dve, own, r, sq, st, var_ready, rooted, c, 2, 0)
                    own.step(V.tensor_tensor(out=r3, in0=r3, in1=rows(bias[:, B_GAMMA, :], TC), op=ALU.mult))
                    own.step(V.tensor_tensor(out=r3, in0=r3, in1=rows(bias[:, B_BETA, :], TC), op=ALU.add))
                    own.step(V.tensor_tensor(out=r, in0=r, in1=X[:, at], op=ALU.add))
                    norm(dve, own, r, sq, st, var_ready, rooted, c, 2, 1)
                    dve.sem_inc(normed, 1)
                    passed(dve, tick)
                    V.tensor_copy(X[:, at], r)
                    dve.wait_ge(mprod, c + 1)
                    V.tensor_tensor(out=tiles3(HB[:, at]), in0=tiles3(hp), in1=rows(bias[:, B_M1, :], TC),
                                    op=ALU.add).then_inc(done, 1)
                    assert own.n == STEPS, own.n

                def sync(self, sp):
                    for c in range(NCH):
                        sp.wait_ge(done, c + 1)
                        sp.dma_start(msg_d[c * CW:(c + 1) * CW].rearrange("(t p) f -> p t f", p=P),
                                     tiles3(HB[:, c * CW:(c + 1) * CW])).then_inc(stored, 16)
                    sp.wait_ge(stored, 16 * NCH)

            return GatEnd()

        def mpnn_end(ctx, name, PS, buf, st, acc_ready, done):
            as_, xs, xT, u = buf
            r, sq = xs, as_
            tp, xp, mp = banks(PS, 0), banks(PS, 2), banks(PS, 4)
            staged, turned, xcopied, uprod, nchain, hidden, delta, var_ready, rooted, stored = sems(
                name, "staged turned xcopied uprod nchain hidden delta var_ready rooted stored")

            class MpnnEnd(Stage):
                def scalar(self, act, c):
                    act.wait_ge(acc_ready, c + 1)
                    act.copy(as_, acc[:, ds(c * CW, CW)])
                    act.copy(xs, X[:, ds(c * CW, CW)]).then_inc(staged, 1)
                    for k in range(2):
                        act.wait_ge(turned, c * 2 + k + 1)
                        act.copy(xT, tp).then_inc(xcopied, 1)
                    for k in range(2):
                        root(act, st, var_ready, rooted, c, 2, k)

                def tensor(self, pe, c):
                    pe.wait_ge(staged, c + 1)
                    turn_tiles(pe, tp, xs).then_inc(turned, 1)
                    times(pe, mp, as_, wcomb[:])
                    pe.wait_ge(xcopied, c * 2 + 1)
                    times(pe, xp, xT, W(W_U1X)).then_inc(uprod, 1)
                    pe.wait_ge(hidden, c + 1)
                    turn_tiles(pe, tp, u).then_inc(turned, 1)
                    pe.wait_ge(xcopied, c * 2 + 2)
                    times(pe, xp, xT, W(W_U2)).then_inc(delta, 1)

                def vector(self, dve, c):
                    STEPS = 10 + 2 * NORM_STEPS
                    own = Chain(dve, nchain, STEPS, c)
                    at, att, r3, u3 = ds(c * CW, CW), ds(c * TC, TC), tiles3(r), tiles3(u)
                    dve.wait_ge(uprod, c + 1)
                    own.step(V.tensor_tensor(out=u3, in0=tiles3(mp), in1=over(cntinv[:, att], D), op=ALU.mult))
                    own.step(V.tensor_tensor(out=u, in0=u, in1=xp, op=ALU.add))
                    own.step(V.tensor_tensor(out=r3, in0=over(has[:, att], D), in1=rows(bias[:, B_V, :], TC), op=ALU.mult))
                    own.step(V.tensor_tensor(out=u, in0=u, in1=r, op=ALU.add))
                    own.step(V.tensor_tensor(out=u3, in0=u3, in1=rows(bias[:, B_U1, :], TC), op=ALU.add))
                    V.tensor_scalar(u, u, 0.0, None, ALU.max).then_inc(hidden, 1)
                    dve.wait_ge(delta, c + 1)
                    own.step(V.tensor_tensor(out=r, in0=X[:, at], in1=xp, op=ALU.add))
                    own.step(V.tensor_tensor(out=r3, in0=r3, in1=rows(bias[:, B_U2, :], TC), op=ALU.add))
                    norm(dve, own, r, sq, st, var_ready, rooted, c, 2, 0)
                    own.step(V.tensor_tensor(out=r3, in0=r3, in1=rows(bias[:, B_LNG, :], TC), op=ALU.mult))
                    own.step(V.tensor_tensor(out=r3, in0=r3, in1=rows(bias[:, B_LNB, :], TC), op=ALU.add))
                    own.step(V.tensor_tensor(out=r, in0=r, in1=X[:, at], op=ALU.add))
                    norm(dve, own, r, sq, st, var_ready, rooted, c, 2, 1)
                    passed(dve, tick)
                    V.tensor_copy(X[:, at], r).then_inc(done, 1)
                    assert own.n == STEPS, own.n

                def sync(self, sp):
                    for c in range(NCH):
                        sp.wait_ge(done, c + 1)
                        full = min((c + 1) * CW, NPAD - P)
                        sp.dma_start(out[c * CW:full].rearrange("(t p) f -> p t f", p=P),
                                     tiles3(X[:, c * CW:full])).then_inc(stored, 16)
                    sp.dma_start(out[NPAD - P:N], X[0:NLAST, NPAD - P:]).then_inc(stored, 16)
                    sp.wait_ge(stored, 16 * (NCH + 1))

            return MpnnEnd()

        aggregate("gcn_edges", gcn_d, src_d, gcn_end, weighted=True)
        for l, stage in enumerate((ggnn_next, ggnn_end)):
            aggregate(f"ggnn{l}_edges", trans_d[l].rearrange("n (t f) -> (n t) f", t=T), row_d, stage)
        early.close()

        with ExitStack() as ctx:
            ctx.callback(end_stage)
            sjm = sb(ctx, "sjm", [P, NT, H])
            real = sb(ctx, "real", [P, NT])
            A = sb(ctx, "A", [P, NT, 2 * H])
            J = sb(ctx, "J", [P, NT, 2 * H])
            J3 = sb(ctx, "J3", [P, NT, 3, 2 * H], BF16)
            zr = sb(ctx, "zr", [P, 6 * H], BF16)
            mx = sb(ctx, "mx", [P, H])
            m8 = sb(ctx, "m8", [H, 1])
            dg = sb(ctx, "dg", [H, H])
            mb = sb(ctx, "mb", [P, H])
            mp = ps(ctx, "mp", [P, P])
            bp = ps(ctx, "bp", [P, H])
            iotas, maxed, turned, diag, spread, tables, stored, chain = sems(
                "max", "iotas maxed turned diag spread tables stored chain")
            with nc.Block() as block:
                @block.gpsimd
                def _(pool):
                    pool.iota(real[:], [[P, NT]], base=0, channel_multiplier=1,
                              allow_small_or_imprecise_dtypes=True).then_inc(iotas, 1)

                @block.vector
                def _(dve):
                    own = Chain(dve, chain)
                    own.step(V.memset(zr[:], 0.0))
                    dve.wait_ge(iotas, 1)
                    own.step(V.tensor_scalar(real[:], real[:], float(N), None, ALU.is_lt))
                    own.step(V.tensor_tensor(out=sjm[:], in0=S[:, :, H:2 * H], in1=over(real[:], H), op=ALU.mult))
                    own.step(V.tensor_scalar(real[:], real[:], 3e38, -3e38, ALU.mult, ALU.add))
                    own.step(V.tensor_tensor(out=sjm[:], in0=sjm[:], in1=over(real[:], H), op=ALU.add))
                    V.tensor_reduce(mx[:], sjm[:].rearrange("p t h -> p h t"), AX, ALU.max).then_inc(maxed, 1)
                    dve.wait_ge(turned, 1)
                    own.step(V.tensor_reduce(m8[:], mp[0:H, :], AX, ALU.max))
                    V.tensor_scalar(dg[:], ident[0:H, 0:H], m8[:, 0:1], None, ALU.mult).then_inc(diag, 1)
                    dve.wait_ge(spread, 1)
                    own.step(V.tensor_copy(mb[:], bp[:]))
                    own.step(V.tensor_copy(A[:, :, 0:H], S[:, :, 0:H]))
                    own.step(V.tensor_tensor(out=J[:, :, 0:H], in0=S[:, :, 0:H], in1=rows(mb[:], NT), op=ALU.add))
                    own.step(V.scalar_tensor_tensor(out=A[:, :, H:2 * H], in0=J[:, :, 0:H], scalar=ALPHA, in1=J[:, :, 0:H],
                                                    op0=ALU.mult, op1=ALU.max))
                    own.step(V.memset(J[:, :, H:2 * H], 1.0))
                    own.step(V.tensor_copy(J[:, :, 0:H], S[:, :, H:2 * H]))
                    for a in range(3):
                        own.step(V.tensor_copy(J3[:, :, a, :], J[:]))
                        own.step(V.tensor_tensor(out=J[:], in0=J[:], in1=J3[:, :, a, :], op=ALU.subtract))
                    dve.sem_inc(tables, 1)

                @block.tensor
                def _(pe):
                    pe.wait_ge(maxed, 1)
                    pe.transpose(mp[0:H, :], mx[:], ident[:]).then_inc(turned, 1)
                    pe.wait_ge(diag, 1)
                    pe.matmul(bp[:], ones[0:H, :], dg[:], start=True, stop=True).then_inc(spread, 1)

                @block.sync
                def _(sp):
                    sp.wait_ge(tables, 1)
                    sp.dma_start(att_d.rearrange("(t p) s -> p t s", p=P), A[:]).then_inc(stored, 16)
                    sp.dma_start(sj_d[0:NPAD].rearrange("(t p) s -> p t s", p=P),
                                 J3[:].rearrange("p t a s -> p t (a s)")).then_inc(stored, 16)
                    sp.dma_start(sj_d[NPAD:ACCW], zr[:]).then_inc(stored, 16)
                    sp.wait_ge(stored, 48)

        gat = whole.enter_context(ExitStack())
        ex = sb(gat, "ex", [P, NG * GC * H])
        NX, NQ = 4, GC // 2
        assert SL * NQ % NX == 0
        with ExitStack() as ctx:
            ctx.callback(end_stage)
            G = sb(ctx, "at_G", [P, SL, GC, 2 * H])
            dr = sb(ctx, "dr", [P, 2, GE], I32)
            ohT = sb(ctx, "ohT", [P, GC, P], BF16)
            ohl = [acc[:, b * GE:(b + 1) * GE].rearrange("p (c n) -> p c n", c=GC) for b in range(2)]
            exh = sb(ctx, "exh", [P, NX, 2, NT, H])
            sjw = sb(ctx, "sjw", [P, SL, 3, 2 * H], BF16)
            idx = sb(ctx, "at_idx", [P, SL, GC], I32)
            srch = sb(ctx, "srch", [P, GC], I32)
            srcl = sb(ctx, "srcl", [P, GC], I32)
            itm = sb(ctx, "at_itm", [P, SL, 4], I32)
            e_ = sb(ctx, "e_", [P, GC, H])
            x_ = sb(ctx, "x_", [P, GC, H])
            em = sb(ctx, "em", [P, GC, H])
            zero = sb(ctx, "zero2", [P, NT * H])
            jps = [ps(ctx, f"jp{b}", [P, GC, 2 * H]) for b in range(2)]
            dp = ps(ctx, "dp", [P, NT * H])
            gathered = sems("at", " ".join(f"gathered{s}" for s in range(SL)))
            idx_ready = sems("at", " ".join(f"idx_ready{s}" for s in range(SL)))
            item_ready, done, window_in, oht_ready, sj_ready, chain, diff, exped, exh_ready, exh_free, zeroed, summed = sems(
                "at", "item_ready done window_in oht_ready sj_ready chain diff exped exh_ready exh_free zeroed summed")
            with nc.Block() as block:
                @block.sync
                def _(sp):
                    n = sp.value_load(turns_to[0:1, NCH:NCH + 1], min_val=1, max_val=KCAP // SL)
                    with sp.Fori(0, n) as i:
                        for s in range(SL):
                            k = i * SL + s
                            sp.wait_ge(done, k + 1)
                            sp.dma_start(itm[:, s, :], items_d[ds(k, 1), :].to_broadcast([P, 4])
                                         ).then_inc(item_ready, 16)
                            sp.wait_ge(item_ready, k * 16 + 16)
                            passed(sp, tick)
                            g = sp.value_load(itm[0:1, s, 2:3], min_val=0, max_val=NG - 1)
                            col = sp.value_load(itm[0:1, s, 1:2], min_val=0, max_val=N - 1)
                            sp.dma_start(idx[:, s, :], src_d[ds(g, 1), :].rearrange("a (p c) -> (a p) c", c=GC)
                                         ).then_inc(idx_ready[s], 16)
                            sp.wait_ge(oht_ready, k + 1)
                            sp.dma_start(dr[:, s % 2], dst_d[ds(g, 1), :].to_broadcast([P, GE])).then_inc(window_in, 16)
                            sp.dma_start(sjw[:, s].rearrange("p a h -> p (a h)"), sj_d[ds(col, P), :]).then_inc(window_in, 16)

                @block.scalar
                def _(act):
                    n = act.value_load(turns_to[0:1, NCH:NCH + 1], min_val=1, max_val=KCAP // SL)
                    with act.Fori(0, n) as i:
                        for s in range(SL):
                            act.wait_ge(diff, i * SL + s + 1)
                            act.activation(x_[:], e_[:], ACT.Exp).then_inc(exped, 1)

                @block.gpsimd
                def _(pool):
                    n = pool.value_load(turns_to[0:1, NCH:NCH + 1], min_val=1, max_val=KCAP // SL)
                    with pool.Fori(0, n) as i:
                        for s in range(SL):
                            pool.wait_ge(idx_ready[s], i * 16 + 16)
                            passed(pool, tick)
                            for c in range(GC):
                                pool.indirect_dma_start(
                                    G[:, s, c, :], None, att_d,
                                    bass.IndirectOffsetOnAxis(ap=idx[:, s, c:c + 1].bitcast(U32), axis=0)
                                ).then_inc(gathered[s], 16)

                @block.tensor
                def _(pe):
                    pe.wait_ge(zeroed, 1)
                    pe.matmul(dp[:], zero[:, 0:P], zero[:], start=True, stop=False, skip_group_check=True)\
                        .then_inc(exh_free, NX + NQ)
                    n = pe.value_load(turns_to[0:1, NCH:NCH + 1], min_val=1, max_val=KCAP // SL)

                    with pe.Fori(0, n) as i:
                        def spread_sj(s):
                            pe.wait_ge(oht_ready, i * SL + s + 3)
                            for c in range(GC):
                                for a in range(3):
                                    mm = pe.matmul(jps[s % 2][:, c, :], ohT[:, c, :], sjw[:, s, a, :], start=a == 0, stop=a == 2)
                            mm.then_inc(sj_ready, 1)

                        spread_sj(0)
                        for s in range(SL):
                            if s + 1 < SL:
                                spread_sj(s + 1)
                            for q in range(NQ):
                                pe.wait_ge(exh_ready, (i * SL + s) * NQ + q + 1)
                                for c in range(2):
                                    mm = pe.matmul(dp[:], ohl[s % 2][:, 2 * q + c, :],
                                                   exh[:, (s * NQ + q) % NX, c].rearrange("p t h -> p (t h)"),
                                                   start=False, stop=False, skip_group_check=True)
                                mm.then_inc(exh_free, 1)
                    pe.matmul(dp[:], zero[:, 0:P], zero[:], start=False, stop=True, skip_group_check=True).then_inc(summed, 1)

                @block.vector
                def _(dve):
                    V.memset(zero[:], 0.0).then_inc(zeroed, 1)
                    V.memset(ex[:], 0.0).then_inc(chain, 1)
                    dve.wait_ge(chain, 1)
                    dve.sem_inc(done, SL)
                    dve.sem_inc(oht_ready, 2)
                    n = dve.value_load(turns_to[0:1, NCH:NCH + 1], min_val=1, max_val=KCAP // SL)
                    STEPS = SL * 7
                    with dve.Fori(0, n) as i:
                        own = Chain(dve, chain)
                        own.base = i * STEPS + 1

                        def window_hot(s):
                            k = i * SL + s
                            dve.wait_ge(window_in, k * 32 + 32)
                            V.tensor_scalar(ohT[:], dr[:, s % 2].rearrange("n (p c) -> n c p", c=GC), itm[:, s, 0:1], iota_colI[:, 0:1],
                                            ALU.subtract, ALU.is_equal).then_inc(oht_ready, 1)

                        window_hot(0)
                        for s in range(SL):
                            k = i * SL + s
                            jp = jps[s % 2]
                            dve.wait_ge(idx_ready[s], i * 16 + 16)
                            own.step(V.tensor_single_scalar(srcl[:], idx[:, s, :], P - 1, op=ALU.bitwise_and))
                            own.step(V.tensor_single_scalar(srch[:], idx[:, s, :], 7, op=ALU.arith_shift_right))
                            passed(dve, tick)
                            g = dve.value_load(itm[0:1, s, 2:3], min_val=0, max_val=NG - 1)
                            dve.wait_ge(gathered[s], i * 16 * GC + 16 * GC)
                            dve.wait_ge(sj_ready, k + 1)
                            own.step(V.tensor_tensor(out=x_[:], in0=G[:, s, :, 0:H], in1=jp[:, :, 0:H], op=ALU.add))
                            own.step(V.scalar_tensor_tensor(out=e_[:], in0=x_[:], scalar=ALPHA, in1=x_[:], op0=ALU.mult, op1=ALU.max))
                            own.step(V.tensor_tensor(out=e_[:], in0=e_[:], in1=G[:, s, :, H:2 * H], op=ALU.subtract))
                            V.tensor_scalar(e_[:], e_[:], 0.0, None, ALU.min).then_inc(diff, 1)
                            dve.wait_ge(exh_free, k * NQ + NX)
                            V.tensor_tensor(out=ohl[s % 2], in0=over(srcl[:], P), in1=rows(iota_row[:], GC), op=ALU.is_equal)
                            if s + 1 < SL:
                                window_hot(s + 1)
                            dve.wait_ge(exped, k + 1)
                            own.step(V.tensor_tensor(out=em[:], in0=x_[:], in1=jp[:, :, H:2 * H], op=ALU.mult))
                            for q in range(NQ):
                                dve.wait_ge(exh_free, (k + 1) * NQ + q + 1)
                                for c in range(2):
                                    j = 2 * q + c
                                    last = V.scalar_tensor_tensor(
                                        out=exh[:, (s * NQ + q) % NX, c], in0=over(iota_row[:, 0:NT], H),
                                        scalar=srch[:, j:j + 1], in1=rows(em[:, j, :], NT), op0=ALU.is_equal, op1=ALU.mult)
                                last.then_inc(exh_ready, 1)
                            exg = ex[:, ds(g * GC * H, GC * H)].rearrange("p (c h) -> p c h", h=H)
                            own.step(V.tensor_tensor(out=exg, in0=exg, in1=em[:], op=ALU.add))
                            dve.sem_inc(done, 1)
                        assert own.n == STEPS, own.n
                    dve.wait_ge(summed, 1)
                    V.tensor_copy(den[:].rearrange("p t h -> p (t h)"), dp[:]).then_inc(zeroed, 1)
                    dve.wait_ge(zeroed, 2)

        with ExitStack() as ctx:
            ctx.callback(end_stage)
            chain, scaled, stored = sems("heads", "chain scaled stored")
            with nc.Block() as block:
                @block.vector
                def _(dve):
                    own = Chain(dve, chain)
                    own.step(V.tensor_scalar(den[:], den[:], 1e-30, None, ALU.max))
                    own.step(V.reciprocal(den[:], den[:]))
                    hb = HB[:].rearrange("p (q j) -> p q j", j=HD)
                    V.tensor_tensor(out=hb, in0=hb, in1=over(den[:].rearrange("p t h -> p (t h)"), HD),
                                    op=ALU.mult).then_inc(scaled, 1)

                @block.sync
                def _(sp):
                    sp.wait_ge(scaled, 1)
                    sp.dma_start(heads_d.rearrange("(t p) f -> p t f", p=P), tiles3(HB[:])).then_inc(stored, 16)
                    sp.wait_ge(stored, 16)

        aggregate("gat_edges", heads_d, src_d, gat_end, ex=ex)
        gat.close()
        aggregate("mpnn_edges", msg_d, src_d, mpnn_end, attr=True)


_INS = ['x', 'src', 'dst', 'edge_attr_64', 'edge_type_8', 'edge_weight', 'L0_gnn_W', 'L0_gnn_b', 'L1_gnn_node_proj_w',
        'L1_gnn_node_proj_b', 'L1_gnn_edge_W', 'L1_gnn_edge_b', 'L1_gnn_gru_wih', 'L1_gnn_gru_whh', 'L1_gnn_gru_bih',
        'L1_gnn_gru_bhh', 'L1_gnn_out_w', 'L1_gnn_out_b', 'L2_gnn_W', 'L2_gnn_a', 'L2_gnn_ln_gamma', 'L2_gnn_ln_beta',
        'L3_gnn_global_state', 'L3_gnn_Wm1', 'L3_gnn_bm1', 'L3_gnn_Wm2', 'L3_gnn_bm2', 'L3_gnn_Wu1', 'L3_gnn_bu1',
        'L3_gnn_Wu2', 'L3_gnn_bu2', 'L3_gnn_ln_g', 'L3_gnn_ln_b']


def kernel(**inputs):
    import concourse.bacc as _bacc
    import numpy as _np
    from concourse.bass_utils import run_bass_kernel_spmd as _run

    nc = _bacc.Bacc("TRN2", target_bir_lowering=False, num_devices=1)
    arrays, args = {}, []
    for name in _INS:
        a = _np.ascontiguousarray(inputs[name])
        arrays[f"in_{name}"] = a
        args.append(nc.dram_tensor(f"in_{name}", a.shape, mybir.dt.from_np(a.dtype), kind="ExternalInput").ap())
    args.append(nc.dram_tensor("out_0", (N, D), F32, kind="ExternalOutput").ap())
    build(nc, *args)
    r = _run(nc, [arrays], core_ids=[0])
    return r.results[0]["out_0"]
```

```python
from contextlib import ExitStack

import concourse.bass as bass
from concourse import mybir

F32 = mybir.dt.float32
BF16 = mybir.dt.bfloat16
I32 = mybir.dt.int32
U32 = mybir.dt.uint32
ALU = mybir.AluOpType
ACT = mybir.ActivationFunctionType
AX = mybir.AxisListType.X
ds = bass.ds

P = 128
D = 128
N = 6250
E = 200000
NT = -(-N // P)
NPAD = NT * P
NLAST = N - (NT - 1) * P
TC = 7
NCH = NT // TC
CW = TC * P
GC = 14
GE = GC * P
NG = -(-E // GE)
PLAST = (E - (NG - 1) * GE) // GC
CLAST = (E - (NG - 1) * GE) % GC
SL = 4
T = 8
H = 8
HD = 16
ED = 64
ACCW = NPAD + P
FAR = 1000000
KCAP = -(-(NG * NT) // P) * P
KT = KCAP // P
NOBASE = 8000000.0
EPS = 1e-5
ALPHA = 0.2
E_TOP = 60.0
DEN_LOW, DEN_HIGH = 1e-20, 1e25
ROUNDS = 32
assert NT == NCH * TC and NG <= P and CLAST > 0

W_PROJ, W_EDGE, W_IH, W_HH, W_OUT, W_HEADS, W_M1X, W_M1E, W_M1G, W_U1X, W_U1A, W_U1G, W_U2 = (
    0, 1, 17, 23, 29, 30, 31, 32, 33, 34, 35, 36, 37)
NW = 40


class Chain:

    def __init__(self, eng, sem, per_turn=0, turn=0):
        self.eng, self.sem, self.n, self.base = eng, sem, 0, turn * per_turn

    def step(self, ins):
        ins.then_inc(self.sem, 1)
        self.n += 1
        self.eng.wait_ge(self.sem, self.base + self.n)


def passed(eng, tick):
    eng.sem_inc(tick, 1)


def over(ap, n):
    return ap.unsqueeze(2).to_broadcast([ap.shape[0], ap.shape[1], n])


def rows(ap, n):
    return ap.unsqueeze(1).to_broadcast([ap.shape[0], n, ap.shape[1]])


def build(nc, x, src, dst, edge_attr_64, edge_type_8, edge_weight, L0_gnn_W, L0_gnn_b, L1_gnn_node_proj_w,
          L1_gnn_node_proj_b, L1_gnn_edge_W, L1_gnn_edge_b, L1_gnn_gru_wih, L1_gnn_gru_whh, L1_gnn_gru_bih,
          L1_gnn_gru_bhh, L1_gnn_out_w, L1_gnn_out_b, L2_gnn_W, L2_gnn_a, L2_gnn_ln_gamma, L2_gnn_ln_beta,
          L3_gnn_global_state, L3_gnn_Wm1, L3_gnn_bm1, L3_gnn_Wm2, L3_gnn_bm2, L3_gnn_Wu1, L3_gnn_bu1,
          L3_gnn_Wu2, L3_gnn_bu2, L3_gnn_ln_g, L3_gnn_ln_b, out):
    V = nc.vector

    def dram(name, shape, dt=F32):
        return nc.dram_tensor(name, shape, dt, kind="Internal").ap()

    items_d = dram("items_d", [KCAP, 4], I32)
    dst_d = dram("dst_d", [NG, GE], I32)
    src_d = dram("src_d", [NG, GE], I32)
    row_d = dram("row_d", [NG, GE], I32)
    gcn_d = dram("gcn_d", [NPAD, D])
    trans_d = [dram(f"trans_d{l}", [NPAD, T * D]) for l in range(2)]
    att_d = dram("att_d", [NPAD, 2 * H])
    sj_d = dram("sj_d", [ACCW, 6 * H], BF16)
    heads_d = dram("heads_d", [NPAD, D])
    msg_d = dram("msg_d", [NPAD, D])

    def sb(ctx, name, shape, dt=F32):
        return ctx.enter_context(nc.sbuf_tensor(name, shape, dt))

    def ps(ctx, name, shape):
        return ctx.enter_context(nc.psum_tensor(name, shape, F32))

    in_stage = []

    def sems(prefix, names):
        made = [nc.alloc_semaphore(name=f"{prefix}_{n}") for n in names.split()]
        in_stage.extend(made)
        return made

    def end_stage():
        nc.clear_and_free_semaphores(list(in_stage))
        in_stage.clear()
        nc.all_engine_barrier()

    with ExitStack() as whole:
        tick = whole.enter_context(nc.semaphore("tick"))
        X = sb(whole, "X", [P, NPAD])
        HB = sb(whole, "HB", [P, NPAD])
        acc = sb(whole, "acc", [P, ACCW])
        dstI = sb(whole, "dstI", [P, NG * GC], I32)
        iota_row = sb(whole, "iota_row", [P, P])
        iota_col = sb(whole, "iota_col", [P, 1])
        iota_colI = sb(whole, "iota_colI", [P, 1], I32)
        ident = sb(whole, "ident", [P, P])
        ones = sb(whole, "ones", [P, P])
        wt_late = sb(whole, "wt_late", [P, (NW - W_HEADS) * P])
        w0 = sb(whole, "w0", [P, D])
        wall = sb(whole, "wall", [P, D])
        wa = sb(whole, "wa", [P, 2 * H])
        wcomb = sb(whole, "wcomb", [P, D])
        bias = sb(whole, "bias", [P, 11, D])
        bcol = sb(whole, "bcol", [P, 32])
        deg = sb(whole, "deg", [P, 2, NT])
        dinv = sb(whole, "dinv", [P, NT])
        cntinv = sb(whole, "cntinv", [P, NT])
        has = sb(whole, "has", [P, NT])
        turns_to = sb(whole, "turns_to", [1, 2 * (NCH + 1)], I32)
        S = sb(whole, "S", [P, NT, 2 * H])
        den = sb(whole, "den", [P, NT, H])
        sj_ends = sb(whole, "sj_ends", [P, 2 * H])
        real = sb(whole, "real", [P, NT])
        rounds = sb(whole, "rounds", [1, 1], I32)

        B_L0, B_OUT, B_GAMMA, B_BETA, B_M1, B_U1, B_U2, B_LNG, B_LNB, B_M2, B_V = range(11)
        C_PROJ, C_IH, C_HH, C_RZ = 0, 1, 7, 13

        early = whole.enter_context(ExitStack())
        wgt = sb(early, "wgt", [P, NG * GC])
        wt_early = sb(early, "wt_early", [P, W_HEADS * P])

        def W(i, n=1):
            return wt_early[:, i * P:(i + n) * P] if i < W_HEADS else wt_late[:, (i - W_HEADS) * P:(i - W_HEADS + n) * P]

        with ExitStack() as ctx:
            ctx.callback(end_stage)
            ws = sb(ctx, "ws", [P, NW * P])
            wm2 = sb(ctx, "wm2", [P, D])
            srcI = sb(ctx, "srcI", [P, NG * GC], I32)
            typI = sb(ctx, "typI", [P, NG * GC], I32)
            rowI = sb(ctx, "rowI", [P, NG * GC], I32)
            acol = sb(ctx, "acol", [P, 2])
            a_blk = sb(ctx, "a_blk", [P, 2 * H])
            hmask = sb(ctx, "hmask", [P, H])
            h8 = sb(ctx, "h8", [P, H])
            gcol = sb(ctx, "gcol", [ED, 1])
            bm2c = sb(ctx, "bm2c", [P, 1])
            vecs = sb(ctx, "vecs", [P, 2, P])
            wps = ps(ctx, "wps", [P, 2, 512])
            sps = ps(ctx, "sps", [P, 512])
            fill, x_in, edges_in, w_in, small_in, iotas, wtp, wtc, mini, minis, made, chain, rowed = sems(
                "setup", "fill x_in edges_in w_in small_in iotas wtp wtc mini minis made chain rowed")
            with nc.Block() as block:
                w_loads = []

                def wload(slot, ap, n=1, view=None):
                    w_loads.append((slot, ap, n))

                wload(W_PROJ, L1_gnn_node_proj_w)
                for l in range(2):
                    w_loads.append((W_EDGE + 8 * l, L1_gnn_edge_W[l].rearrange("t d h -> d t h"), 8))
                    w_loads.append((W_IH + 3 * l, L1_gnn_gru_wih[l].rearrange("(k d) h -> d k h", k=3), 3))
                    w_loads.append((W_HH + 3 * l, L1_gnn_gru_whh[l].rearrange("(k d) h -> d k h", k=3), 3))
                wload(W_OUT, L1_gnn_out_w)
                wload(W_M1X, L3_gnn_Wm1[:, 0:D])
                wload(W_U1X, L3_gnn_Wu1[:, 0:D])
                wload(W_U1A, L3_gnn_Wu1[:, D:2 * D])
                wload(W_U2, L3_gnn_Wu2)
                half_loads = [
                    (W_M1E * P, L3_gnn_Wm1[:, D:D + ED]), (W_M1E * P + ED, L3_gnn_Wm1[:, D:D + ED]),
                    (W_M1G * P, L3_gnn_Wm1[:, D + ED:D + 2 * ED]), (W_U1G * P, L3_gnn_Wu1[:, 2 * D:2 * D + ED])]
                bias_loads = [L0_gnn_b, L1_gnn_out_b, L2_gnn_ln_gamma, L2_gnn_ln_beta, L3_gnn_bm1, L3_gnn_bu1,
                              L3_gnn_bu2, L3_gnn_ln_g, L3_gnn_ln_b, L3_gnn_bm2]
                col_loads = [(C_PROJ, 1, L1_gnn_node_proj_b.rearrange("(p a) -> p a", a=1))]
                for l in range(2):
                    col_loads.append((C_IH + 3 * l, 3, L1_gnn_gru_bih[l].rearrange("(k p) -> p k", k=3)))
                    col_loads.append((C_HH + 3 * l, 3, L1_gnn_gru_bhh[l].rearrange("(k p) -> p k", k=3)))
                NWL = len(w_loads) + len(half_loads) + 1
                NSL = 4 + len(bias_loads) + len(col_loads)

                @block.sync
                def _(sp):
                    sp.wait_ge(fill, 6)
                    body = E // GE * GE
                    for tile, array in ((dstI, dst), (srcI, src), (typI, edge_type_8), (wgt, edge_weight)):
                        sp.dma_start(tile[:, 0:(NG - 1) * GC].rearrange("p (g c) -> p g c", c=GC),
                                     array[0:body].rearrange("(g p c) -> p g c", p=P, c=GC)).then_inc(edges_in, 16)
                        sp.dma_start(tile[0:PLAST, (NG - 1) * GC:],
                                     array[body:body + PLAST * GC].rearrange("(p c) -> p c", c=GC)).then_inc(edges_in, 16)
                        sp.dma_start(tile[PLAST:PLAST + 1, (NG - 1) * GC:(NG - 1) * GC + CLAST],
                                     array[body + PLAST * GC:E].unsqueeze(0)).then_inc(edges_in, 16)
                    sp.dma_start(X[:, 0:NPAD - P].rearrange("p (t f) -> p t f", f=D),
                                 x[0:NPAD - P, :].rearrange("(t p) f -> p t f", p=P)).then_inc(x_in, 16)
                    sp.dma_start(X[0:NLAST, NPAD - P:], x[NPAD - P:N, :]).then_inc(x_in, 16)
                    for slot, ap, n in w_loads:
                        view = ws[:, slot * P:(slot + n) * P]
                        sp.dma_start(view if n == 1 else view.rearrange("p (n h) -> p n h", n=n), ap).then_inc(w_in, 16)
                    for col, ap in half_loads:
                        sp.dma_start(ws[:, col:col + ED], ap).then_inc(w_in, 16)
                    sp.dma_start(wm2[:], L3_gnn_Wm2).then_inc(w_in, 16)
                    sp.dma_start(w0[:], L0_gnn_W).then_inc(small_in, 16)
                    sp.dma_start(wall[:].rearrange("i (h j) -> i h j", h=H),
                                 L2_gnn_W.rearrange("h i j -> i h j")).then_inc(small_in, 16)
                    for b, ap in enumerate(bias_loads):
                        sp.dma_start(bias[:, b, :], ap.unsqueeze(0).to_broadcast([P, D])).then_inc(small_in, 16)
                    sp.dma_start(gcol[:], L3_gnn_global_state.rearrange("(p a) -> p a", a=1)).then_inc(small_in, 16)
                    sp.dma_start(bm2c[:], L3_gnn_bm2.rearrange("(p a) -> p a", a=1)).then_inc(small_in, 16)
                    with nc.allow_non_contiguous_dma("a few columns of biases"):
                        for col, n, ap in col_loads:
                            sp.dma_start(bcol[:, col:col + n], ap).then_inc(small_in, 16)
                        for t in range(2):
                            for h in range(H):
                                sp.dma_start(acol[h * HD:(h + 1) * HD, t:t + 1],
                                             L2_gnn_a[h, t * HD:(t + 1) * HD, :]).then_inc(small_in, 16)
                    sp.wait_ge(edges_in, 12 * 16)
                    for table, tile in ((dst_d, dstI), (src_d, srcI), (row_d, rowI)):
                        if tile is rowI:
                            sp.wait_ge(rowed, 1)
                        sp.dma_start(table.rearrange("g (p c) -> p g c", c=GC),
                                     tile[:].rearrange("p (g c) -> p g c", c=GC)).then_inc(edges_in, 16)
                    sp.wait_ge(edges_in, 15 * 16)
                    sp.wait_ge(x_in, 32)

                @block.gpsimd
                def _(pool):
                    pool.iota(iota_row[:], [[1, P]], base=0, channel_multiplier=0,
                              allow_small_or_imprecise_dtypes=True).then_inc(iotas, 1)
                    pool.iota(iota_colI[:], [[0, 1]], base=0, channel_multiplier=1).then_inc(iotas, 1)
                    pool.iota(h8[:], [[-HD, H]], base=0, channel_multiplier=1,
                              allow_small_or_imprecise_dtypes=True).then_inc(iotas, 1)
                    pool.memset(X[:, NPAD - P:], 0.0).then_inc(fill, 1)
                    pool.memset(dstI[:, (NG - 1) * GC:], FAR).then_inc(fill, 1)
                    pool.memset(srcI[:, (NG - 1) * GC:], 0).then_inc(fill, 1)
                    pool.memset(typI[:, (NG - 1) * GC:], 0).then_inc(fill, 1)
                    pool.memset(wgt[:, (NG - 1) * GC:], 0.0).then_inc(fill, 1)
                    pool.memset(ws[:], 0.0).then_inc(fill, 1)

                @block.tensor
                def _(pe):
                    pe.wait_ge(w_in, 16 * NWL)
                    pe.wait_ge(made, 1)
                    pe.wait_ge(made, 2)
                    for q in range(NW // 4):
                        if q >= 2:
                            pe.wait_ge(wtc, q - 1)
                        for j in range(4):
                            mm = pe.transpose(wps[:, q % 2, j * P:(j + 1) * P], ws[:, (4 * q + j) * P:(4 * q + j + 1) * P],
                                              ident[:])
                        mm.then_inc(wtp, 1)
                    pe.wait_ge(wtc, NW // 4)
                    pe.wait_ge(made, 3)
                    pe.matmul(sps[:, 0:16], W(W_HEADS), a_blk[:], start=True, stop=True)
                    pe.matmul(sps[:, 128:256], vecs[0:ED, 0, :], W(W_M1G)[0:ED, :], start=True, stop=True)
                    pe.matmul(sps[:, 256:384], vecs[0:ED, 0, :], W(W_U1G)[0:ED, :], start=True, stop=True)
                    pe.matmul(sps[:, 384:512], vecs[:, 1, :], W(W_U1A), start=True, stop=True).then_inc(mini, 1)
                    pe.wait_ge(minis, 1)
                    pe.matmul(sps[:, 0:128], wm2[:], W(W_U1A), start=True, stop=True).then_inc(mini, 1)

                @block.scalar
                def _(act):
                    for q in range(NW // 4):
                        act.wait_ge(wtp, q + 1)
                        for j in range(0, 4, 2):
                            cp = act.copy(W(4 * q + j, 2), wps[:, q % 2, j * P:(j + 2) * P])
                        cp.then_inc(wtc, 1)

                @block.vector
                def _(dve):
                    own = Chain(dve, chain)
                    dve.wait_ge(iotas, 3)
                    own.step(V.tensor_copy(iota_col[:], iota_colI[:]))
                    own.step(V.memset(ones[:], 1.0))
                    V.tensor_tensor(out=ident[:], in0=iota_row[:], in1=iota_col[:].to_broadcast([P, P]),
                                    op=ALU.is_equal).then_inc(made, 1)
                    dve.wait_ge(small_in, 16 * (2 + len(bias_loads) + 2 + len(col_loads) + 2 * H))
                    dve.wait_ge(w_in, 16 * NWL)
                    V.tensor_copy(ws[:, W_HEADS * P:(W_HEADS + 1) * P], wall[:]).then_inc(made, 1)
                    own.step(V.tensor_scalar(hmask[:], h8[:], 0.0, None, ALU.is_ge))
                    own.step(V.tensor_scalar(h8[:], h8[:], float(HD), None, ALU.is_lt))
                    own.step(V.tensor_tensor(out=hmask[:], in0=hmask[:], in1=h8[:], op=ALU.mult))
                    for t in range(2):
                        own.step(V.tensor_scalar(a_blk[:, t * H:(t + 1) * H], hmask[:], acol[:, t:t + 1], None, ALU.mult))
                    own.step(V.tensor_scalar(vecs[0:ED, 0, :], ones[0:ED, :], gcol[:, 0:1], None, ALU.mult))
                    own.step(V.tensor_scalar(vecs[:, 1, :], ones[:], bm2c[:, 0:1], None, ALU.mult))
                    V.tensor_tensor(out=bcol[:, C_RZ:C_RZ + 6], in0=bcol[:, C_IH:C_IH + 6], in1=bcol[:, C_HH:C_HH + 6],
                                    op=ALU.add).then_inc(made, 1)
                    dve.wait_ge(edges_in, 12 * 16)
                    V.scalar_tensor_tensor(out=rowI[:], in0=srcI[:], scalar=float(T), in1=typI[:],
                                           op0=ALU.mult, op1=ALU.add).then_inc(rowed, 1)
                    dve.wait_ge(mini, 1)
                    own.step(V.tensor_copy(wa[:], sps[:, 0:16]))
                    own.step(V.tensor_tensor(out=bias[:, B_M1, :], in0=bias[:, B_M1, :], in1=sps[:, 128:256], op=ALU.add))
                    own.step(V.tensor_tensor(out=bias[:, B_U1, :], in0=bias[:, B_U1, :], in1=sps[:, 256:384], op=ALU.add))
                    own.step(V.tensor_copy(bias[:, B_V, :], sps[:, 384:512]))
                    dve.sem_inc(minis, 1)
                    dve.wait_ge(mini, 2)
                    own.step(V.tensor_copy(wcomb[:], sps[:, 0:128]))

        def turn_tiles(pe, out_ps, in_sb):
            for t in range(TC):
                mm = pe.transpose(out_ps[:, t * P:(t + 1) * P], in_sb[:, t * P:(t + 1) * P], ident[:])
            return mm

        def times(pe, out_ps, tiles_sb, w, width=D):
            for t in range(TC):
                mm = pe.matmul(out_ps[:, t * width:(t + 1) * width], tiles_sb[:, t * P:(t + 1) * P], w, start=True, stop=True)
            return mm

        def norm(dve, own, r, sq, st, var_ready, rooted, turn, n, k):
            r3, q3 = r.rearrange("p (t f) -> p t f", f=D), sq.rearrange("p (t f) -> p t f", f=D)
            own.step(V.tensor_reduce(st[:, 0:TC], r3, AX, ALU.add))
            own.step(V.tensor_scalar(st[:, 0:TC], st[:, 0:TC], 1.0 / D, None, ALU.mult))
            own.step(V.tensor_tensor(out=r3, in0=r3, in1=over(st[:, 0:TC], D), op=ALU.subtract))
            own.step(V.tensor_tensor(out=q3, in0=r3, in1=r3, op=ALU.mult))
            own.step(V.tensor_reduce(st[:, TC:2 * TC], q3, AX, ALU.add))
            V.tensor_scalar(st[:, TC:2 * TC], st[:, TC:2 * TC], 1.0 / D, EPS, ALU.mult, ALU.add).then_inc(var_ready, 1)
            dve.wait_ge(rooted, turn * n + (k + 1))
            own.step(V.reciprocal(st[:, TC:2 * TC], st[:, TC:2 * TC]))
            own.step(V.tensor_tensor(out=r3, in0=r3, in1=over(st[:, TC:2 * TC], D), op=ALU.mult))

        NORM_STEPS = 7

        def root(act, st, var_ready, rooted, turn, n, k):
            act.wait_ge(var_ready, turn * n + (k + 1))
            act.activation(st[:, TC:2 * TC], st[:, TC:2 * TC], ACT.Sqrt).then_inc(rooted, 1)

        def tiles3(ap):
            return ap.rearrange("p (t f) -> p t f", f=D)

        parts = whole.enter_context(ExitStack())
        w4 = sb(parts, "w4", [P, NG * GC, 4], BF16)
        with ExitStack() as ctx:
            ctx.callback(end_stage)
            dstF = sb(ctx, "dstF", [P, NG * GC])
            near = sb(ctx, "near", [P, NG * GC])
            mm_ = sb(ctx, "mm_", [P, 2, P])
            gm = sb(ctx, "gm", [P, 8])
            nwI = sb(ctx, "nwI", [P, 1], I32)
            upto = sb(ctx, "upto", [P, P])
            kk = sb(ctx, "kk", [P, KCAP])
            sel = sb(ctx, "sel", [P, KCAP])
            vals = sb(ctx, "vals", [P, 4])
            kcol = sb(ctx, "kcol", [P, KT])
            it = sb(ctx, "it", [P, KT, 4])
            itI = sb(ctx, "itI", [P, KT, 4], I32)
            kf = sb(ctx, "kf", [P, KCAP // SL + 1])
            before = sb(ctx, "before", [P, 3, NCH, KT])
            last = sb(ctx, "last", [P, P])
            tt = sb(ctx, "tt", [P, 3])
            ttI = sb(ctx, "ttI", [P, 1], I32)
            tps = ps(ctx, "tps", [P, 2, P])
            cps = ps(ctx, "cps", [P, 8])
            lps = ps(ctx, "lps", [P, P])
            ips = ps(ctx, "ips", [P, KT, 4])
            iotas, mins, turned, nwin, cums, sels, itp, table, stored, chain, lastm, lastt, tcol, trow = sems(
                "items", "iotas mins turned nwin cums sels itp table stored chain lastm lastt tcol trow")
            xs = acc[:, 0:2 * CW].rearrange("p (a n) -> p a n", a=2)
            xT = acc[:, 2 * CW:4 * CW].rearrange("p (a n) -> p a n", a=2)
            wr = acc[:, 4 * CW:4 * CW + NG * GC]
            xp = ps(ctx, "xp", [P, CW])
            hp = ps(ctx, "hp", [P, CW])
            staged, xturned, xcopied, product, taken, split = sems("h", "staged xturned xcopied product taken split")
            with nc.Block() as block:
                @block.gpsimd
                def _(pool):
                    pool.iota(kk[:], [[1, KCAP]], base=0, channel_multiplier=0,
                              allow_small_or_imprecise_dtypes=True).then_inc(iotas, 1)
                    pool.iota(kcol[:], [[P, KT]], base=0, channel_multiplier=1,
                              allow_small_or_imprecise_dtypes=True).then_inc(iotas, 1)
                    pool.iota(kf[:], [[SL, KCAP // SL + 1]], base=0, channel_multiplier=0,
                              allow_small_or_imprecise_dtypes=True).then_inc(iotas, 1)
                    own = Chain(pool, split)
                    own.step(nc.gpsimd.memset(w4[:], 1.0))
                    own.step(nc.gpsimd.tensor_copy(w4[:, :, 0], wgt[:]))
                    own.step(nc.gpsimd.tensor_tensor(out=wr, in0=wgt[:], in1=w4[:, :, 0], op=ALU.subtract))
                    own.step(nc.gpsimd.tensor_copy(w4[:, :, 1], wr))
                    own.step(nc.gpsimd.tensor_tensor(out=wr, in0=wr, in1=w4[:, :, 1], op=ALU.subtract))
                    own.step(nc.gpsimd.tensor_copy(w4[:, :, 2], wr))

                @block.scalar
                def _(act):
                    for c in range(2):
                        act.copy(xs[:, c], X[:, c * CW:(c + 1) * CW]).then_inc(staged, 1)
                    for c in range(NCH):
                        act.wait_ge(xturned, c + 1)
                        act.copy(xT[:, c % 2], xp[:]).then_inc(xcopied, 1)
                        if c + 2 < NCH:
                            act.copy(xs[:, c % 2], X[:, (c + 2) * CW:(c + 3) * CW]).then_inc(staged, 1)
                        act.wait_ge(product, c + 1)
                        act.copy(HB[:, c * CW:(c + 1) * CW], hp[:]).then_inc(taken, 1)

                @block.vector
                def _(dve):
                    own = Chain(dve, chain)
                    own.step(V.tensor_copy(dstF[:], dstI[:]))
                    own.step(V.memset(mm_[:], 0.0))
                    own.step(V.tensor_reduce(mm_[:, 0, 0:NG], dstF[:].rearrange("p (g c) -> p g c", c=GC), AX, ALU.min))
                    own.step(V.tensor_scalar(near[:], dstF[:], float(N), None, ALU.is_lt))
                    own.step(V.tensor_tensor(out=near[:], in0=near[:], in1=dstF[:], op=ALU.mult))
                    V.tensor_reduce(mm_[:, 1, 0:NG], near[:].rearrange("p (g c) -> p g c", c=GC), AX,
                                    ALU.max).then_inc(mins, 1)
                    dve.wait_ge(turned, 1)
                    own.step(V.tensor_reduce(gm[0:NG, 0:1], tps[0:NG, 0, :], AX, ALU.min))
                    own.step(V.tensor_reduce(gm[0:NG, 1:2], tps[0:NG, 1, :], AX, ALU.max))
                    own.step(V.tensor_tensor(out=nwI[0:NG], in0=gm[0:NG, 1:2], in1=gm[0:NG, 0:1], op=ALU.subtract))
                    own.step(V.tensor_single_scalar(nwI[0:NG], nwI[0:NG], 7, op=ALU.arith_shift_right))
                    own.step(V.tensor_scalar(gm[0:NG, 2:3], nwI[0:NG], 1.0, None, ALU.add))
                    own.step(V.tensor_tensor(out=upto[:], in0=iota_row[:], in1=iota_col[:].to_broadcast([P, P]), op=ALU.is_ge))
                    dve.sem_inc(nwin, 1)
                    dve.wait_ge(cums, 1)
                    own.step(V.tensor_copy(gm[0:NG, 3:4], cps[0:NG, 0:1]))
                    own.step(V.tensor_tensor(out=gm[0:NG, 4:5], in0=gm[0:NG, 3:4], in1=gm[0:NG, 2:3], op=ALU.subtract))
                    own.step(V.scalar_tensor_tensor(out=vals[0:NG, 0:1], in0=gm[0:NG, 4:5], scalar=-float(P),
                                                    in1=gm[0:NG, 0:1], op0=ALU.mult, op1=ALU.add))
                    own.step(V.tensor_copy(vals[0:NG, 1:2], iota_col[0:NG]))
                    own.step(V.memset(vals[0:NG, 2:4], 1.0))
                    dve.wait_ge(iotas, 3)
                    own.step(V.tensor_scalar(sel[0:NG], kk[0:NG], gm[0:NG, 3:4], None, ALU.is_lt))
                    V.scalar_tensor_tensor(out=sel[0:NG], in0=kk[0:NG], scalar=gm[0:NG, 4:5], in1=sel[0:NG],
                                           op0=ALU.is_ge, op1=ALU.mult).then_inc(sels, 1)
                    dve.wait_ge(itp, 1)
                    own.step(V.tensor_copy(it[:], ips[:]))
                    own.step(V.scalar_tensor_tensor(out=it[:, :, 0], in0=kcol[:], scalar=float(P), in1=it[:, :, 0],
                                                    op0=ALU.mult, op1=ALU.add))
                    own.step(V.tensor_scalar(it[:, :, 3], it[:, :, 2], -NOBASE, NOBASE, ALU.mult, ALU.add))
                    own.step(V.tensor_tensor(out=itI[:, :, 0], in0=it[:, :, 0], in1=it[:, :, 3], op=ALU.add))
                    own.step(V.tensor_tensor(out=itI[:, :, 1], in0=it[:, :, 0], in1=it[:, :, 2], op=ALU.mult))
                    own.step(V.tensor_copy(itI[:, :, 2:4], it[:, :, 1:3]))
                    dve.sem_inc(table, 1)
                    own.step(V.tensor_scalar(before[:, 1, 0, :], kcol[:], 1.0, None, ALU.add))
                    own.step(V.tensor_tensor(out=before[:, 1, 0, :], in0=before[:, 1, 0, :], in1=it[:, :, 2], op=ALU.mult))
                    own.step(V.memset(last[:], 0.0))
                    for c in range(NCH):
                        own.step(V.scalar_tensor_tensor(out=before[:, 0, c, :], in0=it[:, :, 0], scalar=float(CW * (c + 1)),
                                                        in1=before[:, 1, 0, :], op0=ALU.is_lt, op1=ALU.mult))
                    own.step(V.tensor_reduce(last[:, 0:NCH], before[:, 0], AX, ALU.max))
                    dve.sem_inc(lastm, 1)
                    dve.wait_ge(lastt, 1)
                    own.step(V.tensor_reduce(tt[0:NCH, 0:1], lps[0:NCH, :], AX, ALU.max))
                    own.step(V.tensor_scalar(kf[0:NCH], kf[0:NCH], tt[0:NCH, 0:1], None, ALU.is_lt))
                    own.step(V.tensor_reduce(tt[0:NCH, 1:2], kf[0:NCH], AX, ALU.add))
                    own.step(V.tensor_scalar(ttI[0:NCH], tt[0:NCH, 1:2], 1.0, None, ALU.add))
                    own.step(V.tensor_single_scalar(ttI[0:NCH], ttI[0:NCH], 1, op=ALU.arith_shift_right))
                    own.step(V.tensor_copy(tt[0:NCH, 2:3], ttI[0:NCH]))
                    dve.sem_inc(tcol, 1)
                    dve.wait_ge(trow, 1)
                    own.step(V.memset(turns_to[:], 0))
                    own.step(V.tensor_copy(turns_to[:, 1:NCH + 1], lps[0:1, 0:NCH]))
                    own.step(V.tensor_copy(turns_to[:, NCH + 2:], lps[0:1, NCH:2 * NCH]))

                @block.tensor
                def _(pe):
                    def x_times_w(c0, c1):
                        for c in range(c0, c1):
                            pe.wait_ge(staged, c + 1)
                            if c >= 1:
                                pe.wait_ge(xcopied, c)
                            turn_tiles(pe, xp, xs[:, c % 2]).then_inc(xturned, 1)
                            pe.wait_ge(xcopied, c + 1)
                            if c >= 1:
                                pe.wait_ge(taken, c)
                            times(pe, hp, xT[:, c % 2], w0[:]).then_inc(product, 1)

                    x_times_w(0, 1)
                    pe.wait_ge(mins, 1)
                    pe.transpose(tps[:, 0, :], mm_[:, 0, :], ident[:])
                    pe.transpose(tps[:, 1, :], mm_[:, 1, :], ident[:]).then_inc(turned, 1)
                    pe.wait_ge(nwin, 1)
                    pe.matmul(cps[0:NG, 0:1], upto[0:NG, 0:NG], gm[0:NG, 2:3], start=True, stop=True).then_inc(cums, 1)
                    x_times_w(1, 3)
                    pe.wait_ge(sels, 1)
                    for k in range(KT):
                        mm = pe.matmul(ips[:, k, :], sel[0:NG, k * P:(k + 1) * P], vals[0:NG, :], start=True, stop=True)
                    mm.then_inc(itp, 1)
                    x_times_w(3, 4)
                    pe.wait_ge(lastm, 1)
                    pe.transpose(lps[:], last[:], ident[:]).then_inc(lastt, 1)
                    pe.wait_ge(tcol, 1)
                    pe.transpose(lps[0:1, 0:NCH], tt[0:NCH, 1:2], ident[0:NCH, 0:NCH])
                    pe.transpose(lps[0:1, NCH:2 * NCH], tt[0:NCH, 2:3], ident[0:NCH, 0:NCH]).then_inc(trow, 1)
                    x_times_w(4, NCH)

                @block.sync
                def _(sp):
                    sp.wait_ge(table, 1)
                    sp.dma_start(items_d.rearrange("(k p) c -> p k c", p=P), itI[:]).then_inc(stored, 16)
                    sp.wait_ge(stored, 16)

        with ExitStack() as ctx:
            ctx.callback(end_stage)
            iota_gc = sb(ctx, "iota_gc", [P, P, GC], BF16)
            at = sb(ctx, "deg_at", [P, SL, GC], BF16)
            OH = sb(ctx, "deg_OH", [P, 2, P, GC], BF16)
            dg = sb(ctx, "deg_dg", [P, SL, GC], I32)
            wg = sb(ctx, "wg", [P, SL, GC, 4], BF16)
            itm = sb(ctx, "deg_itm", [P, SL, 4], I32)
            zero = sb(ctx, "zero", [P, P], BF16)
            dps = [ps(ctx, f"dps{b}", [4, P]) for b in range(2)]
            tps = ps(ctx, "deg_tps", [P, NT, 4])
            item_ready = sems("deg", " ".join(f"item_ready{s}" for s in range(SL)))
            taken, placed, hot, product, done, chain, zeroed, turned, dsq, rooted, final, scaled, stored, late = sems(
                "deg", "taken placed hot product done chain zeroed turned dsq rooted final scaled stored late")
            with nc.Block() as block:
                @block.sync
                def _(sp):
                    n = sp.value_load(turns_to[0:1, NCH:NCH + 1], min_val=1, max_val=KCAP // SL)
                    sp.wait_ge(zeroed, 1)
                    with sp.Fori(0, n) as i:
                        for s in range(SL):
                            k = i * SL + s
                            sp.wait_ge(done, k + 1)
                            sp.dma_start(itm[:, s, :], items_d[ds(k, 1), :].to_broadcast([P, 4])
                                         ).then_inc(item_ready[s], 16)
                    for c in range(NCH):
                        sp.wait_ge(scaled, c + 1)
                        sp.dma_start(gcn_d[c * CW:(c + 1) * CW].rearrange("(t p) f -> p t f", p=P),
                                     tiles3(HB[:, c * CW:(c + 1) * CW])).then_inc(stored, 16)
                    sp.wait_ge(stored, NCH * 16)

                @block.vector
                def _(dve):
                    own = Chain(dve, chain)
                    own.step(V.memset(itm[:], 0))
                    own.step(V.memset(acc[0:4, :], 0.0))
                    V.memset(zero[:], 0.0).then_inc(zeroed, 1)
                    own.step(V.tensor_copy(iota_gc[:], over(iota_row[:], GC)))
                    dve.sem_inc(done, SL - 1)

                    def add_item(k, s):
                        col = dve.value_load(itm[0:1, s, 1:2], min_val=0, max_val=N - 1)
                        dve.wait_ge(product, k + 1)
                        dve.wait_ge(done, k + SL - 1)
                        passed(dve, tick)
                        V.tensor_tensor(out=acc[0:4, ds(col, P)], in0=acc[0:4, ds(col, P)], in1=dps[s % 2][:],
                                        op=ALU.add).then_inc(done, 1)

                    n = dve.value_load(turns_to[0:1, NCH:NCH + 1], min_val=1, max_val=KCAP // SL)
                    with dve.Fori(0, n) as i:
                        for s in range(SL):
                            k = i * SL + s
                            dve.wait_ge(placed, k + 1)
                            V.tensor_tensor(out=OH[:, s % 2], in0=rows(at[:, s], P), in1=iota_gc[:],
                                            op=ALU.is_equal).then_inc(hot, 1)
                            add_item(k, (s - 1) % SL)
                    add_item(n * SL, SL - 1)
                    dve.wait_ge(done, n * SL + SL)
                    dve.sem_inc(final, 1)
                    own = Chain(dve, late)
                    dve.wait_ge(turned, 1)
                    own.step(V.tensor_reduce(deg[:, 0, :], tps[:, :, 0:3], AX, ALU.add))
                    own.step(V.tensor_scalar(deg[:, 0, :], deg[:, 0, :], 1.0, None, ALU.add))
                    own.step(V.tensor_copy(deg[:, 1, :], tps[:, :, 3]))
                    own.step(V.tensor_scalar(dinv[:], deg[:, 0, :], 1e-30, None, ALU.max))
                    own.step(V.reciprocal(dinv[:], dinv[:]))
                    dve.sem_inc(dsq, 1)
                    dve.wait_ge(rooted, 1)
                    own.step(V.scalar_tensor_tensor(out=dinv[:], in0=deg[:, 0, :], scalar=0.0, in1=dinv[:],
                                                    op0=ALU.is_gt, op1=ALU.mult))
                    for c in range(NCH):
                        hb = tiles3(HB[:, c * CW:(c + 1) * CW])
                        V.tensor_tensor(out=hb, in0=hb, in1=over(dinv[:, c * TC:(c + 1) * TC], D),
                                        op=ALU.mult).then_inc(scaled, 1)
                    own.step(V.tensor_scalar(cntinv[:], deg[:, 1, :], 1.0, None, ALU.max))
                    own.step(V.reciprocal(cntinv[:], cntinv[:]))
                    own.step(V.tensor_scalar(has[:], deg[:, 1, :], 0.0, None, ALU.is_gt))

                @block.gpsimd
                def _(pool):
                    n = pool.value_load(turns_to[0:1, NCH:NCH + 1], min_val=1, max_val=KCAP // SL)
                    with pool.Fori(0, n) as i:
                        for s in range(SL):
                            pool.wait_ge(item_ready[s], i * 16 + 16)
                            passed(pool, tick)
                            g = pool.value_load(itm[0:1, s, 2:3], min_val=0, max_val=NG - 1)
                            nc.gpsimd.tensor_copy(wg[:, s], w4[:, ds(g * GC, GC), :])
                            nc.gpsimd.tensor_copy(dg[:, s], dstI[:, ds(g * GC, GC)]).then_inc(taken, 1)
                            pool.wait_ge(taken, i * SL + s + 1)
                            passed(pool, tick)
                            nc.gpsimd.tensor_scalar(at[:, s], dg[:, s], itm[:, s, 0:1], None,
                                                    ALU.subtract).then_inc(placed, 1)

                @block.scalar
                def _(act):
                    act.wait_ge(dsq, 1)
                    act.activation(dinv[:], dinv[:], ACT.Sqrt).then_inc(rooted, 1)

                @block.tensor
                def _(pe):
                    pe.wait_ge(zeroed, 1)
                    pe.matmul(dps[(SL - 1) % 2][:], zero[:, 0:4], zero[:], start=True, stop=True).then_inc(product, 1)
                    n = pe.value_load(turns_to[0:1, NCH:NCH + 1], min_val=1, max_val=KCAP // SL)
                    with pe.Fori(0, n) as i:
                        for s in range(SL):
                            k = i * SL + s
                            pe.wait_ge(hot, k + 1)
                            pe.wait_ge(done, k + SL - 1)
                            for c in range(GC):
                                mm = pe.matmul(dps[s % 2][:], wg[:, s, c, :], OH[:, s % 2, :, c], start=c == 0,
                                               stop=c == GC - 1)
                            mm.then_inc(product, 1)
                    pe.wait_ge(final, 1)
                    for t in range(NT):
                        mm = pe.transpose(tps[:, t, :], acc[0:4, t * P:(t + 1) * P], ident[0:4, 0:4])
                    mm.then_inc(turned, 1)
        parts.close()

        def turns(eng, to, c, body):
            t0 = eng.value_load(to[0:1, ds(c, 1)], min_val=0, max_val=KCAP // SL)
            t1 = eng.value_load(to[0:1, ds(c + 1, 1)], min_val=0, max_val=KCAP // SL)
            with eng.If(t0 < t1):
                with eng.Fori(t0, t1) as i:
                    body(i)

        def aggregate(name, table, index, stage, weighted=False, ex=None, attr=False, sl=SL):
            to = turns_to[:, (sl // SL - 1) * (NCH + 1):(sl // SL) * (NCH + 1)]
            with ExitStack() as ctx:
                ctx.callback(end_stage)
                G = sb(ctx, f"{name}_G", [P, sl, GC, D])
                OH = sb(ctx, f"{name}_OH", [P, 2, GC, P])
                idx = sb(ctx, f"{name}_idx", [P, sl, GC], I32)
                itm = sb(ctx, f"{name}_itm", [P, sl, 4], I32)
                PS = ps(ctx, f"{name}_PS", [P, 8, 512])
                wp = [PS[:, 6, 0:P], PS[:, 7, 0:P]]
                OHf = OH[:].rearrange("p a c n -> p (a c n)")
                buf = [OHf[:, k * CW:(k + 1) * CW] for k in range(4)]
                st = sb(ctx, f"{name}_st", [P, 2 * TC])
                gathered = sems(name, " ".join(f"gathered{s}" for s in range(sl)))
                idx_ready = sems(name, " ".join(f"idx_ready{s}" for s in range(sl)))
                item_ready, added, product, oh_ready, chain, rows_ready, acc_ready, done = sems(
                    name, "item_ready added product oh_ready chain rows_ready acc_ready done")
                if attr:
                    at_ = sb(ctx, f"{name}_at", [P, sl, GC, ED])
                    atT = sb(ctx, f"{name}_atT", [P, GC // 2, P])
                    tp = PS[:, 0:2].rearrange("p a n -> p (a n)")[:, 0:GC // 2 * P].rearrange("p (q n) -> p q n", n=P)
                    ep = [PS[:, 2 + 2 * a:4 + 2 * a].rearrange("p a n -> p (a n)")[:, 0:GC // 2 * P].rearrange(
                        "p (q n) -> p q n", n=P) for a in range(2)]
                    attr_in = sems(name, " ".join(f"attr_in{s}" for s in range(sl)))
                    turned, copied, ep_ready, summed, at_zeroed = sems(
                        name, "at_turned at_copied ep_ready summed at_zeroed")
                    full = (NG - 1) * GE
                    at_rows = edge_attr_64[0:full, :].rearrange("(g p c) f -> g p (c f)", p=P, c=GC)
                    at_last = edge_attr_64[full:full + PLAST * GC, :].rearrange("(p c) f -> p (c f)", c=GC)
                    at_rest = edge_attr_64[full + PLAST * GC:E, :].rearrange("(p c) f -> p (c f)", c=CLAST)
                run = stage(ctx, name, PS, buf, st, acc_ready, done)
                with nc.Block() as block:
                    @block.sync
                    def _(sp):
                        n = sp.value_load(to[0:1, NCH:NCH + 1], min_val=1, max_val=KCAP // sl)
                        with sp.Fori(0, n) as i:
                            for s in range(sl):
                                k = i * sl + s
                                sp.wait_ge(added, k + 1)
                                sp.dma_start(itm[:, s, :], items_d[ds(k, 1), :].to_broadcast([P, 4])
                                             ).then_inc(item_ready, 16)
                                sp.wait_ge(item_ready, k * 16 + 16)
                                passed(sp, tick)
                                g = sp.value_load(itm[0:1, s, 2:3], min_val=0, max_val=NG - 1)
                                sp.dma_start(idx[:, s, :], index[ds(g, 1), :].rearrange("a (p c) -> (a p) c", c=GC)
                                             ).then_inc(idx_ready[s], 16)
                                if attr:
                                    sp.wait_ge(at_zeroed, 1)
                                    with sp.If(g < NG - 1):
                                        g = sp.value_load(itm[0:1, s, 2:3], min_val=0, max_val=NG - 2)
                                        sp.dma_start(at_[:, s].rearrange("p c f -> p (c f)"),
                                                     at_rows[ds(g, 1)].rearrange("a p f -> (a p) f")).then_inc(attr_in[s], 32)
                                    with sp.Else():
                                        at = at_[:, s].rearrange("p c f -> p (c f)")
                                        sp.dma_start(at[0:PLAST], at_last).then_inc(attr_in[s], 16)
                                        sp.dma_start(at[PLAST:PLAST + 1, 0:CLAST * ED], at_rest).then_inc(attr_in[s], 16)
                        run.sync(sp)

                    @block.scalar
                    def _(act):
                        def items(i):
                            def attr_copy(s):
                                act.wait_ge(turned, i * sl + s + 1)
                                act.copy(atT[:], tp).then_inc(copied, 1)

                            attr_copy(0)
                            attr_copy(1)
                            for s in range(sl):
                                act.wait_ge(summed, i * sl + s + 1)
                                act.activation(G[:, s], G[:, s], ACT.Relu).then_inc(rows_ready, 1)
                                if s + 2 < sl:
                                    attr_copy(s + 2)

                        run.before(act)
                        with act.Fori(0, NCH) as c:
                            if attr:
                                turns(act, to, c, items)
                            run.scalar(act, c)

                    @block.gpsimd
                    def _(pool):
                        n = pool.value_load(to[0:1, NCH:NCH + 1], min_val=1, max_val=KCAP // sl)
                        with pool.Fori(0, n) as i:
                            for s in range(sl):
                                pool.wait_ge(idx_ready[s], i * 16 + 16)
                                passed(pool, tick)
                                for c in range(GC):
                                    pool.indirect_dma_start(
                                        G[:, s, c, :], None, table,
                                        bass.IndirectOffsetOnAxis(ap=idx[:, s, c:c + 1].bitcast(U32), axis=0)
                                    ).then_inc(gathered[s], 16)

                    @block.vector
                    def _(dve):
                        dve.sem_inc(added, sl)
                        if attr:
                            V.memset(at_[:], 0.0).then_inc(at_zeroed, 1)
                        V.memset(acc[:], 0.0).then_inc(chain, 1)
                        first = 1
                        dve.wait_ge(chain, first)

                        def items(i):
                            own = Chain(dve, chain)
                            own.base = i * sl + first
                            g = [None] * sl

                            def one_hot(s):
                                dve.wait_ge(item_ready, (i * sl + s) * 16 + 16)
                                passed(dve, tick)
                                g[s] = dve.value_load(itm[0:1, s, 2:3], min_val=0, max_val=NG - 1)
                                oh = V.scalar_tensor_tensor(
                                    out=OH[:, s % 2], in0=over(dstI[:, ds(g[s] * GC, GC)], P), scalar=itm[:, s, 0:1],
                                    in1=rows(iota_row[:], GC), op0=ALU.subtract, op1=ALU.is_equal)
                                if weighted:
                                    own.step(oh)
                                    oh = V.tensor_tensor(out=OH[:, s % 2], in0=OH[:, s % 2],
                                                         in1=over(wgt[:, ds(g[s] * GC, GC)], P), op=ALU.mult)
                                oh.then_inc(oh_ready, 1)

                            def own_part(s):
                                if ex is not None:
                                    dve.wait_ge(gathered[s], i * 16 * GC + 16 * GC)
                                    V.tensor_tensor(out=G[:, s].rearrange("p c (h j) -> p (c h) j", h=H),
                                                    in0=G[:, s].rearrange("p c (h j) -> p (c h) j", h=H),
                                                    in1=over(ex[:, ds(g[s] * GC * H, GC * H)], HD),
                                                    op=ALU.mult).then_inc(rows_ready, 1)
                                if attr:
                                    dve.wait_ge(gathered[s], i * 16 * GC + 16 * GC)
                                    dve.wait_ge(ep_ready, i * sl + s + 1)
                                    for a in range(2):
                                        ga = G[:, s].rearrange("p (q a) f -> p q a f", a=2)[:, :, a, :]
                                        last = V.tensor_tensor(out=ga, in0=ga, in1=ep[a], op=ALU.add)
                                    last.then_inc(summed, 1)

                            one_hot(0)
                            own_part(0)
                            for s in range(sl):
                                k = i * sl + s
                                if s + 1 < sl:
                                    one_hot(s + 1)
                                    own_part(s + 1)
                                col = dve.value_load(itm[0:1, s, 1:2], min_val=0, max_val=N - 1)
                                dve.wait_ge(product, k + 1)
                                dve.wait_ge(added, k + sl)
                                V.tensor_tensor(out=acc[:, ds(col, P)], in0=acc[:, ds(col, P)], in1=wp[s % 2],
                                                op=ALU.add).then_inc(added, 1)

                        with dve.Fori(0, NCH) as c:
                            turns(dve, to, c, items)
                            t1 = dve.value_load(to[0:1, ds(c + 1, 1)], min_val=0, max_val=KCAP // sl)
                            dve.wait_ge(added, t1 * sl + sl)
                            dve.sem_inc(acc_ready, 1)
                            run.vector(dve, c)
                            dve.wait_ge(done, c + 1)

                    @block.tensor
                    def _(pe):
                        def items(i):
                            def attr_turn(s):
                                pe.wait_ge(attr_in[s], i * 32 + 32)
                                for c in range(GC // 2):
                                    mm = pe.transpose(tp[:, c, :], at_[:, s, 2 * c:2 * c + 2].rearrange("p a f -> p (a f)"),
                                                      ident[:])
                                mm.then_inc(turned, 1)

                            def attr_product(s):
                                pe.wait_ge(copied, i * sl + s + 1)
                                for c in range(GC):
                                    h = c % 2 * ED
                                    mm = pe.matmul(ep[c % 2][:, c // 2, :], atT[h:h + ED, c // 2, :],
                                                   W(W_M1E)[h:h + ED, :], start=True, stop=True)
                                mm.then_inc(ep_ready, 1)

                            if attr:
                                attr_turn(0)
                                attr_product(0)
                                attr_turn(1)
                            for s in range(sl):
                                k = i * sl + s
                                if attr and s + 1 < sl:
                                    pe.wait_ge(summed, k + 1)
                                    attr_product(s + 1)
                                    if s + 2 < sl:
                                        attr_turn(s + 2)
                                pe.wait_ge(gathered[s], i * 16 * GC + 16 * GC)
                                pe.wait_ge(oh_ready, k + 1)
                                if ex is not None or attr:
                                    pe.wait_ge(rows_ready, k + 1)
                                pe.wait_ge(added, k + sl - 1)
                                for c in range(GC):
                                    mm = pe.matmul(wp[s % 2], G[:, s, c, :], OH[:, s % 2, c, :], start=c == 0, stop=c == GC - 1)
                                mm.then_inc(product, 1)

                        with pe.Fori(0, NCH) as c:
                            turns(pe, to, c, items)
                            pe.wait_ge(acc_ready, c + 1)
                            run.tensor(pe, c)
                            pe.wait_ge(done, c + 1)

        class Stage:

            def before(self, act):
                pass

            def sync(self, sp):
                pass

        def banks(PS, b, n=CW):
            return PS[:, b:b + 2].rearrange("p a n -> p (a n)")[:, 0:n]

        HW_ = CW // 2

        def transformer(ctx, name, l, PS, hs):
            tb = sb(ctx, f"{name}_tb", [P, 2, T * D])
            pp = [PS[:, 2 * s:2 * s + 2] for s in range(2)]
            tprod, = sems(name, "tprod")
            copied = sems(name, "tcopied0 tcopied1")
            stored = sems(name, "stored0 stored1")
            per = [TC - TC // 2, TC // 2]
            rows_d = trans_d[l].rearrange("(t p) f -> t p f", p=P)

            class Transformer:
                def before(self, act):
                    for s in range(2):
                        act.sem_inc(copied[s], 1)
                        act.sem_inc(stored[s], 16)

                def tensor(self, pe, c):
                    for t in range(TC):
                        s = t % 2
                        pe.wait_ge(copied[s], c * per[s] + t // 2 + 1)
                        for a in range(2):
                            mm = pe.matmul(pp[s][:, a, :], hs[:, t * P:(t + 1) * P], W(W_EDGE + 8 * l + 4 * a, 4),
                                           start=True, stop=True)
                        mm.then_inc(tprod, 1)

                def tile(self, eng, c, t, copy):
                    s = t % 2
                    eng.wait_ge(tprod, c * TC + t + 1)
                    eng.wait_ge(stored[s], (c * per[s] + t // 2 + 1) * 16)
                    copy(tb[:, s, :], pp[s].rearrange("p a f -> p (a f)")).then_inc(copied[s], 1)

                def vector(self, dve, c):
                    for t in range(1, TC, 2):
                        self.tile(dve, c, t, V.tensor_copy)

                def scalar(self, act, c):
                    for t in range(TC):
                        s = t % 2
                        if s == 0:
                            self.tile(act, c, t, act.copy)
                        act.wait_ge(copied[s], c * per[s] + t // 2 + 2)
                        act.dma_start(rows_d[ds(c * TC + t, 1)].rearrange("a p f -> (a p) f"), tb[:, s, :]
                                      ).then_inc(stored[s], 16)

                def sync(self, sp):
                    for s in range(2):
                        sp.wait_ge(stored[s], (NCH * per[s] + 1) * 16)

            return Transformer()

        def gcn_end(ctx, name, PS, buf, st, acc_ready, done):
            st_, r, sq, xT = buf
            hs = sq
            ap_, tp, hp = banks(PS, 0), banks(PS, 2), PS[:, 4:6, 0:HW_]
            staged, turned, nchain, var_ready, rooted, normed, xturned, xcopied, hprod, hready, kept = sems(
                name, "staged turned nchain var_ready rooted normed xturned xcopied hprod hready kept")
            table = transformer(ctx, name, 0, PS, hs)

            class GcnEnd(Stage):
                before, sync = table.before, table.sync

                def scalar(self, act, c):
                    act.wait_ge(acc_ready, c + 1)
                    act.copy(st_, acc[:, ds(c * CW, CW)]).then_inc(staged, 1)
                    root(act, st, var_ready, rooted, c, 1, 0)
                    act.wait_ge(xturned, c + 1)
                    act.copy(xT, tp).then_inc(xcopied, 1)
                    act.wait_ge(hprod, c + 1)
                    act.activation(hs.rearrange("p (a n) -> p a n", a=2), hp, ACT.Relu,
                                   bias=bcol[:, C_PROJ:C_PROJ + 1]).then_inc(hready, 1)
                    table.scalar(act, c)
                    act.wait_ge(kept, c + 1)
                    act.sem_inc(done, 1)

                def tensor(self, pe, c):
                    pe.wait_ge(staged, c + 1)
                    turn_tiles(pe, ap_, st_).then_inc(turned, 1)
                    pe.wait_ge(normed, c + 1)
                    turn_tiles(pe, tp, r).then_inc(xturned, 1)
                    pe.wait_ge(xcopied, c + 1)
                    for a in range(2):
                        mm = pe.matmul(hp[:, a, :], W(W_PROJ), xT[:, a * HW_:(a + 1) * HW_], start=True, stop=True)
                    mm.then_inc(hprod, 1)
                    pe.wait_ge(hready, c + 1)
                    table.tensor(pe, c)

                def vector(self, dve, c):
                    own = Chain(dve, nchain, 4 + NORM_STEPS, c)
                    at, r3 = ds(c * CW, CW), tiles3(r)
                    dve.wait_ge(turned, c + 1)
                    own.step(V.tensor_tensor(out=r, in0=HB[:, at], in1=ap_, op=ALU.add))
                    own.step(V.tensor_tensor(out=r3, in0=r3, in1=over(dinv[:, ds(c * TC, TC)], D), op=ALU.mult))
                    own.step(V.tensor_tensor(out=r3, in0=r3, in1=rows(bias[:, B_L0, :], TC), op=ALU.add))
                    own.step(V.tensor_tensor(out=r, in0=r, in1=X[:, at], op=ALU.add))
                    norm(dve, own, r, sq, st, var_ready, rooted, c, 1, 0)
                    dve.sem_inc(normed, 1)
                    passed(dve, tick)
                    V.tensor_copy(X[:, at], r)
                    dve.wait_ge(hready, c + 1)
                    passed(dve, tick)
                    V.tensor_copy(HB[:, at], hs).then_inc(kept, 1)
                    table.vector(dve, c)
                    assert own.n == 4 + NORM_STEPS, own.n

            return GcnEnd()

        def gru_parts(name, l, PS, buf):
            rg, zg, ng, hs = (b.rearrange("p (a n) -> p a n", a=2) for b in buf)
            gp = [PS[:, 2 * k:2 * k + 2, 0:HW_] for k in range(4)]
            gprod, gates, pre, tanhed, gchain, hready = sems(name, "gprod gates pre tanhed gchain hready")

            class Gru:
                ready = hready

                def tensor(self, pe, c):
                    for a in range(2):
                        x_ = acc[:, ds(c * CW + a * HW_, HW_)]
                        h_ = HB[:, ds(c * CW + a * HW_, HW_)]
                        for k in range(2):
                            pe.matmul(gp[k][:, a, :], W(W_IH + 3 * l + k), x_, start=True, stop=False)
                            pe.matmul(gp[k][:, a, :], W(W_HH + 3 * l + k), h_, start=False, stop=True)
                        pe.matmul(gp[2][:, a, :], W(W_IH + 3 * l + 2), x_, start=True, stop=True)
                        mm = pe.matmul(gp[3][:, a, :], W(W_HH + 3 * l + 2), h_, start=True, stop=True)
                    mm.then_inc(gprod, 1)

                def scalar(self, act, c):
                    rz = C_RZ + 3 * l
                    act.wait_ge(gprod, c + 1)
                    act.activation(rg, gp[0], ACT.Sigmoid, bias=bcol[:, rz:rz + 1]).then_inc(gates, 1)
                    act.activation(zg, gp[1], ACT.Sigmoid, bias=bcol[:, rz + 1:rz + 2]).then_inc(gates, 1)
                    act.wait_ge(pre, c + 1)
                    act.activation(ng, ng, ACT.Tanh, bias=bcol[:, C_IH + 3 * l + 2:C_IH + 3 * l + 3]).then_inc(tanhed, 1)

                def vector(self, dve, c):
                    own = Chain(dve, gchain, 4, c)
                    h_ = HB[:, ds(c * CW, CW)].rearrange("p (a n) -> p a n", a=2)
                    hh = C_HH + 3 * l + 2
                    dve.wait_ge(gates, c * 2 + 2)
                    own.step(V.scalar_tensor_tensor(out=ng, in0=gp[3], scalar=bcol[:, hh:hh + 1], in1=rg,
                                                    op0=ALU.add, op1=ALU.mult))
                    V.tensor_tensor(out=ng, in0=ng, in1=gp[2], op=ALU.add).then_inc(pre, 1)
                    dve.wait_ge(tanhed, c + 1)
                    own.step(V.tensor_tensor(out=rg, in0=h_, in1=ng, op=ALU.subtract))
                    own.step(V.tensor_tensor(out=rg, in0=rg, in1=zg, op=ALU.mult))
                    own.step(V.tensor_tensor(out=rg, in0=rg, in1=ng, op=ALU.add))
                    V.tensor_scalar(hs, rg, 0.0, None, ALU.max).then_inc(hready, 1)

            return Gru()

        def ggnn_next(ctx, name, PS, buf, st, acc_ready, done):
            hs = buf[3]
            kept, = sems(name, "kept")
            gru, table = gru_parts(name, 0, PS, buf), transformer(ctx, name, 1, PS, hs)

            class GgnnNext(Stage):
                before, sync = table.before, table.sync

                def scalar(self, act, c):
                    gru.scalar(act, c)
                    table.scalar(act, c)
                    act.wait_ge(kept, c + 1)
                    act.sem_inc(done, 1)

                def tensor(self, pe, c):
                    gru.tensor(pe, c)
                    pe.wait_ge(gru.ready, c + 1)
                    table.tensor(pe, c)

                def vector(self, dve, c):
                    gru.vector(dve, c)
                    dve.wait_ge(gru.ready, c + 1)
                    passed(dve, tick)
                    V.tensor_copy(HB[:, ds(c * CW, CW)], hs).then_inc(kept, 1)
                    table.vector(dve, c)

            return GgnnNext()

        def ggnn_end(ctx, name, PS, buf, st, acc_ready, done):
            r, sq, xT, hs = buf
            op_, tp, xp, sp_ = banks(PS, 0), banks(PS, 2), banks(PS, 4), PS[:, 6, 0:TC * 2 * H]
            gru = gru_parts(name, 1, PS, buf)
            oprod, nchain, var_ready, rooted, normed, xturned, xcopied, heads = sems(
                name, "oprod nchain var_ready rooted normed xturned xcopied heads")

            class GgnnEnd(Stage):
                def scalar(self, act, c):
                    gru.scalar(act, c)
                    root(act, st, var_ready, rooted, c, 1, 0)
                    act.wait_ge(xturned, c + 1)
                    act.copy(xT, tp).then_inc(xcopied, 1)

                def tensor(self, pe, c):
                    gru.tensor(pe, c)
                    pe.wait_ge(gru.ready, c + 1)
                    times(pe, op_, hs, W(W_OUT)).then_inc(oprod, 1)
                    pe.wait_ge(normed, c + 1)
                    turn_tiles(pe, tp, r).then_inc(xturned, 1)
                    pe.wait_ge(xcopied, c + 1)
                    times(pe, xp, xT, wall[:])
                    times(pe, sp_, xT, wa[:], width=2 * H).then_inc(heads, 1)

                def vector(self, dve, c):
                    gru.vector(dve, c)
                    STEPS = 2 + NORM_STEPS + 1
                    own = Chain(dve, nchain, STEPS, c)
                    at, r3 = ds(c * CW, CW), tiles3(r)
                    dve.wait_ge(oprod, c + 1)
                    own.step(V.tensor_tensor(out=r, in0=X[:, at], in1=op_, op=ALU.add))
                    own.step(V.tensor_tensor(out=r3, in0=r3, in1=rows(bias[:, B_OUT, :], TC), op=ALU.add))
                    norm(dve, own, r, sq, st, var_ready, rooted, c, 1, 0)
                    dve.sem_inc(normed, 1)
                    passed(dve, tick)
                    V.tensor_copy(X[:, at], r)
                    dve.wait_ge(heads, c + 1)
                    passed(dve, tick)
                    own.step(V.tensor_copy(S[:, ds(c * TC, TC), :], sp_.rearrange("p (t s) -> p t s", t=TC)))
                    passed(dve, tick)
                    V.tensor_copy(HB[:, at], xp).then_inc(done, 1)
                    assert own.n == STEPS, own.n

            return GgnnEnd()

        def gat_end(ctx, name, PS, buf, st, acc_ready, done):
            st_, r, sq, xT = buf
            ap_, tp, hp = banks(PS, 0), banks(PS, 2), banks(PS, 4)
            staged, turned, nchain, var_ready, rooted, normed, xturned, xcopied, mprod, stored = sems(
                name, "staged turned nchain var_ready rooted normed xturned xcopied mprod stored")

            class GatEnd(Stage):
                def scalar(self, act, c):
                    act.wait_ge(acc_ready, c + 1)
                    act.copy(st_, acc[:, ds(c * CW, CW)]).then_inc(staged, 1)
                    for k in range(2):
                        root(act, st, var_ready, rooted, c, 2, k)
                    act.wait_ge(xturned, c + 1)
                    act.copy(xT, tp).then_inc(xcopied, 1)

                def tensor(self, pe, c):
                    pe.wait_ge(staged, c + 1)
                    turn_tiles(pe, ap_, st_).then_inc(turned, 1)
                    pe.wait_ge(normed, c + 1)
                    turn_tiles(pe, tp, r).then_inc(xturned, 1)
                    pe.wait_ge(xcopied, c + 1)
                    times(pe, hp, xT, W(W_M1X)).then_inc(mprod, 1)

                def vector(self, dve, c):
                    STEPS = 4 + 2 * NORM_STEPS
                    own = Chain(dve, nchain, STEPS, c)
                    at, r3 = ds(c * CW, CW), tiles3(r)
                    dve.wait_ge(turned, c + 1)
                    own.step(V.tensor_tensor(out=r, in0=X[:, at], in1=ap_, op=ALU.add))
                    norm(dve, own, r, sq, st, var_ready, rooted, c, 2, 0)
                    own.step(V.tensor_tensor(out=r3, in0=r3, in1=rows(bias[:, B_GAMMA, :], TC), op=ALU.mult))
                    own.step(V.tensor_tensor(out=r3, in0=r3, in1=rows(bias[:, B_BETA, :], TC), op=ALU.add))
                    own.step(V.tensor_tensor(out=r, in0=r, in1=X[:, at], op=ALU.add))
                    norm(dve, own, r, sq, st, var_ready, rooted, c, 2, 1)
                    dve.sem_inc(normed, 1)
                    passed(dve, tick)
                    V.tensor_copy(X[:, at], r)
                    dve.wait_ge(mprod, c + 1)
                    V.tensor_tensor(out=tiles3(HB[:, at]), in0=tiles3(hp), in1=rows(bias[:, B_M1, :], TC),
                                    op=ALU.add).then_inc(done, 1)
                    assert own.n == STEPS, own.n

                def sync(self, sp):
                    for c in range(NCH):
                        sp.wait_ge(done, c + 1)
                        sp.dma_start(msg_d[c * CW:(c + 1) * CW].rearrange("(t p) f -> p t f", p=P),
                                     tiles3(HB[:, c * CW:(c + 1) * CW])).then_inc(stored, 16)
                    sp.wait_ge(stored, 16 * NCH)

            return GatEnd()

        def mpnn_end(ctx, name, PS, buf, st, acc_ready, done):
            as_, xs, xT, u = buf
            r, sq = xs, as_
            tp, xp, mp = banks(PS, 0), banks(PS, 2), banks(PS, 4)
            staged, turned, xcopied, uprod, nchain, hidden, delta, var_ready, rooted, stored = sems(
                name, "staged turned xcopied uprod nchain hidden delta var_ready rooted stored")

            class MpnnEnd(Stage):
                def scalar(self, act, c):
                    act.wait_ge(acc_ready, c + 1)
                    act.copy(as_, acc[:, ds(c * CW, CW)])
                    act.copy(xs, X[:, ds(c * CW, CW)]).then_inc(staged, 1)
                    for k in range(2):
                        act.wait_ge(turned, c * 2 + k + 1)
                        act.copy(xT, tp).then_inc(xcopied, 1)
                    for k in range(2):
                        root(act, st, var_ready, rooted, c, 2, k)

                def tensor(self, pe, c):
                    pe.wait_ge(staged, c + 1)
                    turn_tiles(pe, tp, xs).then_inc(turned, 1)
                    times(pe, mp, as_, wcomb[:])
                    pe.wait_ge(xcopied, c * 2 + 1)
                    times(pe, xp, xT, W(W_U1X)).then_inc(uprod, 1)
                    pe.wait_ge(hidden, c + 1)
                    turn_tiles(pe, tp, u).then_inc(turned, 1)
                    pe.wait_ge(xcopied, c * 2 + 2)
                    times(pe, xp, xT, W(W_U2)).then_inc(delta, 1)

                def vector(self, dve, c):
                    STEPS = 10 + 2 * NORM_STEPS
                    own = Chain(dve, nchain, STEPS, c)
                    at, att, r3, u3 = ds(c * CW, CW), ds(c * TC, TC), tiles3(r), tiles3(u)
                    dve.wait_ge(uprod, c + 1)
                    own.step(V.tensor_tensor(out=u3, in0=tiles3(mp), in1=over(cntinv[:, att], D), op=ALU.mult))
                    own.step(V.tensor_tensor(out=u, in0=u, in1=xp, op=ALU.add))
                    own.step(V.tensor_tensor(out=r3, in0=over(has[:, att], D), in1=rows(bias[:, B_V, :], TC), op=ALU.mult))
                    own.step(V.tensor_tensor(out=u, in0=u, in1=r, op=ALU.add))
                    own.step(V.tensor_tensor(out=u3, in0=u3, in1=rows(bias[:, B_U1, :], TC), op=ALU.add))
                    V.tensor_scalar(u, u, 0.0, None, ALU.max).then_inc(hidden, 1)
                    dve.wait_ge(delta, c + 1)
                    own.step(V.tensor_tensor(out=r, in0=X[:, at], in1=xp, op=ALU.add))
                    own.step(V.tensor_tensor(out=r3, in0=r3, in1=rows(bias[:, B_U2, :], TC), op=ALU.add))
                    norm(dve, own, r, sq, st, var_ready, rooted, c, 2, 0)
                    own.step(V.tensor_tensor(out=r3, in0=r3, in1=rows(bias[:, B_LNG, :], TC), op=ALU.mult))
                    own.step(V.tensor_tensor(out=r3, in0=r3, in1=rows(bias[:, B_LNB, :], TC), op=ALU.add))
                    own.step(V.tensor_tensor(out=r, in0=r, in1=X[:, at], op=ALU.add))
                    norm(dve, own, r, sq, st, var_ready, rooted, c, 2, 1)
                    passed(dve, tick)
                    V.tensor_copy(X[:, at], r).then_inc(done, 1)
                    assert own.n == STEPS, own.n

                def sync(self, sp):
                    for c in range(NCH):
                        sp.wait_ge(done, c + 1)
                        full = min((c + 1) * CW, NPAD - P)
                        sp.dma_start(out[c * CW:full].rearrange("(t p) f -> p t f", p=P),
                                     tiles3(X[:, c * CW:full])).then_inc(stored, 16)
                    sp.dma_start(out[NPAD - P:N], X[0:NLAST, NPAD - P:]).then_inc(stored, 16)
                    sp.wait_ge(stored, 16 * (NCH + 1))

            return MpnnEnd()

        aggregate("gcn_edges", gcn_d, src_d, gcn_end, weighted=True, sl=2 * SL)
        for l, stage in enumerate((ggnn_next, ggnn_end)):
            aggregate(f"ggnn{l}_edges", trans_d[l].rearrange("n (t f) -> (n t) f", t=T), row_d, stage, sl=2 * SL)
        early.close()

        with ExitStack() as ctx:
            ctx.callback(end_stage)
            sjm = sb(ctx, "sjm", [P, NT, 2 * H])
            below = sb(ctx, "below", [P, NT])
            A = sb(ctx, "A", [P, NT, 2 * H])
            J = sb(ctx, "J", [P, NT, 2 * H])
            J3 = sb(ctx, "J3", [P, NT, 3, 2 * H], BF16)
            zr = sb(ctx, "zr", [P, 6 * H], BF16)
            mx = sb(ctx, "mx", [P, 2 * H])
            m16 = sb(ctx, "m16", [2 * H, 1])
            dg = sb(ctx, "dg", [2 * H, 2 * H])
            mp = ps(ctx, "mp", [P, P])
            bp = ps(ctx, "bp", [P, 2 * H])
            iotas, maxed, turned, diag, spread, tables, stored, chain = sems(
                "max", "iotas maxed turned diag spread tables stored chain")
            with nc.Block() as block:
                @block.gpsimd
                def _(pool):
                    pool.iota(real[:], [[P, NT]], base=0, channel_multiplier=1,
                              allow_small_or_imprecise_dtypes=True).then_inc(iotas, 1)

                @block.vector
                def _(dve):
                    own = Chain(dve, chain)
                    own.step(V.memset(zr[:], 0.0))
                    dve.wait_ge(iotas, 1)
                    own.step(V.tensor_scalar(real[:], real[:], float(N), None, ALU.is_lt))
                    own.step(V.tensor_scalar(below[:], real[:], 3e38, -3e38, ALU.mult, ALU.add))
                    own.step(V.tensor_tensor(out=sjm[:, :, 0:H], in0=S[:, :, H:2 * H], in1=over(real[:], H), op=ALU.mult))
                    own.step(V.tensor_scalar(sjm[:, :, H:2 * H], sjm[:, :, 0:H], -1.0, None, ALU.mult))
                    own.step(V.tensor_tensor(out=sjm[:], in0=sjm[:], in1=over(below[:], 2 * H), op=ALU.add))
                    V.tensor_reduce(mx[:], sjm[:].rearrange("p t h -> p h t"), AX, ALU.max).then_inc(maxed, 1)
                    dve.wait_ge(turned, 1)
                    own.step(V.tensor_reduce(m16[:], mp[0:2 * H, :], AX, ALU.max))
                    V.tensor_scalar(dg[:], ident[0:2 * H, 0:2 * H], m16[:, 0:1], None, ALU.mult).then_inc(diag, 1)
                    dve.wait_ge(spread, 1)
                    own.step(V.tensor_copy(sj_ends[:], bp[:]))
                    own.step(V.tensor_copy(A[:, :, 0:H], S[:, :, 0:H]))
                    own.step(V.tensor_tensor(out=J[:, :, 0:H], in0=S[:, :, 0:H], in1=rows(sj_ends[:, 0:H], NT), op=ALU.add))
                    own.step(V.scalar_tensor_tensor(out=A[:, :, H:2 * H], in0=J[:, :, 0:H], scalar=ALPHA, in1=J[:, :, 0:H],
                                                    op0=ALU.mult, op1=ALU.max))
                    own.step(V.memset(J[:, :, H:2 * H], 1.0))
                    own.step(V.tensor_copy(J[:, :, 0:H], S[:, :, H:2 * H]))
                    for a in range(3):
                        own.step(V.tensor_copy(J3[:, :, a, :], J[:]))
                        own.step(V.tensor_tensor(out=J[:], in0=J[:], in1=J3[:, :, a, :], op=ALU.subtract))
                    dve.sem_inc(tables, 1)

                @block.tensor
                def _(pe):
                    pe.wait_ge(maxed, 1)
                    pe.transpose(mp[0:2 * H, :], mx[:], ident[:]).then_inc(turned, 1)
                    pe.wait_ge(diag, 1)
                    pe.matmul(bp[:], ones[0:2 * H, :], dg[:], start=True, stop=True).then_inc(spread, 1)

                @block.sync
                def _(sp):
                    sp.wait_ge(tables, 1)
                    sp.dma_start(att_d.rearrange("(t p) s -> p t s", p=P), A[:]).then_inc(stored, 16)
                    sp.dma_start(sj_d[0:NPAD].rearrange("(t p) s -> p t s", p=P),
                                 J3[:].rearrange("p t a s -> p t (a s)")).then_inc(stored, 16)
                    sp.dma_start(sj_d[NPAD:ACCW], zr[:]).then_inc(stored, 16)
                    sp.wait_ge(stored, 48)

        gat = whole.enter_context(ExitStack())
        ex = sb(gat, "ex", [P, NG * GC * H])
        NX, NQ = 4, GC // 2
        assert SL * NQ % NX == 0
        def spare(k, w=H, n=1):
            at = 2 * GE + k * NT * H
            return acc[:, at:at + n * NT * w].rearrange("p (t h) -> p t h", h=w)

        low, b_lo, b_hi, b_now = (spare(k) for k in range(4))
        sm = spare(4, 2 * H)
        lows = acc[:, ACCW - 1:ACCW]
        assert 2 * GE + 6 * NT * H < ACCW

        def attention(name):
            sl = 2 * SL
            with ExitStack() as ctx:
                ctx.callback(end_stage)
                G = sb(ctx, f"{name}_G", [P, sl, GC, 2 * H])
                dr = sb(ctx, f"{name}_dr", [P, 2, GE], I32)
                ohT = sb(ctx, f"{name}_ohT", [P, GC, P], BF16)
                ohl = [acc[:, b * GE:(b + 1) * GE].rearrange("p (c n) -> p c n", c=GC) for b in range(2)]
                exh = sb(ctx, f"{name}_exh", [P, NX, 2, NT, H])
                sjw = sb(ctx, f"{name}_sjw", [P, sl, 3, 2 * H], BF16)
                idx = sb(ctx, f"{name}_idx", [P, sl, GC], I32)
                srch = sb(ctx, f"{name}_srch", [P, GC], I32)
                srcl = sb(ctx, f"{name}_srcl", [P, GC], I32)
                itm = sb(ctx, f"{name}_itm", [P, sl, 4], I32)
                e_ = sb(ctx, f"{name}_e_", [P, GC, H])
                x_ = sb(ctx, f"{name}_x_", [P, GC, H])
                em = sb(ctx, f"{name}_em", [P, GC, H])
                zero = sb(ctx, f"{name}_zero", [P, NT * H])
                jps = [ps(ctx, f"{name}_jp{b}", [P, GC, 2 * H]) for b in range(2)]
                dp = ps(ctx, f"{name}_dp", [P, NT * H])
                gathered = sems(name, " ".join(f"gathered{s}" for s in range(sl)))
                idx_ready = sems(name, " ".join(f"idx_ready{s}" for s in range(sl)))
                item_ready, done, window_in, oht_ready, sj_ready, chain, diff, exped, exh_ready, exh_free, zeroed, summed, \
                        tested, counted = sems(
                    name, "item_ready done window_in oht_ready sj_ready chain diff exped exh_ready exh_free zeroed summed tested counted")
                with nc.Block() as block:
                    @block.sync
                    def _(sp):
                        n = sp.value_load(turns_to[0:1, 2 * NCH + 1:2 * NCH + 2], min_val=1, max_val=KCAP // sl)
                        with sp.Fori(0, n) as i:
                            for s in range(sl):
                                k = i * sl + s
                                sp.wait_ge(done, k + 1)
                                sp.dma_start(itm[:, s, :], items_d[ds(k, 1), :].to_broadcast([P, 4])
                                             ).then_inc(item_ready, 16)
                                sp.wait_ge(item_ready, k * 16 + 16)
                                passed(sp, tick)
                                g = sp.value_load(itm[0:1, s, 2:3], min_val=0, max_val=NG - 1)
                                col = sp.value_load(itm[0:1, s, 1:2], min_val=0, max_val=N - 1)
                                sp.dma_start(idx[:, s, :], src_d[ds(g, 1), :].rearrange("a (p c) -> (a p) c", c=GC)
                                             ).then_inc(idx_ready[s], 16)
                                sp.wait_ge(oht_ready, k + 1)
                                sp.dma_start(dr[:, s % 2], dst_d[ds(g, 1), :].to_broadcast([P, GE])).then_inc(window_in, 16)
                                sp.dma_start(sjw[:, s].rearrange("p a h -> p (a h)"), sj_d[ds(col, P), :]).then_inc(window_in, 16)

                    @block.scalar
                    def _(act):
                        n = act.value_load(turns_to[0:1, 2 * NCH + 1:2 * NCH + 2], min_val=1, max_val=KCAP // sl)
                        with act.Fori(0, n) as i:
                            for s in range(sl):
                                act.wait_ge(diff, i * sl + s + 1)
                                act.activation(x_[:], e_[:], ACT.Exp).then_inc(exped, 1)

                    @block.gpsimd
                    def _(pool):
                        n = pool.value_load(turns_to[0:1, 2 * NCH + 1:2 * NCH + 2], min_val=1, max_val=KCAP // sl)
                        with pool.Fori(0, n) as i:
                            for s in range(sl):
                                pool.wait_ge(idx_ready[s], i * 16 + 16)
                                passed(pool, tick)
                                for c in range(GC):
                                    pool.indirect_dma_start(
                                        G[:, s, c, :], None, att_d,
                                        bass.IndirectOffsetOnAxis(ap=idx[:, s, c:c + 1].bitcast(U32), axis=0)
                                    ).then_inc(gathered[s], 16)

                    @block.tensor
                    def _(pe):
                        pe.wait_ge(zeroed, 1)
                        pe.matmul(dp[:], zero[:, 0:P], zero[:], start=True, stop=False, skip_group_check=True)\
                            .then_inc(exh_free, NX + NQ)
                        n = pe.value_load(turns_to[0:1, 2 * NCH + 1:2 * NCH + 2], min_val=1, max_val=KCAP // sl)

                        with pe.Fori(0, n) as i:
                            def spread_sj(s):
                                pe.wait_ge(oht_ready, i * sl + s + 3)
                                for c in range(GC):
                                    for a in range(3):
                                        mm = pe.matmul(jps[s % 2][:, c, :], ohT[:, c, :], sjw[:, s, a, :], start=a == 0, stop=a == 2)
                                mm.then_inc(sj_ready, 1)

                            spread_sj(0)
                            for s in range(sl):
                                if s + 1 < sl:
                                    spread_sj(s + 1)
                                for q in range(NQ):
                                    pe.wait_ge(exh_ready, (i * sl + s) * NQ + q + 1)
                                    for c in range(2):
                                        mm = pe.matmul(dp[:], ohl[s % 2][:, 2 * q + c, :],
                                                       exh[:, (s * NQ + q) % NX, c].rearrange("p t h -> p (t h)"),
                                                       start=False, stop=False, skip_group_check=True)
                                    mm.then_inc(exh_free, 1)
                        pe.matmul(dp[:], zero[:, 0:P], zero[:], start=False, stop=True, skip_group_check=True).then_inc(summed, 1)
                        if name == "at":
                            pe.wait_ge(tested, 1)
                            pe.matmul(jps[0][0:1, 0, 0:1], lows, ones[:, 0:1], start=True, stop=True).then_inc(counted, 1)

                    @block.vector
                    def _(dve):
                        dve.sem_inc(done, sl)
                        dve.sem_inc(oht_ready, 2)
                        V.memset(zero[:], 0.0).then_inc(zeroed, 1)
                        V.memset(ex[:], 0.0).then_inc(chain, 1)
                        dve.wait_ge(chain, 1)
                        n = dve.value_load(turns_to[0:1, 2 * NCH + 1:2 * NCH + 2], min_val=1, max_val=KCAP // sl)
                        STEPS = sl * 7
                        with dve.Fori(0, n) as i:
                            own = Chain(dve, chain)
                            own.base = i * STEPS + 1

                            def window_hot(s):
                                k = i * sl + s
                                dve.wait_ge(window_in, k * 32 + 32)
                                V.tensor_scalar(ohT[:], dr[:, s % 2].rearrange("n (p c) -> n c p", c=GC), itm[:, s, 0:1], iota_colI[:, 0:1],
                                                ALU.subtract, ALU.is_equal).then_inc(oht_ready, 1)

                            window_hot(0)
                            for s in range(sl):
                                k = i * sl + s
                                jp = jps[s % 2]
                                dve.wait_ge(idx_ready[s], i * 16 + 16)
                                own.step(V.tensor_single_scalar(srcl[:], idx[:, s, :], P - 1, op=ALU.bitwise_and))
                                own.step(V.tensor_single_scalar(srch[:], idx[:, s, :], 7, op=ALU.arith_shift_right))
                                passed(dve, tick)
                                g = dve.value_load(itm[0:1, s, 2:3], min_val=0, max_val=NG - 1)
                                dve.wait_ge(gathered[s], i * 16 * GC + 16 * GC)
                                dve.wait_ge(sj_ready, k + 1)
                                own.step(V.tensor_tensor(out=x_[:], in0=G[:, s, :, 0:H], in1=jp[:, :, 0:H], op=ALU.add))
                                own.step(V.scalar_tensor_tensor(out=e_[:], in0=x_[:], scalar=ALPHA, in1=x_[:], op0=ALU.mult, op1=ALU.max))
                                own.step(V.tensor_tensor(out=e_[:], in0=e_[:], in1=G[:, s, :, H:2 * H], op=ALU.subtract))
                                V.tensor_scalar(e_[:], e_[:], E_TOP, None, ALU.min).then_inc(diff, 1)
                                dve.wait_ge(exh_free, k * NQ + NX)
                                V.tensor_tensor(out=ohl[s % 2], in0=over(srcl[:], P), in1=rows(iota_row[:], GC), op=ALU.is_equal)
                                if s + 1 < sl:
                                    window_hot(s + 1)
                                dve.wait_ge(exped, k + 1)
                                own.step(V.tensor_tensor(out=em[:], in0=x_[:], in1=jp[:, :, H:2 * H], op=ALU.mult))
                                for q in range(NQ):
                                    dve.wait_ge(exh_free, (k + 1) * NQ + q + 1)
                                    for c in range(2):
                                        j = 2 * q + c
                                        last = V.scalar_tensor_tensor(
                                            out=exh[:, (s * NQ + q) % NX, c], in0=over(iota_row[:, 0:NT], H),
                                            scalar=srch[:, j:j + 1], in1=rows(em[:, j, :], NT), op0=ALU.is_equal, op1=ALU.mult)
                                    last.then_inc(exh_ready, 1)
                                exg = ex[:, ds(g * GC * H, GC * H)].rearrange("p (c h) -> p c h", h=H)
                                own.step(V.tensor_tensor(out=exg, in0=exg, in1=em[:], op=ALU.add))
                                dve.sem_inc(done, 1)
                            assert own.n == STEPS, own.n
                        dve.wait_ge(summed, 1)
                        V.tensor_copy(den[:].rearrange("p t h -> p (t h)"), dp[:]).then_inc(zeroed, 1)
                        dve.wait_ge(zeroed, 2)
                        if name == "at":
                            V.scalar_tensor_tensor(out=low, in0=den[:], scalar=DEN_LOW, in1=over(real[:], H), op0=ALU.is_lt,
                                                   op1=ALU.mult).then_inc(zeroed, 1)
                            dve.wait_ge(zeroed, 3)
                            V.tensor_reduce(lows, low.rearrange("p t h -> p (t h)"), AX, ALU.add).then_inc(tested, 1)
                            dve.wait_ge(counted, 1)
                            V.tensor_scalar(rounds[:], jps[0][0:1, 0, 0:1], 0.0, float(ROUNDS), ALU.is_gt,
                                            ALU.mult).then_inc(zeroed, 1)
                            dve.wait_ge(zeroed, 4)

        attention("at")

        _, (n_rounds,) = nc.values_load_multi_w_load_instructions(rounds[:], min_val=0, max_val=ROUNDS,
                                                                   bass_reorder=False)
        with nc.If(n_rounds > 0):
            nc.all_engine_barrier()
            with ExitStack() as ctx:
                ctx.callback(end_stage)
                ends, = sems("ends", "ends")
                with nc.Block() as block:
                    @block.vector
                    def _(dve):
                        own = Chain(dve, ends)
                        own.step(V.tensor_copy(b_now, rows(sj_ends[:, 0:H], NT)))
                        own.step(V.tensor_copy(b_hi, rows(sj_ends[:, 0:H], NT)))
                        own.step(V.tensor_scalar(b_lo, rows(sj_ends[:, H:2 * H], NT), -1.0, None, ALU.mult))

            with nc.Fori(0, ROUNDS):
                with ExitStack() as ctx:
                    ctx.callback(end_stage)
                    chain, drawn, stored = sems("draw", "chain drawn stored")
                    with nc.Block() as block:
                        @block.vector
                        def _(dve):
                            own = Chain(dve, chain)
                            own.step(V.tensor_scalar(low, den[:], DEN_LOW, None, ALU.is_lt))
                            own.step(V.tensor_tensor(out=sm[:, :, 0:H], in0=b_now, in1=b_hi, op=ALU.subtract))
                            own.step(V.tensor_tensor(out=sm[:, :, 0:H], in0=sm[:, :, 0:H], in1=low, op=ALU.mult))
                            own.step(V.tensor_tensor(out=b_hi, in0=b_hi, in1=sm[:, :, 0:H], op=ALU.add))
                            own.step(V.tensor_tensor(out=sm[:, :, 0:H], in0=b_now, in1=b_lo, op=ALU.subtract))
                            own.step(V.scalar_tensor_tensor(out=sm[:, :, 0:H], in0=den[:], scalar=DEN_HIGH,
                                                            in1=sm[:, :, 0:H], op0=ALU.is_ge, op1=ALU.mult))
                            own.step(V.tensor_tensor(out=b_lo, in0=b_lo, in1=sm[:, :, 0:H], op=ALU.add))
                            own.step(V.scalar_tensor_tensor(out=low, in0=den[:], scalar=DEN_HIGH, in1=low,
                                                            op0=ALU.is_ge, op1=ALU.add))
                            own.step(V.tensor_tensor(out=sm[:, :, 0:H], in0=b_lo, in1=b_hi, op=ALU.add))
                            own.step(V.scalar_tensor_tensor(out=sm[:, :, 0:H], in0=sm[:, :, 0:H], scalar=0.5, in1=b_now,
                                                            op0=ALU.mult, op1=ALU.subtract))
                            own.step(V.tensor_tensor(out=sm[:, :, 0:H], in0=sm[:, :, 0:H], in1=low, op=ALU.mult))
                            own.step(V.tensor_tensor(out=b_now, in0=b_now, in1=sm[:, :, 0:H], op=ALU.add))
                            own.step(V.tensor_tensor(out=low, in0=S[:, :, 0:H], in1=b_now, op=ALU.add))
                            own.step(V.tensor_copy(sm[:, :, 0:H], S[:, :, 0:H]))
                            V.scalar_tensor_tensor(out=sm[:, :, H:2 * H], in0=low, scalar=ALPHA, in1=low,
                                                   op0=ALU.mult, op1=ALU.max).then_inc(drawn, 1)

                        @block.sync
                        def _(sp):
                            sp.wait_ge(drawn, 1)
                            sp.dma_start(att_d.rearrange("(t p) s -> p t s", p=P), sm).then_inc(stored, 16)
                            sp.wait_ge(stored, 16)
                attention("at_again")

        with ExitStack() as ctx:
            ctx.callback(end_stage)
            chain, scaled, stored = sems("heads", "chain scaled stored")
            with nc.Block() as block:
                @block.vector
                def _(dve):
                    own = Chain(dve, chain)
                    own.step(V.tensor_scalar(den[:], den[:], 1e-30, None, ALU.max))
                    own.step(V.reciprocal(den[:], den[:]))
                    hb = HB[:].rearrange("p (q j) -> p q j", j=HD)
                    V.tensor_tensor(out=hb, in0=hb, in1=over(den[:].rearrange("p t h -> p (t h)"), HD),
                                    op=ALU.mult).then_inc(scaled, 1)

                @block.sync
                def _(sp):
                    sp.wait_ge(scaled, 1)
                    sp.dma_start(heads_d.rearrange("(t p) f -> p t f", p=P), tiles3(HB[:])).then_inc(stored, 16)
                    sp.wait_ge(stored, 16)

        aggregate("gat_edges", heads_d, src_d, gat_end, ex=ex)
        gat.close()
        aggregate("mpnn_edges", msg_d, src_d, mpnn_end, attr=True, sl=2 * SL)


_INS = ['x', 'src', 'dst', 'edge_attr_64', 'edge_type_8', 'edge_weight', 'L0_gnn_W', 'L0_gnn_b', 'L1_gnn_node_proj_w',
        'L1_gnn_node_proj_b', 'L1_gnn_edge_W', 'L1_gnn_edge_b', 'L1_gnn_gru_wih', 'L1_gnn_gru_whh', 'L1_gnn_gru_bih',
        'L1_gnn_gru_bhh', 'L1_gnn_out_w', 'L1_gnn_out_b', 'L2_gnn_W', 'L2_gnn_a', 'L2_gnn_ln_gamma', 'L2_gnn_ln_beta',
        'L3_gnn_global_state', 'L3_gnn_Wm1', 'L3_gnn_bm1', 'L3_gnn_Wm2', 'L3_gnn_bm2', 'L3_gnn_Wu1', 'L3_gnn_bu1',
        'L3_gnn_Wu2', 'L3_gnn_bu2', 'L3_gnn_ln_g', 'L3_gnn_ln_b']


def kernel(**inputs):
    import concourse.bacc as _bacc
    import numpy as _np
    from concourse.bass_utils import run_bass_kernel_spmd as _run

    nc = _bacc.Bacc("TRN2", target_bir_lowering=False, num_devices=1)
    arrays, args = {}, []
    for name in _INS:
        a = _np.ascontiguousarray(inputs[name])
        arrays[f"in_{name}"] = a
        args.append(nc.dram_tensor(f"in_{name}", a.shape, mybir.dt.from_np(a.dtype), kind="ExternalInput").ap())
    args.append(nc.dram_tensor("out_0", (N, D), F32, kind="ExternalOutput").ap())
    build(nc, *args)
    r = _run(nc, [arrays], core_ids=[0])
    return r.results[0]["out_0"]
```
